# Optimizing a Trainium2 kernel written in Bass

```python
import numpy as np
import jax
import jax.numpy as jnp

def _softmax(x, axis=-1):
    return jax.nn.softmax(x, axis=axis)

def _gelu(x):
    return jax.nn.gelu(x, approximate=True)

def _silu(x):
    return jax.nn.silu(x)

def _sigmoid(x):
    return jax.nn.sigmoid(x)

def _layernorm(x, axis=-1, eps=1e-05):
    m = jnp.mean(x, axis=axis, keepdims=True)
    v = jnp.var(x, axis=axis, keepdims=True)
    return (x - m) / jnp.sqrt(v + eps)

def _scatter_add(tgt, idx, src, axis=0):
    return tgt.at[idx].add(src)

def _segment_sum(src, seg, n):
    return jax.ops.segment_sum(src, seg, n)
kernel_name = 'mk_gnn_resnorm_d4_gnn_r32_733a72'

def setup_inputs(seed: int=0):
    np.random.seed(seed)
    _w = jnp.asarray

    def _rec_inputs():
        import jax
        import jax.numpy as jnp
        _gk = jax.random.key(seed)
        x = -0.0005121 + 1.001 * jax.random.normal(jax.random.fold_in(_gk, 1), (50000, 64), jnp.float32)
        src = jax.random.randint(jax.random.fold_in(_gk, 2), (50000,), 0, 50000, jnp.int32)
        dst = jax.random.randint(jax.random.fold_in(_gk, 3), (50000,), 0, 50000, jnp.int32)
        _o = jnp.argsort(dst, stable=True)
        src = src[_o]
        dst = dst[_o]
        edge_attr_64 = -9.77346e-05 + 0.999888 * jax.random.normal(jax.random.fold_in(_gk, 12), (50000, 64), jnp.float32)
        edge_weight = 0.000614103 + 0.999867 * jax.random.normal(jax.random.fold_in(_gk, 14), (50000,), jnp.float32)
        return (x, src, dst, edge_attr_64, edge_weight)
    x, src, dst, edge_attr_64, edge_weight = _rec_inputs()

    def _L0_gnn_setup():
        import jax, jax.numpy as jnp
        import numpy as np
        N = 50000
        E = 25000
        D = 64

        def segment_softmax(v, idx, num_segments):
            m = jax.ops.segment_max(v, idx, num_segments=num_segments)
            ex = jnp.exp(v - m[idx])
            s = jax.ops.segment_sum(ex, idx, num_segments=num_segments)
            return ex / (s[idx] + 1e-16)
        key = jax.random.key(seed)
        k1, k2, k3 = jax.random.split(key, 3)
        x = jax.random.normal(k1, (N, D), dtype=jnp.float32)
        edge_index = jax.random.randint(k2, (2, E), 0, N, dtype=jnp.int32)
        val = jax.random.normal(k3, (E,), dtype=jnp.float32)
        return {'x': x, 'edge_index': edge_index, 'val': val}
    _L0_gnn_all = _L0_gnn_setup()
    _L0_gnn_in = {k: v for k, v in _L0_gnn_all.items() if k in ()}
    del _L0_gnn_all

    def _L1_gnn_setup():
        import jax, jax.numpy as jnp
        import numpy as np
        N_NODES = 3125
        N_EDGES = 100000

        def _gcn_layer(x, W, b, src, dst, n_nodes):
            h = x @ W
            ones = jnp.ones(src.shape[0], dtype=x.dtype)
            deg = jax.ops.segment_sum(ones, dst, num_segments=n_nodes)
            dinv = jnp.where(deg > 0, jax.lax.rsqrt(deg), 0.0)
            norm = dinv[src] * dinv[dst]
            msg = h[src] * norm[:, None]
            out = jax.ops.segment_sum(msg, dst, num_segments=n_nodes)
            return out + b
        key = jax.random.key(seed)
        k1, k2, k3, k4 = jax.random.split(key, 4)
        x = jax.random.normal(k1, (N_NODES, 64), dtype=jnp.float32)
        edge_index = jax.random.randint(k2, (2, N_EDGES), 0, N_NODES, dtype=jnp.int64)
        W1 = jax.random.normal(k3, (64, 128), dtype=jnp.float32) * (1.0 / np.sqrt(64))
        b1 = jnp.zeros((128,), dtype=jnp.float32)
        W2 = jax.random.normal(k4, (128, 64), dtype=jnp.float32) * (1.0 / np.sqrt(128))
        b2 = jnp.zeros((64,), dtype=jnp.float32)
        return {'x': x, 'edge_index': edge_index, 'W1': W1, 'b1': b1, 'W2': W2, 'b2': b2}
    _L1_gnn_all = _L1_gnn_setup()
    _L1_gnn_in = {k: v for k, v in _L1_gnn_all.items() if k in ('W1', 'b1', 'W2', 'b2')}
    del _L1_gnn_all

    def _L2_gnn_setup():
        import jax, jax.numpy as jnp
        import numpy as np
        N_NODES = 3125
        N_EDGES = 50000
        EMBED_DIM = 64
        NUM_HEADS = 4
        HEAD_DIM = EMBED_DIM // NUM_HEADS

        def mish(x):
            return x * jnp.tanh(jax.nn.softplus(x))
        key = jax.random.key(seed)
        ks = jax.random.split(key, 8)
        x = jax.random.normal(ks[0], (N_NODES, EMBED_DIM), dtype=jnp.float32)
        senders = jax.random.randint(ks[1], (N_EDGES,), 0, N_NODES, dtype=jnp.int32)
        receivers = jax.random.randint(ks[2], (N_EDGES,), 0, N_NODES, dtype=jnp.int32)
        sc = 1.0 / np.sqrt(EMBED_DIM)
        Ws = jax.random.normal(ks[3], (EMBED_DIM, NUM_HEADS, HEAD_DIM), dtype=jnp.float32) * sc
        bs = jnp.zeros((NUM_HEADS, HEAD_DIM), dtype=jnp.float32)
        Wr = jax.random.normal(ks[4], (EMBED_DIM, NUM_HEADS, HEAD_DIM), dtype=jnp.float32) * sc
        br = jnp.zeros((NUM_HEADS, HEAD_DIM), dtype=jnp.float32)
        aw = jax.random.normal(ks[5], (HEAD_DIM,), dtype=jnp.float32) * (1.0 / np.sqrt(HEAD_DIM))
        ab = jnp.zeros((1,), dtype=jnp.float32)
        return {'x': x, 'Ws': Ws, 'bs': bs, 'Wr': Wr, 'br': br, 'aw': aw, 'ab': ab, 'senders': senders, 'receivers': receivers}
    _L2_gnn_all = _L2_gnn_setup()
    _L2_gnn_in = {k: v for k, v in _L2_gnn_all.items() if k in ('Ws', 'bs', 'Wr', 'br', 'aw', 'ab')}
    del _L2_gnn_all

    def _L3_gnn_setup():
        import jax, jax.numpy as jnp
        import numpy as np
        N_NODES = 50000
        N_EDGES = 25000
        D_FEAT = 64
        AVG_D = float(np.log(17.0))
        EPS_STD = 1e-05
        EPS_BN = 1e-05
        key = jax.random.key(seed)
        k1, k2, k3, k4, k5, k6 = jax.random.split(key, 6)
        h = jax.random.normal(k1, (N_NODES, D_FEAT), jnp.float32)
        ef = jax.random.normal(k2, (N_EDGES, D_FEAT), jnp.float32)
        src = jax.random.randint(k3, (N_EDGES,), 0, N_NODES, jnp.int32)
        dst = jax.random.randint(k4, (N_EDGES,), 0, N_NODES, jnp.int32)
        gamma = jax.random.uniform(k5, (D_FEAT,), jnp.float32, 0.5, 1.5)
        beta = 0.1 * jax.random.normal(k6, (D_FEAT,), jnp.float32)
        return {'h': h, 'ef': ef, 'gamma': gamma, 'beta': beta, 'src': src, 'dst': dst}
    _L3_gnn_all = _L3_gnn_setup()
    _L3_gnn_in = {k: v for k, v in _L3_gnn_all.items() if k in ('gamma', 'beta')}
    del _L3_gnn_all
    return {'x': x, 'src': src, 'dst': dst, 'edge_attr_64': edge_attr_64, 'edge_weight': edge_weight, 'L1_gnn_W1': _L1_gnn_in['W1'], 'L1_gnn_b1': _L1_gnn_in['b1'], 'L1_gnn_W2': _L1_gnn_in['W2'], 'L1_gnn_b2': _L1_gnn_in['b2'], 'L2_gnn_Ws': _L2_gnn_in['Ws'], 'L2_gnn_bs': _L2_gnn_in['bs'], 'L2_gnn_Wr': _L2_gnn_in['Wr'], 'L2_gnn_br': _L2_gnn_in['br'], 'L2_gnn_aw': _L2_gnn_in['aw'], 'L2_gnn_ab': _L2_gnn_in['ab'], 'L3_gnn_gamma': _L3_gnn_in['gamma'], 'L3_gnn_beta': _L3_gnn_in['beta']}

def reference(x, src, dst, edge_attr_64, edge_weight, L1_gnn_W1, L1_gnn_b1, L1_gnn_W2, L1_gnn_b2, L2_gnn_Ws, L2_gnn_bs, L2_gnn_Wr, L2_gnn_br, L2_gnn_aw, L2_gnn_ab, L3_gnn_gamma, L3_gnn_beta):
    import jax
    import jax.numpy as jnp

    def _L0_gnn_ref(x, edge_index, val):
        import jax, jax.numpy as jnp
        import numpy as np
        N = 50000
        E = 25000
        D = 64

        def segment_softmax(v, idx, num_segments):
            m = jax.ops.segment_max(v, idx, num_segments=num_segments)
            ex = jnp.exp(v - m[idx])
            s = jax.ops.segment_sum(ex, idx, num_segments=num_segments)
            return ex / (s[idx] + 1e-16)
        n = x.shape[0]
        src = edge_index[0]
        dst = edge_index[1]
        val_i = segment_softmax(val, dst, n)
        val_j = segment_softmax(val, src, n)
        e = val_i + val_j
        alpha = segment_softmax(e.astype(jnp.float32), src, n)
        msg = alpha[:, None] * x[src]
        out = jax.ops.segment_sum(msg, dst, num_segments=n)
        return jax.nn.relu(out)

    def _L1_gnn_ref(x, edge_index, W1, b1, W2, b2):
        import jax, jax.numpy as jnp
        import numpy as np
        N_NODES = 3125
        N_EDGES = 100000

        def _gcn_layer(x, W, b, src, dst, n_nodes):
            h = x @ W
            ones = jnp.ones(src.shape[0], dtype=x.dtype)
            deg = jax.ops.segment_sum(ones, dst, num_segments=n_nodes)
            dinv = jnp.where(deg > 0, jax.lax.rsqrt(deg), 0.0)
            norm = dinv[src] * dinv[dst]
            msg = h[src] * norm[:, None]
            out = jax.ops.segment_sum(msg, dst, num_segments=n_nodes)
            return out + b
        n = x.shape[0]
        loop = jnp.arange(n, dtype=edge_index.dtype)
        src = jnp.concatenate([edge_index[0], loop])
        dst = jnp.concatenate([edge_index[1], loop])
        h = _gcn_layer(x, W1, b1, src, dst, n)
        h = jax.nn.relu(h)
        out = _gcn_layer(h, W2, b2, src, dst, n)
        return out

    def _L2_gnn_ref(x, Ws, bs, Wr, br, aw, ab, senders, receivers):
        import jax, jax.numpy as jnp
        import numpy as np
        N_NODES = 3125
        N_EDGES = 50000
        EMBED_DIM = 64
        NUM_HEADS = 4
        HEAD_DIM = EMBED_DIM // NUM_HEADS

        def mish(x):
            return x * jnp.tanh(jax.nn.softplus(x))
        n = x.shape[0]
        s_proj = jnp.einsum('nf,fhd->nhd', x, Ws) + bs
        r_proj = jnp.einsum('nf,fhd->nhd', x, Wr) + br
        se = s_proj[senders]
        re = r_proj[receivers]
        logits = jnp.einsum('ehd,d->eh', mish(se + re), aw) + ab[0]
        lmax = jax.ops.segment_max(logits, receivers, num_segments=n)
        ex = jnp.exp(logits - lmax[receivers])
        denom = jax.ops.segment_sum(ex, receivers, num_segments=n)
        alpha = ex / denom[receivers]
        out = jax.ops.segment_sum(alpha[..., None] * se, receivers, num_segments=n)
        return out.reshape(n, -1)

    def _L3_gnn_ref(h, ef, gamma, beta, src, dst):
        import jax, jax.numpy as jnp
        import numpy as np
        N_NODES = 50000
        N_EDGES = 25000
        D_FEAT = 64
        AVG_D = float(np.log(17.0))
        EPS_STD = 1e-05
        EPS_BN = 1e-05
        N, d = h.shape
        z = h[src] + h[dst] + ef
        deg = jax.ops.segment_sum(jnp.ones((z.shape[0],), z.dtype), dst, num_segments=N)
        deg_safe = jnp.maximum(deg, 1.0)[:, None]
        has_edge = (deg > 0)[:, None]
        mean = jax.ops.segment_sum(z, dst, num_segments=N) / deg_safe
        mean_sq = jax.ops.segment_sum(z * z, dst, num_segments=N) / deg_safe
        std = jnp.sqrt(jax.nn.relu(mean_sq - mean * mean) + EPS_STD)
        mx = jnp.where(has_edge, jax.ops.segment_max(z, dst, num_segments=N), 0.0)
        mn = jnp.where(has_edge, jax.ops.segment_min(z, dst, num_segments=N), 0.0)
        agg = jnp.concatenate([mean, mx, mn, std], axis=1)
        log_deg = jnp.log(deg + 1.0)
        amp = agg * (log_deg / AVG_D)[:, None]
        att = agg * (AVG_D / jnp.where(deg > 0, log_deg, 1.0))[:, None]
        h_agg = jnp.concatenate([agg, amp, att], axis=1)
        h_agg = jnp.where(has_edge, h_agg, 0.0)
        hc = jnp.concatenate([h, h_agg], axis=1).reshape(N, 13, d).mean(axis=1)
        mu = hc.mean(axis=0)
        var = hc.var(axis=0)
        out = (hc - mu) / jnp.sqrt(var + EPS_BN) * gamma + beta
        return out
    edge_index = jnp.stack([src, dst])
    x = _layernorm(x + _L0_gnn_ref(x, edge_index, edge_weight), axis=-1)
    x = _layernorm(x + _L1_gnn_ref(x, edge_index, L1_gnn_W1, L1_gnn_b1, L1_gnn_W2, L1_gnn_b2), axis=-1)
    x = _layernorm(x + _L2_gnn_ref(x, L2_gnn_Ws, L2_gnn_bs, L2_gnn_Wr, L2_gnn_br, L2_gnn_aw, L2_gnn_ab, src, dst), axis=-1)
    x = _layernorm(x + _L3_gnn_ref(x, edge_attr_64, L3_gnn_gamma, L3_gnn_beta, src, dst), axis=-1)
    return x

_drawn_inputs = setup_inputs


def setup_inputs(seed=0):
    import zlib

    import numpy as np

    out = dict(_drawn_inputs(seed))
    spreads = {'L1_gnn_b1': (0.0, 0.1),
     'L1_gnn_b2': (0.0, 0.1),
     'L2_gnn_bs': (0.0, 0.1),
     'L2_gnn_br': (0.0, 0.8)}
    factors = {}
    for name, (base, spread) in spreads.items():
        noise = np.random.default_rng([zlib.crc32(name.encode()), seed]).standard_normal(out[name].shape)
        drawn = base * np.exp(spread * noise) if base else spread * noise
        out[name] = jnp.asarray(drawn.astype(out[name].dtype))
    for name, factor in factors.items():
        out[name] = (out[name] * factor).astype(out[name].dtype)
    return out
```

```python
import concourse.bass as bass
from concourse import mybir
from contextlib import ExitStack

ALU = mybir.AluOpType
ACT = mybir.ActivationFunctionType
AX = mybir.AxisListType
F32 = mybir.dt.float32
I32 = mybir.dt.int32

P = 128
N = 50000
E = 50000
D = 64
H = 4
HD = D // H
F1 = 128
G = 7
T = 392
NG = T // G
SLOTS = 2
STEPS = NG // SLOTS
NP = P * T
EDGE0 = NP
BOUND0 = 2 * NP
NR = 2 * NP + P
TAIL = E - (P - 1) * T
PADKEY = NP - 1
BIG = 1e30
EPS = 1e-5
LO, HI, SHIFT = 2.0 ** -40, 2.0 ** 40, 2.0 ** 42

CONT, NBIG, MEND, DINV, ALPHA, CNT, SROW, DROW, SIDX, DIDX, RCNT, AMP = range(12)
NM = 12
AVG_D = 2.833213344056216


def edges_of(a):
    return a.rearrange("(p t) w -> p t w", p=P)


def peeled(eng, n, body):
    body(0)
    with eng.Fori(1, n) as i:
        body(i)


def build(nc, x, src, dst, ef, ew, W1, b1, W2, b2, Ws, bs, Wr, br, aw, ab, gamma, beta, out):
    ctx = ExitStack()
    with ctx:
        taken = {}

        def fresh(name):
            taken[name] = taken.get(name, 0) + 1
            return name if taken[name] == 1 else f"{name}_{taken[name]}"

        def sb(name, shape, dt=F32, c=ctx):
            return c.enter_context(nc.sbuf_tensor(fresh(name), shape, dt))

        def ps(name, shape, c):
            return c.enter_context(nc.psum_tensor(fresh(name), shape, F32))

        def sem(name):
            return ctx.enter_context(nc.semaphore(name))

        def dram(name, shape):
            return nc.dram_tensor(name, shape, F32, kind="Internal").ap()

        srcT_d, encT_d = dram("srcT_d", (T, P)), dram("encT_d", (T, P))
        xs_lin, xd_lin = dram("xs_lin", (NP, D)), dram("xd_lin", (NP, D))
        tab_m, tab_s, tab_sr = dram("tab_m", (NP, 1)), dram("tab_s", (NP, 1)), dram("tab_sr", (NP, 2))

        meta_all = sb("meta", [P, T + SLOTS * G, NM])
        meta = meta_all[:, 0:T, :]
        ident = sb("ident", [P, P])
        ones = sb("ones", [P, P])
        iota_p = sb("iota_p", [P, P])
        iota_j = sb("iota_j", [P, T])
        nidx = sb("nidx", [P, T])
        rowtab_all = sb("rowtab", [P, T + SLOTS * G])
        rowtab = rowtab_all[:, 0:T]
        iso = sb("iso", [P, T])
        carryF = sb("carryF", [P, 2, P])
        carryB = sb("carryB", [P, 2, P])
        carryFx = sb("carryFx", [P, 2, P])
        bidx = sb("bidx", [P, 1], I32)
        metaB = sb("metaB", [P, 1, NM])
        epst = sb("epst", [P, 1])
        w1s = sb("w1s", [D, F1]); w2s = sb("w2s", [F1, D]); wsr = sb("wsr", [D + 1, 2 * D])
        b1c = sb("b1c", [F1, 1]); b2b = sb("b2b", [P, D]); awb = sb("awb", [P, D]); abb = sb("abb", [P, 1])
        own2 = sb("own2", [P, 1, D])
        bn = sb("bn", [1, 4, 2 * D])
        s_load = sem("s_load")
        s_const = sem("s_const")
        s_pad = sem("s_pad")
        s_masks = sem("s_masks")
        s_ends = sem("s_ends"); s_rows = sem("s_rows"); s_scanned = sem("s_scanned"); s_cols = sem("s_cols")
        s_act = sem("s_act"); s_dve = sem("s_dve"); s_tr = sem("s_tr"); s_trc = sem("s_trc"); s_st = sem("s_st")
        ctxS = ExitStack()
        skey = sb("skey", [P, T, 4], F32, ctxS)
        dkey = sb("dkey", [P, T, 3], F32, ctxS)
        wt = sb("wt", [P, T], F32, ctxS)
        vi = sb("vi", [P, T], F32, ctxS)
        lower = sb("lower", [P, P], F32, ctxS)
        with ExitStack() as c1:
            a_ps = ps("a_ps", [P, 4, P], c1)
            r_ps = ps("r_ps", [1, 4, P], c1)
            c_ps = ps("c_ps", [P, 512], c1)
            t_ps = ps("t_ps", [P, 4, 512], c1)
            srcI = sb("srcI", [P, T], I32, c1)
            dstI = sb("dstI", [P, T], I32, c1)
            dstF = sb("dstF", [P, T], F32, c1)
            nbr = sb("nbr", [P, 2], I32, c1)
            nbrF = sb("nbrF", [P, 2], F32, c1)
            qI = sb("qI", [P, T], I32, c1)
            qF = sb("qF", [P, T], F32, c1)
            rF = sb("rF", [P, T], F32, c1)
            fx = sb("fx", [P, T], F32, c1)
            eidx = nidx
            pidx = sb("pidx", [P, 1], F32, c1)
            contb = sb("contb", [P, T], F32, c1)
            nbigb = sb("nbigb", [P, T], F32, c1)
            first = sb("first", [P, T], F32, c1)
            last = sb("last", [P, T], F32, c1)
            bend = sb("bend", [P, T], F32, c1)
            isend = sb("isend", [P, T], F32, c1)
            cc = sb("cc", [P, 4], F32, c1)
            dg = sb("dg", [P, 3, P], F32, c1)
            rowA = sb("rowA", [P, 3, P], F32, c1)
            carryBx = sb("carryBx", [P, 2, P], F32, c1)
            Fs = sb("Fs", [P, T], F32, c1)
            Bs = sb("Bs", [P, T], F32, c1)
            ur = sb("ur", [1, 2, P], F32, c1)
            ct = sb("ct", [1, 2, P], F32, c1)
            cb = sb("cb", [P, 2], F32, c1)
            wm = sb("wm", [P, T], F32, c1)
            ex = sb("ex", [P, T], F32, c1)
            on = sb("on", [P, T], F32, c1)
            tmp = sb("tmp", [P, T], F32, c1)
            tmp2 = sb("tmp2", [P, T], F32, c1)
            tout = sb("tout", [P, 8, P], F32, c1)

            with nc.Block() as block:
                @block.sync
                def _(sp):
                    sp.wait_ge(s_pad, 1)
                    for t, a in ((srcI, src), (dstI, dst)):
                        v = a.rearrange("(n w) -> n w", w=1)
                        sp.dma_start(t[0:P - 1, :], a[0:(P - 1) * T].rearrange("(p t) -> p t", t=T)).then_inc(s_load, 16)
                        sp.dma_start(t[P - 1:P, 0:TAIL], a[(P - 1) * T:E].rearrange("(p t) -> p t", p=1)).then_inc(s_load, 16)
                    sp.dma_start(wt[0:P - 1, :], ew[0:(P - 1) * T].rearrange("(p t) -> p t", t=T)).then_inc(s_load, 16)
                    sp.dma_start(wt[P - 1:P, 0:TAIL], ew[(P - 1) * T:E].rearrange("(p t) -> p t", p=1)).then_inc(s_load, 16)
                    per = dst[0:(P - 1) * T].rearrange("(p t) -> p t", t=T)
                    nxt = dst[0:(P - 1) * T].rearrange("(p t) -> p t", t=T)
                    sp.dma_start(nbr[1:P, 0:1], per[:, T - 1:T], allow_slow_non_contiguous=True).then_inc(s_load, 16)
                    sp.dma_start(nbr[0:P - 2, 1:2], nxt[1:P - 1, 0:1], allow_slow_non_contiguous=True).then_inc(s_load, 16)
                    sp.dma_start(nbr[P - 2:P - 1, 1:2], dst[(P - 1) * T:(P - 1) * T + 1].rearrange("(p t) -> p t", t=1), allow_slow_non_contiguous=True).then_inc(s_load, 16)
                    for k, d in enumerate((srcT_d, encT_d)):
                        for c in range(4):
                            rows = min(P, T - c * P)
                            sp.wait_ge(s_trc, k * 4 + c + 1)
                            sp.dma_start(d[c * P:c * P + rows, :], tout[0:rows, k * 4 + c, :]).then_inc(s_st, 16)
                    sp.wait_ge(s_st, 8 * 16)

                @block.gpsimd
                def _(pool):
                    pool.iota(iota_p[:, :], [[1, P]], base=0, channel_multiplier=0, allow_small_or_imprecise_dtypes=True)
                    pool.iota(iota_j[:, :], [[1, T]], base=0, channel_multiplier=0, allow_small_or_imprecise_dtypes=True)
                    pool.iota(eidx[:, :], [[1, T]], base=0, channel_multiplier=T, allow_small_or_imprecise_dtypes=True)
                    pool.iota(pidx[:, :], [[1, 1]], base=0, channel_multiplier=1, allow_small_or_imprecise_dtypes=True).then_inc(s_const, 1)

                @block.tensor
                def _(pe):
                    pe.wait_ge(s_masks, 1)
                    for k in range(3):
                        nc.tensor.matmul(a_ps[:, k, :], ones[:, :], dg[:, k, :], start=True, stop=True).then_inc(s_rows, 1)
                    for k in range(4):
                        pe.wait_ge(s_ends, k + 1)
                        nc.tensor.transpose(r_ps[0:1, 0, :], Fs[:, T - 1:T], ident[:, :])
                        nc.tensor.transpose(r_ps[0:1, 1, :], Bs[:, 0:1], ident[:, :]).then_inc(s_rows, 1)
                        pe.wait_ge(s_scanned, k + 1)
                        nc.tensor.transpose(c_ps[:, 0:1], ct[0:1, 0, :], ident[0:1, 0:1])
                        nc.tensor.transpose(c_ps[:, 1:2], ct[0:1, 1, :], ident[0:1, 0:1]).then_inc(s_cols, 1)
                    pe.wait_ge(s_tr, 1)
                    for k, f in enumerate((0, 3)):
                        for c in range(4):
                            rows = min(P, T - c * P)
                            n = k * 4 + c
                            if n >= 4:
                                pe.wait_ge(s_trc, n - 3)
                            nc.tensor.transpose(t_ps[0:rows, n % 4, 0:P], skey[:, c * P:c * P + rows, f], ident[:, :]).then_inc(s_dve, 1)

                @block.scalar
                def _(act):
                    act.wait_ge(s_act, 1)
                    nc.scalar.activation(ex[:, :], tmp[:, :], ACT.Exp).then_inc(s_act, 1)
                    act.wait_ge(s_act, 3)
                    nc.scalar.activation(tmp2[:, :], meta[:, :, CNT], ACT.Sqrt, bias=ones[:, 0:1], scale=1.0).then_inc(s_act, 1)
                    act.wait_ge(s_act, 5)
                    nc.scalar.activation(tmp2[:, :], tmp2[:, :], ACT.Ln).then_inc(s_act, 1)
                    for n in range(8):
                        rows = min(P, T - (n % 4) * P)
                        act.wait_ge(s_dve, n + 1)
                        nc.scalar.copy(tout[0:rows, n, :], t_ps[0:rows, n % 4, 0:P]).then_inc(s_trc, 1)

                @block.vector
                def _(dve):
                    V = nc.vector
                    V.memset(srcI[:, :], PADKEY)
                    V.memset(dstI[:, :], PADKEY)
                    V.memset(nbr[:, :], -1)
                    V.memset(ones[:, :], 1.0)
                    V.memset(on[:, :], 1.0)
                    V.memset(wt[:, :], 0.0)
                    V.memset(meta_all[:, :, :], 0.0)
                    V.memset(metaB[:, :, :], 0.0)
                    V.memset(epst[:, :], EPS)
                    V.memset(rowtab_all[:, :], 0.0)
                    dve.drain()
                    V.memset(cc[:, :], 0.0).then_inc(s_pad, 1)
                    dve.wait_ge(s_const, 1)
                    V.tensor_scalar(ident[:, :], iota_p[:, :], pidx[:, 0:1], None, ALU.is_equal)
                    V.tensor_scalar(lower[:, :], iota_p[:, :], pidx[:, 0:1], None, ALU.is_lt)
                    dve.wait_ge(s_load, 9 * 16)
                    V.tensor_copy(skey[:, :, 0], srcI[:, :])
                    V.tensor_copy(nbrF[:, :], nbr[:, :])
                    V.tensor_copy(dstF[:, :], dstI[:, :])
                    dve.drain()
                    for key, kp, kj in ((skey[:, :, 0], skey[:, :, 1], skey[:, :, 2]), (dstF[:, :], dkey[:, :, 0], dkey[:, :, 1])):
                        V.tensor_scalar(qI[:, :], key, 1.0 / T, None, ALU.mult)
                        dve.drain()
                        V.tensor_copy(qF[:, :], qI[:, :])
                        dve.drain()
                        V.scalar_tensor_tensor(rF[:, :], qF[:, :], -float(T), key, ALU.mult, ALU.add)
                        dve.drain()
                        V.tensor_scalar(fx[:, :], rF[:, :], 0.0, None, ALU.is_lt)
                        dve.drain()
                        V.tensor_tensor(qF[:, :], qF[:, :], fx[:, :], ALU.subtract)
                        V.scalar_tensor_tensor(rF[:, :], fx[:, :], float(T), rF[:, :], ALU.mult, ALU.add)
                        dve.drain()
                        V.tensor_scalar(fx[:, :], rF[:, :], float(T), None, ALU.is_ge)
                        dve.drain()
                        V.tensor_tensor(kp, qF[:, :], fx[:, :], ALU.add)
                        V.scalar_tensor_tensor(kj, fx[:, :], -float(T), rF[:, :], ALU.mult, ALU.add)
                        dve.drain()
                    V.tensor_scalar(meta[:, :, SIDX], skey[:, :, 0], float(N - 1), None, ALU.min)
                    V.tensor_scalar(meta[:, :, DIDX], dstF[:, :], float(N - 1), None, ALU.min)
                    V.tensor_tensor(meta[:, 1:T, CONT], dstF[:, 1:T], dstF[:, 0:T - 1], ALU.is_equal)
                    V.memset(contb[:, :], 0.0)
                    V.tensor_tensor(cc[:, 0:1], dstF[:, 0:1], nbrF[:, 0:1], ALU.is_equal)
                    V.tensor_tensor(cc[:, 1:2], dstF[:, T - 1:T], nbrF[:, 1:2], ALU.is_equal)
                    V.tensor_tensor(cc[:, 2:3], dstF[:, 0:1], dstF[:, T - 1:T], ALU.is_equal)
                    V.tensor_scalar(first[:, :], dstF[:, :], dstF[:, 0:1], None, ALU.is_equal)
                    V.tensor_scalar(last[:, :], dstF[:, :], dstF[:, T - 1:T], None, ALU.is_equal)
                    dve.drain()
                    V.tensor_copy(contb[:, 0:T - 1], meta[:, 1:T, CONT])
                    V.tensor_scalar(isend[:, 0:T - 1], meta[:, 1:T, CONT], -1.0, 1.0, ALU.mult, ALU.add)
                    V.tensor_scalar(isend[:, T - 1:T], cc[:, 1:2], -1.0, 1.0, ALU.mult, ALU.add)
                    V.tensor_scalar(meta[:, :, NBIG], meta[:, :, CONT], BIG, -BIG, ALU.mult, ALU.add)
                    for k in range(3):
                        V.tensor_scalar(dg[:, k, :], ident[:, :], cc[:, k:k + 1], None, ALU.mult)
                    dve.drain()
                    V.tensor_scalar(nbigb[:, :], contb[:, :], BIG, -BIG, ALU.mult, ALU.add).then_inc(s_masks, 1)
                    V.scalar_tensor_tensor(bend[:, :], isend[:, :], cc[:, 0:1], first[:, :], ALU.mult, ALU.mult)
                    dve.drain()
                    V.tensor_tensor(meta[:, :, MEND], isend[:, :], bend[:, :], ALU.subtract)
                    V.tensor_tensor(tmp[:, :], bend[:, :], eidx[:, :], ALU.mult)
                    dve.drain()
                    V.tensor_reduce(cb[:, 0:1], tmp[:, :], AX.X, ALU.add)
                    V.scalar_tensor_tensor(tmp2[:, :], eidx[:, :], float(EDGE0), meta[:, :, MEND], ALU.add, ALU.mult)
                    V.tensor_scalar(cc[:, 3:4], pidx[:, 0:1], float(BOUND0), None, ALU.add)
                    dve.drain()
                    V.tensor_copy(bidx[:, :], cb[:, 0:1])
                    V.scalar_tensor_tensor(dkey[:, :, 2], bend[:, :], cc[:, 3:4], tmp2[:, :], ALU.mult, ALU.add)
                    dve.wait_ge(s_rows, 3)
                    V.tensor_copy(rowA[:, :, :], a_ps[:, 0:3, :])
                    V.memset(carryF[:, :, :], 0.0)
                    V.memset(carryB[:, :, :], 0.0)
                    dve.drain()
                    V.tensor_copy(carryF[:, 1, 1:P], rowA[:, 0, 1:P])
                    V.tensor_tensor(carryF[:, 0, 1:P], rowA[:, 0, 1:P], rowA[:, 2, 0:P - 1], ALU.mult)
                    V.tensor_copy(carryB[:, 1, 0:P - 1], rowA[:, 1, 0:P - 1])
                    V.tensor_tensor(carryB[:, 0, 0:P - 1], rowA[:, 1, 0:P - 1], rowA[:, 2, 1:P], ALU.mult)
                    dve.drain()
                    V.tensor_scalar(carryFx[:, :, :], carryF[:, :, :], BIG, -BIG, ALU.mult, ALU.add)
                    V.tensor_scalar(carryBx[:, :, :], carryB[:, :, :], BIG, -BIG, ALU.mult, ALU.add)
                    dve.drain()

                    def total(k, val, res, is_max):
                        o0, o1 = (ALU.add, ALU.max) if is_max else (ALU.mult, ALU.add)
                        a = meta[:, :, NBIG] if is_max else meta[:, :, CONT]
                        b = nbigb if is_max else contb
                        cf, cbk = (carryFx, carryBx) if is_max else (carryF, carryB)
                        init = -BIG if is_max else 0.0
                        V.tensor_tensor_scan(Fs[:, :], a, val, initial=init, op0=o0, op1=o1)
                        V.tensor_tensor_scan(Bs[:, :][:, ::-1], b[:, :][:, ::-1], val[:, ::-1], initial=init, op0=o0, op1=o1).then_inc(s_ends, 1)
                        dve.wait_ge(s_ends, k + 1)
                        V.memset(ur[:, :, :], init)
                        dve.wait_ge(s_rows, 3 + k + 1)
                        dve.drain()
                        m = ALU.add if is_max else ALU.mult
                        V.tensor_tensor(ur[0:1, 0, 1:P], cf[0:1, 1, 1:P], r_ps[0:1, 0, 0:P - 1], m)
                        V.tensor_tensor(ur[0:1, 1, 0:P - 1], cbk[0:1, 1, 0:P - 1], r_ps[0:1, 1, 1:P], m)
                        dve.drain()
                        V.tensor_tensor_scan(ct[0:1, 0, :], cf[0:1, 0, :], ur[0:1, 0, :], initial=init, op0=o0, op1=o1)
                        V.tensor_tensor_scan(ct[0:1, 1, :][:, ::-1], cbk[0:1, 0, :][:, ::-1], ur[0:1, 1, :][:, ::-1], initial=init, op0=o0, op1=o1).then_inc(s_scanned, 1)
                        dve.wait_ge(s_cols, k + 1)
                        if is_max:
                            V.tensor_scalar(tmp[:, :], first[:, :], BIG, -BIG, ALU.mult, ALU.add)
                            V.tensor_scalar(tmp2[:, :], last[:, :], BIG, -BIG, ALU.mult, ALU.add)
                            V.tensor_tensor(res, Fs[:, :], Bs[:, :], ALU.max)
                            V.tensor_copy(cb[:, :], c_ps[:, 0:2])
                            dve.drain()
                            V.scalar_tensor_tensor(res, tmp[:, :], cb[:, 0:1], res, ALU.add, ALU.max)
                            dve.drain()
                            V.scalar_tensor_tensor(res, tmp2[:, :], cb[:, 1:2], res, ALU.add, ALU.max)
                        else:
                            V.tensor_tensor(res, Fs[:, :], Bs[:, :], ALU.add)
                            V.tensor_copy(cb[:, :], c_ps[:, 0:2])
                            dve.drain()
                            V.tensor_tensor(res, res, val, ALU.subtract)
                            dve.drain()
                            V.scalar_tensor_tensor(res, first[:, :], cb[:, 0:1], res, ALU.mult, ALU.add)
                            dve.drain()
                            V.scalar_tensor_tensor(res, last[:, :], cb[:, 1:2], res, ALU.mult, ALU.add)
                        dve.drain()

                    total(0, wt[:, :], wm[:, :], True)
                    V.tensor_tensor(tmp[:, :], wt[:, :], wm[:, :], ALU.subtract).then_inc(s_act, 1)
                    dve.drain()
                    V.tensor_scalar(wm[:, :], wt[:, :], -1.0, None, ALU.mult)
                    dve.drain()
                    V.tensor_tensor(wm[:, :], wm[:, :], wt[:, :], ALU.max)
                    V.tensor_scalar(fx[:, :], wt[:, :], 0.0, None, ALU.is_ge)
                    dve.drain()
                    V.tensor_scalar(wm[:, :], wm[:, :], LO, HI, ALU.max, ALU.min)
                    dve.drain()
                    V.tensor_scalar(qF[:, :], wm[:, :], SHIFT, None, ALU.mult)
                    V.tensor_scalar(tmp2[:, :].bitcast(I32), wm[:, :].bitcast(I32), 0x7FFFFFFF, None, ALU.bitwise_xor)
                    dve.drain()
                    V.tensor_scalar(rF[:, :], tmp2[:, :], 1.0 / SHIFT, None, ALU.mult)
                    dve.drain()
                    V.copy_predicated(rF[:, :], fx[:, :].bitcast(I32), qF[:, :])
                    dve.drain()
                    V.tensor_copy(skey[:, :, 3], rF[:, :]).then_inc(s_tr, 1)
                    dve.wait_ge(s_act, 2)
                    total(1, ex[:, :], wm[:, :], False)
                    V.tensor_scalar(wm[:, :], wm[:, :], 1e-16, None, ALU.add)
                    dve.drain()
                    V.reciprocal(wm[:, :], wm[:, :])
                    dve.drain()
                    V.tensor_tensor(vi[:, :], ex[:, :], wm[:, :], ALU.mult)
                    total(2, on[:, :], meta[:, :, CNT], False)
                    V.tensor_copy(cb[:, 0:1], cb[:, 1:2])
                    dve.drain()
                    V.memset(cc[:, 3:4], 0.0).then_inc(s_act, 1)
                    dve.wait_ge(s_act, 4)
                    V.reciprocal(meta[:, :, DINV], tmp2[:, :])
                    V.tensor_copy(tmp[:, :], dkey[:, :, 2])
                    dve.drain()
                    total(3, tmp[:, :], meta[:, :, DROW], False)
                    V.scalar_tensor_tensor(meta[:, :, MEND], dstF[:, :], float(N), meta[:, :, MEND], ALU.is_lt, ALU.mult)
                    V.tensor_scalar(meta[:, :, DROW], meta[:, :, DROW], -float(EDGE0), None, ALU.add)
                    V.reciprocal(meta[:, :, RCNT], meta[:, :, CNT])
                    V.tensor_scalar(tmp2[:, :], meta[:, :, CNT], 1.0, None, ALU.add).then_inc(s_act, 1)
                    dve.wait_ge(s_act, 6)
                    V.reciprocal(fx[:, :], tmp2[:, :])
                    V.tensor_scalar(tmp2[:, :], tmp2[:, :], 1.0 / AVG_D, 1.0, ALU.mult, ALU.add)
                    dve.drain()
                    V.scalar_tensor_tensor(meta[:, :, AMP], fx[:, :], AVG_D, tmp2[:, :], ALU.mult, ALU.add)
                    dve.drain()
                    for f in (DINV, RCNT, AMP):
                        V.tensor_tensor(tmp[:, :], meta[:, :, f], bend[:, :], ALU.mult)
                        dve.drain()
                        V.tensor_reduce(metaB[:, :, f], tmp[:, :].unsqueeze(1), AX.X, ALU.add)
                        dve.drain()
                    V.tensor_reduce(metaB[:, :, MEND], bend[:, :].unsqueeze(1), AX.X, ALU.add)
        tbl = sb("tbl", [P, T], F32, ctxS)
        sr = sb("sr", [P, T, 2], F32, ctxS)
        s_idx = sem("s_idx"); s_row = [sem(f"s_row{k}") for k in range(SLOTS)]
        s_gx = [sem(f"s_gx{k}") for k in range(SLOTS)]; s_sx = [sem(f"s_sx{k}") for k in range(SLOTS)]
        s_hot = sem("s_hot"); s_mm = sem("s_mm"); s_rmw = sem("s_rmw"); s_eq = sem("s_eq"); s_turn = sem("s_turn")
        s_tab = sem("s_tab")
        with ExitStack() as c1:
            pt = ps("pt", [P, G, 512], c1)
            srow = sb("srow", [P, SLOTS, G, P], F32, c1)
            erow = sb("erow", [P, SLOTS, G, P], F32, c1)
            xi = sb("xi", [P, SLOTS, 2, G], I32, c1)
            xg = sb("xg", [P, SLOTS, 2, G, D], F32, c1)
            ks = sb("ks", [P, SLOTS, G, 4], F32, c1)
            eq = sb("eq", [P, G, P], F32, c1)
            ev = sb("ev", [P, G, P], F32, c1)
            vt = sb("vt", [P, G], F32, c1)
            lt = sb("lt", [P, G], F32, c1)
            hp = sb("hp", [P, SLOTS, G, P], F32, c1)
            hj = sb("hj", [P, SLOTS, G, T], F32, c1)
            dec = sb("dec", [P, T], F32, c1)
            dec2 = sb("dec2", [P, T], F32, c1)
            with nc.Block() as block:
                @block.sync
                def _(sp):
                    def body(i):
                        for k in range(SLOTS):
                            g = i * SLOTS + k
                            if not isinstance(i, int):
                                sp.wait_ge(s_eq, (i - 1) * SLOTS + k + 1)
                            for d, t in ((srcT_d, srow), (encT_d, erow)):
                                sp.dma_start(t[:, k, :, :], d[bass.ds(g * G, G), :].rearrange("(o a) b -> o a b", o=1).broadcast_to([P, G, P])).then_inc(s_row[k], 16)
                    peeled(sp, STEPS, body)
                    sp.wait_ge(s_tab, 1)
                    sp.dma_start(tab_m.rearrange("(p t) w -> p (t w)", p=P), dec[:, :]).then_inc(s_st, 16)
                    sp.wait_ge(s_st, 9 * 16)

                @block.gpsimd
                def _(pool):
                    def body(i):
                        for k in range(SLOTS):
                            pool.wait_ge(s_idx, i * SLOTS + k + 1)
                            pool.sem_inc(s_turn, 1)
                            if not isinstance(i, int):
                                pool.wait_ge(s_sx[k], i * 32)
                                pool.sem_inc(s_turn, 1)
                            for q in range(2):
                                for t in range(G):
                                    pool.indirect_dma_start(out=xg[:, k, q, t, :], out_offset=None, in_=x, in_offset=bass.IndirectOffsetOnAxis(ap=xi[:, k, q, t:t + 1], axis=0)).then_inc(s_gx[k], 16)
                    peeled(pool, STEPS, body)

                @block.scalar
                def _(act):
                    def store(i, k):
                        for q, d in enumerate((xs_lin, xd_lin)):
                            act.dma_start(edges_of(d)[:, bass.ds((i * SLOTS + k) * G, G), :], xg[:, k, q, :, :]).then_inc(s_sx[k], 16)

                    def body(i):
                        for k in range(SLOTS):
                            j = (i * SLOTS + k) * G
                            if not isinstance(i, int):
                                act.wait_ge(s_gx[k], i * 2 * G * 16)
                                store(i - 1, k)
                            nc.scalar.copy(xi[:, k, 0, :], meta[:, bass.ds(j, G), SIDX])
                            nc.scalar.copy(xi[:, k, 1, :], meta[:, bass.ds(j, G), DIDX]).then_inc(s_idx, 1)
                    peeled(act, STEPS, body)
                    for k in range(SLOTS):
                        act.wait_ge(s_gx[k], STEPS * 2 * G * 16)
                        store(STEPS - 1, k)
                    for k in range(SLOTS):
                        act.wait_ge(s_sx[k], STEPS * 32)

                @block.tensor
                def _(pe):
                    def body(i):
                        for k in range(SLOTS):
                            pe.wait_ge(s_hot, i * SLOTS + k + 1)
                            if k or not isinstance(i, int):
                                pe.wait_ge(s_rmw, i * SLOTS + k)
                            for t in range(G):
                                last = nc.tensor.matmul(pt[:, t, 0:T], hp[:, k, t, :], hj[:, k, t, :], start=True, stop=True)
                            last.then_inc(s_mm, 1)
                    peeled(pe, STEPS, body)

                @block.vector
                def _(dve):
                    V = nc.vector

                    def take(g):
                        dve.wait_ge(s_mm, g + 1)
                        for t in range(G):
                            last = V.tensor_tensor(tbl[:, :], tbl[:, :], pt[:, t, 0:T], ALU.max)
                            if t < G - 1:
                                dve.drain()
                        last.then_inc(s_rmw, 1)

                    def body(i):
                        for k in range(SLOTS):
                            g = i * SLOTS + k
                            V.tensor_copy(ks[:, k, :, :], skey[:, bass.ds(g * G, G), :])
                            dve.drain()
                            dve.wait_ge(s_row[k], i * 32 + 32)
                            V.tensor_tensor(eq[:, :, :], srow[:, k, :, :], ks[:, k, :, 0:1].broadcast_to([P, G, P]), ALU.is_equal)
                            dve.drain()
                            V.tensor_tensor(ev[:, :, :], eq[:, :, :], erow[:, k, :, :], ALU.mult).then_inc(s_eq, 1)
                            dve.drain()
                            V.tensor_reduce(vt[:, :], ev[:, :, :], AX.X, ALU.max)
                            dve.drain()
                            V.tensor_tensor(ev[:, :, :], eq[:, :, :], lower[:, :].unsqueeze(1).broadcast_to([P, G, P]), ALU.mult)
                            dve.drain()
                            V.tensor_reduce(lt[:, :], ev[:, :, :], AX.X, ALU.add)
                            dve.drain()
                            V.scalar_tensor_tensor(vt[:, :], lt[:, :], 0.0, vt[:, :], ALU.is_equal, ALU.mult)
                            dve.drain()
                            if not isinstance(i, int):
                                dve.wait_ge(s_mm, g - 1)
                            for t in range(G):
                                V.tensor_scalar(hp[:, k, t, :], iota_p[:, :], ks[:, k, t, 1:2], vt[:, t:t + 1], ALU.is_equal, ALU.mult)
                                last = V.tensor_scalar(hj[:, k, t, :], iota_j[:, :], ks[:, k, t, 2:3], None, ALU.is_equal)
                            last.then_inc(s_hot, 1)
                            if k or not isinstance(i, int):
                                take(g - 1)
                    V.memset(tbl[:, :], LO / SHIFT / 2)
                    dve.drain()
                    peeled(dve, STEPS, body)
                    take(NG - 1)
                    dve.drain()
                    V.tensor_scalar(dec2[:, :], tbl[:, :], SHIFT, None, ALU.mult)
                    dve.drain()
                    V.tensor_scalar(dec2[:, :].bitcast(I32), dec2[:, :].bitcast(I32), 0x7FFFFFFF, None, ALU.bitwise_xor)
                    dve.drain()
                    V.tensor_scalar(dec[:, :], dec2[:, :], -1.0, None, ALU.mult)
                    dve.drain()
                    V.tensor_scalar(dec2[:, :], tbl[:, :], 1.0 / SHIFT, None, ALU.mult)
                    V.tensor_scalar(sr[:, :, 0], tbl[:, :], 1.0, None, ALU.is_ge)
                    dve.drain()
                    V.tensor_copy(iso[:, :], sr[:, :, 0])
                    dve.drain()
                    V.copy_predicated(dec[:, :], iso[:, :].bitcast(I32), dec2[:, :]).then_inc(s_tab, 1)

        exj = sb("exj", [P, T], F32, ctxS)
        s_gs = [[sem(f"s_gs{n}_{k}") for k in range(SLOTS)] for n in range(3)]
        s_si = [sem(f"s_si{n}") for n in range(3)]
        s_dif = [sem(f"s_dif{n}") for n in range(2)]; s_exp = [sem(f"s_exp{n}") for n in range(2)]
        s_fh = [sem(f"s_fh{n}") for n in range(2)]; s_fm = [sem(f"s_fm{n}") for n in range(2)]
        s_use = sem("s_use")
        for n in range(2):
            with ExitStack() as c1:
                table = (tab_m, tab_s)[n]
                pa = ps("pa", [P, 2, 512], c1)
                gi = sb("gi", [P, SLOTS, G], I32, c1)
                gv = sb("gv", [P, SLOTS, G, 1], F32, c1)
                dif = sb("dif", [P, SLOTS, G], F32, c1)
                zero = sb("zero", [P, P], F32, c1)
                hp = sb("hp", [P, SLOTS, 2, G, P], F32, c1)
                hj = sb("hj", [P, SLOTS, 2, G, T], F32, c1)
                ks = sb("ks", [P, SLOTS, G, 4], F32, c1)
                kd = sb("kd", [P, SLOTS, G, 3], F32, c1)
                nk = 2 if n == 0 else 1
                with nc.Block() as block:
                    @block.sync
                    def _(sp):
                        if n == 0:
                            sp.wait_ge(s_tab, 2)
                            sp.dma_start(tab_s.rearrange("(p t) w -> p (t w)", p=P), tbl[:, :]).then_inc(s_st, 16)
                            sp.wait_ge(s_st, 10 * 16)
                        if n == 1:
                            sp.wait_ge(s_tab, 3)
                            sp.dma_start(tab_sr.rearrange("(p t) w -> p (t w)", p=P), sr[:, :, :].rearrange("p t w -> p (t w)")).then_inc(s_st, 16)
                            sp.wait_ge(s_st, 11 * 16)

                    @block.gpsimd
                    def _(pool):
                        def body(i):
                            for k in range(SLOTS):
                                pool.wait_ge(s_si[n], i * SLOTS + k + 1)
                                pool.sem_inc(s_turn, 1)
                                for t in range(G):
                                    pool.indirect_dma_start(out=gv[:, k, t, :], out_offset=None, in_=table, in_offset=bass.IndirectOffsetOnAxis(ap=gi[:, k, t:t + 1], axis=0)).then_inc(s_gs[n][k], 16)
                        peeled(pool, STEPS, body)

                    @block.scalar
                    def _(act):
                        def exps(g, k):
                            act.wait_ge(s_dif[n], g + 1)
                            nc.scalar.activation(exj[:, bass.ds(g * G, G)], dif[:, k, :], ACT.Exp).then_inc(s_exp[n], 1)

                        def body(i):
                            for k in range(SLOTS):
                                g = i * SLOTS + k
                                if not isinstance(i, int):
                                    act.wait_ge(s_gs[n][k], i * G * 16)
                                    exps(g - SLOTS, k)
                                nc.scalar.copy(gi[:, k, :], skey[:, bass.ds(g * G, G), 0]).then_inc(s_si[n], 1)
                        peeled(act, STEPS, body)
                        for k in range(SLOTS):
                            g = NG - SLOTS + k
                            act.wait_ge(s_gs[n][k], STEPS * G * 16)
                            exps(g, k)

                    @block.tensor
                    def _(pe):
                        pe.wait_ge(s_fh[n], 1)
                        for q in range(nk):
                            nc.tensor.matmul(pa[:, q, 0:T], zero[:, :], iota_j[:, :], start=True, stop=False)

                        def body(i):
                            for k in range(SLOTS):
                                pe.wait_ge(s_fh[n], i * SLOTS + k + 2)
                                for q in range(nk):
                                    for t in range(G):
                                        last = nc.tensor.matmul(pa[:, q, 0:T], hp[:, k, q, t, :], hj[:, k, q, t, :], start=False, stop=False)
                                last.then_inc(s_fm[n], 1)
                        peeled(pe, STEPS, body)
                        for q in range(nk):
                            last = nc.tensor.matmul(pa[:, q, 0:T], zero[:, :], iota_j[:, :], start=False, stop=True)
                        last.then_inc(s_fm[n], 1)

                    @block.vector
                    def _(dve):
                        V = nc.vector
                        V.memset(zero[:, :], 0.0).then_inc(s_fh[n], 1)

                        def body(i):
                            for k in range(SLOTS):
                                g = i * SLOTS + k
                                j = bass.ds(g * G, G)
                                V.tensor_copy(ks[:, k, :, :], skey[:, j, :])
                                if n == 0:
                                    V.tensor_copy(kd[:, k, :, :], dkey[:, j, :])
                                dve.wait_ge(s_gs[n][k], i * G * 16 + G * 16)
                                if n == 0:
                                    V.tensor_tensor(dif[:, k, :], wt[:, j], gv[:, k, :, 0], ALU.subtract).then_inc(s_dif[n], 1)
                                else:
                                    V.tensor_scalar(dif[:, k, :], gv[:, k, :, 0], 1e-16, None, ALU.add)
                                    dve.drain()
                                    V.reciprocal(dif[:, k, :], dif[:, k, :])
                                    dve.drain()
                                    V.tensor_tensor(dif[:, k, :], dif[:, k, :], exj[:, j], ALU.mult)
                                    dve.drain()
                                    V.tensor_tensor(dif[:, k, :], dif[:, k, :], vi[:, j], ALU.add).then_inc(s_dif[n], 1)
                                dve.drain()
                                if not isinstance(i, int):
                                    dve.wait_ge(s_fm[n], g - 1)
                                for t in range(G):
                                    last = V.tensor_scalar(hj[:, k, 0, t, :], iota_j[:, :], ks[:, k, t, 2:3], None, ALU.is_equal)
                                    if n == 0:
                                        V.tensor_scalar(hp[:, k, 1, t, :], iota_p[:, :], kd[:, k, t, 0:1], kd[:, k, t, 2:3], ALU.is_equal, ALU.mult)
                                        V.tensor_scalar(hj[:, k, 1, t, :], iota_j[:, :], kd[:, k, t, 1:2], None, ALU.is_equal)
                                dve.wait_ge(s_exp[n], g + 1)
                                V.tensor_scalar(ks[:, k, :, 3], exj[:, j], 1.0, None, ALU.mult)
                                dve.drain()
                                for t in range(G):
                                    last = V.tensor_scalar(hp[:, k, 0, t, :], iota_p[:, :], ks[:, k, t, 1:2], ks[:, k, t, 3:4], ALU.is_equal, ALU.mult)
                                last.then_inc(s_fh[n], 1)
                        peeled(dve, STEPS, body)
                        dve.wait_ge(s_fm[n], NG + 1)
                        if n == 0:
                            V.tensor_copy(tbl[:, :], pa[:, 0, 0:T]).then_inc(s_tab, 1)
                            V.tensor_scalar(iso[:, :], pa[:, 1, 0:T], 0.0, None, ALU.is_equal)
                            dve.drain()
                            V.scalar_tensor_tensor(rowtab[:, :], nidx[:, :], 1.0, iso[:, :], ALU.mult, ALU.mult)
                            dve.drain()
                            V.tensor_tensor(rowtab[:, :], rowtab[:, :], pa[:, 1, 0:T], ALU.add)
                            V.scalar_tensor_tensor(iso[:, :], nidx[:, :], float(N), iso[:, :], ALU.is_lt, ALU.mult)
                        else:
                            V.tensor_copy(sr[:, :, 0], pa[:, 0, 0:T])
                            V.tensor_copy(sr[:, :, 1], rowtab[:, :])
                            dve.drain()
                            V.memset(zero[:, :], 0.0).then_inc(s_tab, 1)
        T1, T2, T3s, T4 = (dram(f"rows{k}", (NR, D)) for k in range(4))
        T3r = dram("rows_r", (NP + P, D))
        T5 = dram("rows5", (NR, 2 * D))
        S_lin = {w: dram(f"sums{w}", (NP, w)) for w in (D, 72, 4 * D)}
        ef_tail = dram("ef_tail", (T, D))
        PARTS = ((0, 112), (112, 15), (127, 1))

        s_w = sem("s_w")
        s_peturn = sem("s_peturn"); s_spturn = sem("s_spturn")

        def row_stage(tag):
            names = ("ain", "tp", "tc", "hp", "hc", "o", "pin", "ptp", "ptc", "pj", "var", "sd")
            return {k: sem(f"s_{k}_{tag}") for k in names}

        def buffers(c, n=G):
            return dict(
                y=sb("y", [P, n, D], F32, c), sq=sb("sq", [P, n, D], F32, c), mu=sb("mu", [P, n], F32, c),
                va=sb("va", [P, n], F32, c), sd=sb("sd", [P, n], F32, c), rs=sb("rs", [P, n], F32, c))

        def norm_a(dve, B, n, S):
            V = nc.vector
            y = B["y"][:, 0:n, :]
            V.tensor_reduce(B["mu"][:, 0:n], y, AX.X, ALU.add)
            dve.drain()
            V.tensor_scalar(B["mu"][:, 0:n], B["mu"][:, 0:n], -1.0 / D, None, ALU.mult)
            dve.drain()
            V.tensor_tensor(y, y, B["mu"][:, 0:n].unsqueeze(2).broadcast_to([P, n, D]), ALU.add)
            dve.drain()
            V.tensor_tensor(B["sq"][:, 0:n, :], y, y, ALU.mult)
            dve.drain()
            V.tensor_reduce(B["va"][:, 0:n], B["sq"][:, 0:n, :], AX.X, ALU.add).then_inc(S["var"], 1)

        def norm_act(act, B, n, S, count):
            act.wait_ge(S["var"], count)
            nc.scalar.activation(B["sd"][:, 0:n], B["va"][:, 0:n], ACT.Sqrt, bias=epst[:, 0:1], scale=1.0 / D).then_inc(S["sd"], 1)

        def norm_b(dve, B, n, S, count, res):
            V = nc.vector
            dve.wait_ge(S["sd"], count)
            V.reciprocal(B["rs"][:, 0:n], B["sd"][:, 0:n])
            dve.drain()
            V.tensor_tensor(res, B["y"][:, 0:n, :], B["rs"][:, 0:n].unsqueeze(2).broadcast_to([P, n, D]), ALU.mult)

        def mlp_pe(pe, M, n, S, count):
            pe.wait_ge(S["ain"], count)
            pe.sem_inc(s_peturn, 1)
            for t in range(n):
                last = nc.tensor.transpose(M["aTp"][0:D, t * P:(t + 1) * P], M["a"][:, t, :], ident[:, :])
            last.then_inc(S["tp"], 1)
            pe.wait_ge(S["tc"], count)
            for c0 in range(0, n * P, 512):
                c1_ = min(n * P, c0 + 512)
                last = nc.tensor.matmul(M["hTp"][:, c0:c1_], w1s[:, :], M["aT"][0:D, c0:c1_], start=True, stop=True)
            last.then_inc(S["hp"], 1)
            pe.wait_ge(S["hc"], count)
            for t in range(n):
                last = nc.tensor.matmul(M["op"][:, t * D:(t + 1) * D], M["hT"][:, t * P:(t + 1) * P], w2s[:, :], start=True, stop=True)
            last.then_inc(S["o"], 1)

        def mlp_act(act, M, n, S, count):
            act.wait_ge(S["tp"], count)
            nc.scalar.activation(M["aT"][0:D, 0:n * P], M["aTp"][0:D, 0:n * P], ACT.Copy).then_inc(S["tc"], 1)
            act.wait_ge(S["hp"], count)
            nc.scalar.activation(M["hT"][:, 0:n * P], M["hTp"][:, 0:n * P], ACT.Relu, bias=b1c[:, 0:1], scale=1.0).then_inc(S["hc"], 1)

        def proj_pe(pe, M, rows, n, S, count):
            pe.wait_ge(S["pin"], count)
            pe.sem_inc(s_peturn, 1)
            for t in range(n):
                last = nc.tensor.transpose(M["xTp"][0:D, t * P:(t + 1) * P], rows[:, t, :], ident[:, :])
            last.then_inc(S["ptp"], 1)
            pe.wait_ge(S["ptc"], count)
            for t in range(n):
                last = nc.tensor.matmul(M["pj"][:, t * 2 * D:(t + 1) * 2 * D], M["xT"][:, t * P:(t + 1) * P], wsr[:, :], start=True, stop=True)
            last.then_inc(S["pj"], 1)

        def proj_act(act, M, n, S, count):
            act.wait_ge(S["ptp"], count)
            nc.scalar.activation(M["xT"][0:D, 0:n * P], M["xTp"][0:D, 0:n * P], ACT.Copy).then_inc(S["ptc"], 1)

        def mlp_buffers(c, n=G):
            return dict(a=sb("a", [P, n, D], F32, c), aT=sb("aT", [D, n * P], F32, c), hT=sb("hT", [F1, n * P], F32, c),
                        aTp=ps("aTp", [P, 1024], c), hTp=ps("hTp", [P, 1024], c), op=ps("op", [P, 512], c))

        def proj_buffers(c, xTp=None, n=G):
            return dict(xT=sb("xT", [D + 1, n * P], F32, c), xTp=xTp or ps("xTp", [P, 1024], c), pj=ps("pj", [P, 1024], c))

        def wait_used(eng, s, count):
            if not isinstance(count, int) or count > 0:
                eng.wait_ge(s, count)

        def peeled2(eng, n, body):
            body(0)
            body(1)
            with eng.Fori(2, n) as i:
                body(i)

        with ExitStack() as c1:
            s_nst1 = [sem(f"s_nst1_{k}") for k in range(SLOTS)]
            s_nst2 = [sem(f"s_nst2_{k}") for k in range(SLOTS)]
            s_nconst = sem("s_nconst"); s_bnm = sem("s_bnm")
            s_cen, s_sq1, s_va1, s_sd1, s_sq2, s_va2, s_sd2 = (sem(f"s_{k}_n") for k in ("cen", "sq1", "va1", "sd1", "sq2", "va2", "sd2"))
            s_x1, s_x2, s_x3, s_tp, s_tc, s_hp, s_hc, s_op, s_pj, s_o3, s_hq = (sem(f"s_{k}_n") for k in ("x1", "x2", "x3", "tp", "tc", "hp", "hc", "op", "pj", "o3", "hq"))
            gi = sb("gi", [P, SLOTS, G], I32, c1)
            gv = sb("gv", [P, SLOTS, G, 2], F32, c1)
            Xn = sb("Xn", [P, T, D], F32, c1)
            y1 = sb("y1", [P, G, D], F32, c1)
            sq1 = sb("sq1", [P, G, D], F32, c1)
            sq2 = sb("sq2", [P, G, D], F32, c1)
            mu1 = sb("mu1", [P, G], F32, c1)
            va = sb("va", [P, 2, G], F32, c1)
            sd = sb("sd", [P, 3, G], F32, c1)
            rs = sb("rs", [P, 3, G], F32, c1)
            x1 = sb("x1", [P, SLOTS, G, D], F32, c1)
            x2 = sb("x2", [P, G, D], F32, c1)
            o2 = sb("o2", [P, SLOTS, G, D], F32, c1)
            o3 = sb("o3", [P, SLOTS, G, D], F32, c1)
            o5 = sb("o5", [P, SLOTS, G, 3 * D], F32, c1)
            aT = sb("aT", [D + 1, G * P], F32, c1)
            xT = sb("xT", [D + 1, G * P], F32, c1)
            hT = sb("hT", [F1, G * P], F32, c1)
            mk = sb("mk", [P, SLOTS, G], F32, c1)
            zc = sb("zc", [P, 1], F32, c1)
            w2c = sb("w2c", [F1, D], F32, c1)
            cen = sb("cen", [D + 1, D], F32, c1)
            wm = sb("wm", [P, 2], F32, c1)
            eps2 = sb("eps2", [P, 1], F32, c1)
            tps = ps("tps", [P, 1024], c1)
            hTp = ps("hTp", [P, 1024], c1)
            op = ps("op", [P, 1024], c1)
            pj = ps("pj", [P, 512], c1)
            bnp = ps("bnp", [1, 512], c1)
            opg = op[:, 0:G * 2 * D].rearrange("p (t d) -> p t d", d=2 * D)
            with nc.Block() as block:
                @block.sync
                def _(sp):
                    sp.wait_ge(s_nconst, 1)
                    for p0, k in PARTS:
                        w = TAIL if p0 == P - 1 else T
                        sp.dma_start(Xn[p0:p0 + k, 0:w, :], x[p0 * T:p0 * T + (k - 1) * T + w, :].rearrange("(p t) d -> p t d", t=w)).then_inc(s_w, 16)
                    sp.dma_start(w1s[:, :], W1).then_inc(s_w, 16)
                    sp.dma_start(w2s[:, :], W2).then_inc(s_w, 16)
                    sp.dma_start(wsr[0:D, 0:D], Ws.rearrange("f h d -> f (h d)")).then_inc(s_w, 16)
                    sp.dma_start(wsr[0:D, D:2 * D], Wr.rearrange("f h d -> f (h d)")).then_inc(s_w, 16)
                    sp.dma_start(wsr[D:D + 1, 0:D], bs.rearrange("(o h) d -> o (h d)", o=1)).then_inc(s_w, 16)
                    sp.dma_start(wsr[D:D + 1, D:2 * D], br.rearrange("(o h) d -> o (h d)", o=1)).then_inc(s_w, 16)
                    sp.dma_start(b1c[:, :], b1.rearrange("(f o) -> f o", o=1)).then_inc(s_w, 16)
                    sp.dma_start(b2b[:, :], b2.rearrange("(o f) -> o f", o=1).broadcast_to([P, D])).then_inc(s_w, 16)
                    for h in range(H):
                        sp.dma_start(awb[:, h * HD:(h + 1) * HD], aw.rearrange("(o f) -> o f", o=1).broadcast_to([P, HD])).then_inc(s_w, 16)
                    sp.dma_start(abb[:, :], ab.rearrange("(o f) -> o f", o=1).broadcast_to([P, 1])).then_inc(s_w, 16)
                    sp.dma_start(ef_tail[0:TAIL, :], ef[(P - 1) * T:E, :]).then_inc(s_w, 16)
                    sp.dma_start(ef_tail[TAIL:T, :], ef[0:T - TAIL, :]).then_inc(s_w, 16)
                    sp.wait_ge(s_w, 18 * 16)
                    sp.sem_inc(s_w, 1)

                    def rows(t, g):
                        return edges_of(t[0:NP, :])[:, bass.ds(g * G, G), :]

                    def back(g, k):
                        sp.wait_ge(s_o3, g + 1)
                        sp.sem_inc(s_spturn, 1)
                        sp.dma_start(rows(T3s, g), o3[:, k, :, :]).then_inc(s_nst2[k], 16)
                        sp.wait_ge(s_hq, g + 1)
                        sp.sem_inc(s_spturn, 1)
                        sp.dma_start(rows(T4, g), o5[:, k, :, 0:D]).then_inc(s_nst2[k], 16)
                        sp.dma_start(rows(T5, g), o5[:, k, :, 0:2 * D]).then_inc(s_nst2[k], 16)

                    def body(i):
                        for k in range(SLOTS):
                            g = i * SLOTS + k
                            if k or not isinstance(i, int) or i:
                                back(g - 1, 1 - k)
                            sp.wait_ge(s_x1, g + 1)
                            sp.sem_inc(s_spturn, 1)
                            sp.dma_start(rows(T1, g), x1[:, k, :, :]).then_inc(s_nst1[k], 16)
                            sp.wait_ge(s_sq2, g + 1)
                            sp.sem_inc(s_spturn, 1)
                            sp.dma_start(rows(T2, g), o2[:, k, :, :]).then_inc(s_nst1[k], 16)
                    peeled2(sp, STEPS, body)
                    back(NG - 1, 1)
                    for k in range(SLOTS):
                        sp.wait_ge(s_nst1[k], STEPS * 32)
                        sp.wait_ge(s_nst2[k], STEPS * 48)

                @block.gpsimd
                def _(pool):
                    def body(i):
                        for k in range(SLOTS):
                            pool.wait_ge(s_si[2], i * SLOTS + k + 1)
                            pool.sem_inc(s_turn, 1)
                            for t in range(G):
                                pool.indirect_dma_start(out=gv[:, k, t, :], out_offset=None, in_=tab_sr, in_offset=bass.IndirectOffsetOnAxis(ap=gi[:, k, t:t + 1], axis=0)).then_inc(s_gs[2][k], 16)
                    peeled(pool, STEPS, body)

                @block.tensor
                def _(pe):
                    pe.wait_ge(s_nconst, 2)
                    nc.tensor.matmul(bnp[0:1, 0:2 * D], zc[:, :], ident[:, :], start=True, stop=False)

                    def back_rows(g):
                        pe.wait_ge(s_x2, g + 1)
                        pe.sem_inc(s_peturn, 1)
                        for t in range(G):
                            last = nc.tensor.transpose(tps[0:D, t * P:(t + 1) * P], x2[:, t, :], ident[:, :])
                        last.then_inc(s_tp, 1)
                        pe.wait_ge(s_tc, g * 2 + 2)
                        wait_used(pe, s_o3, g)
                        for t in range(G):
                            last = nc.tensor.matmul(pj[:, t * D:(t + 1) * D], xT[:, t * P:(t + 1) * P], wsr[:, 0:D], start=True, stop=True)
                        last.then_inc(s_pj, 1)

                    def front(g, k):
                        pe.wait_ge(s_x1, g + 1)
                        pe.sem_inc(s_peturn, 1)
                        for t in range(G):
                            last = nc.tensor.transpose(tps[0:D, t * P:(t + 1) * P], x1[:, k, t, :], ident[:, :])
                        last.then_inc(s_tp, 1)
                        pe.wait_ge(s_tc, g * 2 + 1)
                        for c0 in range(0, G * P, 512):
                            c1_ = min(G * P, c0 + 512)
                            last = nc.tensor.matmul(hTp[:, c0:c1_], w1s[:, :], aT[0:D, c0:c1_], start=True, stop=True)
                        last.then_inc(s_hp, 1)
                        pe.wait_ge(s_hc, g + 1)
                        wait_used(pe, s_x3, g)
                        for t in range(G):
                            h, a, o = hT[:, t * P:(t + 1) * P], aT[:, t * P:(t + 1) * P], t * 2 * D
                            nc.tensor.matmul(op[:, o:o + D], h, w2s[:, :], start=True, stop=True)
                            nc.tensor.matmul(op[:, o + D:o + 2 * D], h, w2c[:, :], start=True, stop=False)
                            last = nc.tensor.matmul(op[:, o + D:o + 2 * D], a, cen[:, :], start=False, stop=True)
                        last.then_inc(s_op, 1)

                    def back_sums(g, k):
                        pe.wait_ge(s_hq, g + 1)
                        for t in range(G):
                            last = nc.tensor.matmul(bnp[0:1, 0:2 * D], mk[:, k, t:t + 1], o5[:, k, t, D:3 * D], start=False, stop=False)
                        last.then_inc(s_bnm, 1)

                    def body(i):
                        for k in range(SLOTS):
                            g = i * SLOTS + k
                            first = isinstance(i, int) and i + k == 0
                            if not first:
                                back_rows(g - 1)
                            front(g, k)
                            if not first:
                                back_sums(g - 1, 1 - k)
                    peeled2(pe, STEPS, body)
                    back_rows(NG - 1)
                    back_sums(NG - 1, 1)
                    nc.tensor.matmul(bnp[0:1, 0:2 * D], zc[:, :], ident[:, :], start=False, stop=True).then_inc(s_bnm, 1)

                @block.scalar
                def _(act):
                    A = nc.scalar

                    def taken_in(g, k):
                        A.copy(meta[:, bass.ds(g * G, G), ALPHA], gv[:, k, :, 0])
                        A.copy(meta[:, bass.ds(g * G, G), SROW], gv[:, k, :, 1]).then_inc(s_use, 1)

                    def gathers(g, k, i):
                        if not isinstance(i, int) or i:
                            act.wait_ge(s_gs[2][k], i * G * 16)
                            taken_in(g - SLOTS, k)
                            act.wait_ge(s_use, g - 1)
                        A.copy(gi[:, k, :], skey[:, bass.ds(g * G, G), 0]).then_inc(s_si[2], 1)

                    def front_squares(g):
                        act.wait_ge(s_cen, g + 1)
                        A.activation(sq1[:, :, :], y1[:, :, :], ACT.Square).then_inc(s_sq1, 1)

                    def front_deviation(g):
                        act.wait_ge(s_va1, g + 1)
                        A.activation(sd[:, 0, :], va[:, 0, :], ACT.Sqrt, bias=epst[:, 0:1], scale=1.0 / D).then_inc(s_sd1, 1)

                    def front_products(g, k, used):
                        act.wait_ge(s_tp, g * 2 + 1)
                        A.activation(aT[0:D, :], tps[0:D, 0:G * P], ACT.Copy).then_inc(s_tc, 1)
                        act.wait_ge(s_hp, g + 1)
                        A.activation(hT[:, :], hTp[:, 0:G * P], ACT.Relu, bias=b1c[:, 0:1], scale=1.0).then_inc(s_hc, 1)

                    def front_results(g, k, used):
                        wait_used(act, s_nst1[k], used * 32)
                        act.wait_ge(s_op, g + 1)
                        A.activation(o2[:, k, :, :], opg[:, :, 0:D], ACT.Copy)
                        A.activation(sq2[:, :, :], opg[:, :, D:2 * D], ACT.Square).then_inc(s_sq2, 1)

                    def back_deviations(g):
                        act.wait_ge(s_va2, g + 1)
                        A.activation(sd[:, 1, :], va[:, 1, :], ACT.Sqrt, bias=epst[:, 0:1], scale=1.0 / D)
                        A.activation(sd[:, 2, :], va[:, 1, :], ACT.Sqrt, bias=eps2[:, 0:1], scale=(1.0 + EPS) / D).then_inc(s_sd2, 1)

                    def back_rows(g):
                        act.wait_ge(s_tp, g * 2 + 2)
                        A.activation(xT[0:D, :], tps[0:D, 0:G * P], ACT.Copy).then_inc(s_tc, 1)

                    def back_results(g, k, used):
                        wait_used(act, s_nst2[k], used * 48)
                        act.wait_ge(s_pj, g + 1)
                        A.activation(o3[:, k, :, :], pj[:, 0:G * D].rearrange("p (t d) -> p t d", d=D), ACT.Copy).then_inc(s_o3, 1)
                        act.wait_ge(s_x3, g + 1)
                        A.activation(o5[:, k, :, 2 * D:3 * D], o5[:, k, :, 0:D], ACT.Square, scale=1.0 / 13).then_inc(s_hq, 1)

                    act.wait_ge(s_nconst, 2)

                    def body(i):
                        for k in range(SLOTS):
                            g = i * SLOTS + k
                            first = isinstance(i, int) and i + k == 0
                            gathers(g, k, i)
                            front_squares(g)
                            if not first:
                                back_deviations(g - 1)
                            front_deviation(g)
                            if not first:
                                back_rows(g - 1)
                            front_products(g, k, i)
                            if not first:
                                back_results(g - 1, 1 - k, i - 1 + k)
                            front_results(g, k, i)
                    peeled2(act, STEPS, body)
                    back_deviations(NG - 1)
                    back_rows(NG - 1)
                    back_results(NG - 1, 1, STEPS - 1)
                    for k in range(SLOTS):
                        act.wait_ge(s_gs[2][k], STEPS * G * 16)
                        taken_in(NG - SLOTS + k, k)

                @block.vector
                def _(dve):
                    V = nc.vector
                    V.memset(Xn[96:P, TAIL:T, :], 0.0)
                    V.memset(aT[D:D + 1, :], 1.0)
                    V.memset(xT[D:D + 1, :], 1.0)
                    V.memset(bn[:, :, :], 0.0)
                    V.memset(eps2[:, :], EPS * EPS)
                    V.memset(zc[:, :], 0.0)
                    dve.drain()
                    V.memset(wm[:, :], 0.0).then_inc(s_nconst, 1)
                    dve.wait_ge(s_w, 18 * 16 + 1)
                    dve.drain()
                    V.tensor_reduce(wm[:, 0:1], w2s[:, :], AX.X, ALU.add)
                    V.tensor_reduce(wm[D:D + 1, 1:2], b2b[D:D + 1, :], AX.X, ALU.add)
                    V.tensor_scalar(cen[0:D, :], ident[0:D, 0:D], 1.0 / D, None, ALU.subtract)
                    dve.drain()
                    V.tensor_scalar(wm[:, :], wm[:, :], 1.0 / D, None, ALU.mult)
                    dve.drain()
                    V.tensor_scalar(w2c[:, :], w2s[:, :], wm[:, 0:1], None, ALU.subtract)
                    V.tensor_scalar(cen[D:D + 1, :], b2b[D:D + 1, :], wm[D:D + 1, 1:2], None, ALU.subtract)
                    dve.drain()
                    V.memset(wm[:, :], 0.0).then_inc(s_nconst, 1)

                    def wide(v):
                        return v.unsqueeze(2).broadcast_to([P, G, D])

                    def centre(g):
                        xv = Xn[:, bass.ds(g * G, G), :]
                        V.tensor_reduce(mu1[:, :], xv, AX.X, ALU.add)
                        dve.drain()
                        V.scalar_tensor_tensor(y1[:, :, :], wide(mu1[:, :]), -1.0 / D, xv, ALU.mult, ALU.add).then_inc(s_cen, 1)

                    def front_sums(g):
                        dve.wait_ge(s_sq1, g + 1)
                        V.tensor_reduce(va[:, 0, :], sq1[:, :, :], AX.X, ALU.add).then_inc(s_va1, 1)

                    def front_norm(g, k, used):
                        wait_used(dve, s_nst1[k], used * 32)
                        dve.wait_ge(s_sd1, g + 1)
                        V.reciprocal(rs[:, 0, :], sd[:, 0, :])
                        dve.drain()
                        V.tensor_tensor(x1[:, k, :, :], y1[:, :, :], wide(rs[:, 0, :]), ALU.mult).then_inc(s_x1, 1)

                    def back_sums(g):
                        dve.wait_ge(s_sq2, g + 1)
                        V.tensor_reduce(va[:, 1, :], sq2[:, :, :], AX.X, ALU.add).then_inc(s_va2, 1)

                    def back_norm(g, k, used):
                        wait_used(dve, s_nst2[k], used * 48)
                        wait_used(dve, s_bnm, g - 1)
                        V.tensor_scalar(mk[:, k, :], iso[:, bass.ds(g * G, G)], 1.0, None, ALU.mult)
                        dve.wait_ge(s_sd2, g + 1)
                        V.reciprocal(rs[:, 1:3, :], sd[:, 1:3, :])
                        dve.drain()
                        V.tensor_tensor(x2[:, :, :], opg[:, :, D:2 * D], wide(rs[:, 1, :]), ALU.mult).then_inc(s_x2, 1)
                        V.tensor_tensor(o5[:, k, :, 0:D], opg[:, :, D:2 * D], wide(rs[:, 2, :]), ALU.mult)
                        dve.drain()
                        V.tensor_scalar(o5[:, k, :, D:2 * D], o5[:, k, :, 0:D], 1.0 / 13, None, ALU.mult).then_inc(s_x3, 1)

                    def body(i):
                        for k in range(SLOTS):
                            g = i * SLOTS + k
                            first = isinstance(i, int) and i + k == 0
                            centre(g)
                            if not first:
                                back_sums(g - 1)
                            front_sums(g)
                            if not first:
                                back_norm(g - 1, 1 - k, i - 1 + k)
                            front_norm(g, k, i)
                    peeled2(dve, STEPS, body)
                    back_sums(NG - 1)
                    back_norm(NG - 1, 1, STEPS - 1)
                    dve.wait_ge(s_bnm, NG + 1)
                    V.tensor_copy(bn[0:1, 0, :], bnp[0:1, 0:2 * D])
                    dve.wait_ge(s_use, NG)
                    V.tensor_scalar(meta[:, :, ALPHA], meta[:, :, ALPHA], 1e-16, None, ALU.add)
                    dve.drain()
                    V.reciprocal(meta[:, :, ALPHA], meta[:, :, ALPHA])
                    dve.drain()
                    V.tensor_tensor(meta[:, :, ALPHA], meta[:, :, ALPHA], exj[:, :], ALU.mult)
        ctxS.close()
        X = sb("X", [P, T, D])
        XB = sb("XB", [P, 1, D])
        roles = {}

        def edge_phase(kind):
            W = {"gat": 72, "pna": 4 * D}.get(kind, D)
            S_d = S_lin[W]
            normed = kind in ("att", "gcn2", "gat")
            gathered = {"att": (), "gcn1": ((T1, SROW),), "gcn2": ((T2, SROW),), "gat": ((T3s, SROW), (T3r, DROW)),
                        "pna": ((T4, SROW),)}[kind]
            linear = {"att": 1, "gcn2": 1, "pna": 3}.get(kind, 0)
            outs = {"att": ((T1, D),), "gcn1": ((T2, D),), "gcn2": ((T3s, D), (T3r, D)), "gat": ((T4, D),), "pna": ((T5, 2 * D),)}[kind]
            lag = 1 if kind in ("att", "gcn1", "pna") else 2
            S = {}

            def psem(name):
                if name not in roles:
                    roles[name] = sem("edge_" + name[2:])
                return roles[name]

            for name in {"att": ("var", "sd"), "gcn1": ("ain", "tp", "tc", "hp", "hc", "o"), "gcn2": ("var", "sd", "pin", "ptp", "ptc", "pj"),
                         "gat": ("var", "sd", "z", "u", "dm", "f"), "pna": ("var", "sd", "hq", "bn")}[kind]:
                S[name] = psem(f"s_{name}")
            s_acc = psem("s_acc"); s_res = psem("s_res"); s_used = psem("s_used")
            s_idx = psem("s_idx"); s_bc = psem("s_bc"); s_bp = psem("s_bp"); s_xl = psem("s_xl"); s_bs = psem("s_bs"); s_bt = psem("s_bt")
            s_g = [sem(f"s_g{k}_{kind}") for k in range(SLOTS)]
            s_l = [psem(f"s_l{k}") for k in range(SLOTS)]
            s_so = [psem(f"s_so{k}") for k in range(SLOTS)]
            s_ro = [psem(f"s_ro{k}") for k in range(SLOTS)]
            per_gather = G * 16 * len(gathered)
            with ExitStack() as c1:
                B = buffers(c1) if normed else None
                M = mlp_buffers(c1) if kind == "gcn1" else None
                J = proj_buffers(c1) if kind == "gcn2" else None
                xr = sb("xr", [P, G, D], F32, c1) if kind == "gcn2" else None
                cps = ps("cps", [P, 2, 512], c1)
                idx = sb("idx", [P, SLOTS, 2, G], I32, c1)
                gx = sb("gx", [P, SLOTS, max(1, len(gathered)), G, D], F32, c1)
                lx = sb("lx", [P, SLOTS, G, D], F32, c1) if linear else None
                acc = sb("acc", [P, SLOTS * G, W], F32, c1)
                md = sb("md", [P, SLOTS, G, NM], F32, c1)
                msg = sb("msg", [P, G, W], F32, c1)
                res = [sb("res", [P, SLOTS, G, w], F32, c1) for _, w in outs]
                sB = sb("sB", [P, 1, W], F32, c1)
                cr = sb("cr", [P, 2, P], F32, c1)
                ct = sb("ct", [P, 2, P], F32, c1)
                if kind == "pna":
                    hb = sb("hb", [P, G, D], F32, c1)
                    mm = sb("mm", [P, G, D], F32, c1)
                    hq = sb("hq", [P, G, 2 * D], F32, c1)
                    zc = sb("zc", [P, 1], F32, c1)
                    bnp = ps("bnp", [1, 512], c1)
                if kind == "gat":
                    zz = sb("zz", [P, SLOTS, G, D], F32, c1)
                    uu = sb("uu", [P, SLOTS, G, D], F32, c1)
                    t1 = sb("t1", [P, G, D], F32, c1)
                    t2 = sb("t2", [P, G, D], F32, c1)
                    lg = sb("lg", [P, G, H], F32, c1)
                    dm = sb("dm", [P, 2, G, H], F32, c1)
                    ff = sb("ff", [P, 2, G, H], F32, c1)
                    mx = sb("mx", [P, SLOTS * G, H], F32, c1)
                    mB = sb("mB", [P, 2, H], F32, c1)
                    m68 = sb("m68", [P, 4, 68], F32, c1)
                    fB = sb("fB", [P, 2, P], F32, c1)

                def has(i, k, n):
                    return not isinstance(i, int) or i * SLOTS + k >= n

                with nc.Block() as block:
                    @block.sync
                    def _(sp):
                        if kind == "att":
                            sp.dma_start(X[:, :, :], edges_of(xd_lin)).then_inc(s_xl, 16)

                        def store_sums(g, n, k):
                            sp.wait_ge(s_acc, g + 1)
                            sp.sem_inc(s_spturn, 1)
                            sp.dma_start(edges_of(S_d)[:, bass.ds(g * G, G), :], acc[:, k * G:(k + 1) * G, :]).then_inc(s_so[k], 16)

                        def store_rows(g, k):
                            sp.wait_ge(s_res, g + 1)
                            sp.sem_inc(s_spturn, 1)
                            for (d, w), r in zip(outs, res):
                                base = 0 if d is T3r else EDGE0
                                sp.dma_start(edges_of(d[base:base + NP, :])[:, bass.ds(g * G, G), :], r[:, k, :, :]).then_inc(s_ro[k], 16)

                        def load(i, k):
                            g = i * SLOTS + k
                            j = bass.ds(g * G, G)
                            if has(i, k, 2) and linear:
                                sp.wait_ge(s_used, g - 1 + (SLOTS if gathered else 0))
                                sp.sem_inc(s_spturn, 1)
                            if kind == "att":
                                sp.dma_start(lx[:, k, :, :], edges_of(xs_lin)[:, j, :]).then_inc(s_l[k], 16)
                            if kind == "gcn2":
                                sp.dma_start(lx[:, k, :, :], edges_of(T2[EDGE0:EDGE0 + NP, :])[:, j, :]).then_inc(s_l[k], 16)
                            if kind == "pna":
                                for p0, n in PARTS[0:2]:
                                    v = ef[p0 * T:(p0 + n) * T, :].rearrange("(p t) d -> p t d", t=T)
                                    sp.dma_start(lx[p0:p0 + n, k, :, :], v[:, j, :]).then_inc(s_l[k], 16)
                                sp.dma_start(lx[P - 1:P, k, :, :], ef_tail[j, :].rearrange("(o t) d -> o t d", o=1)).then_inc(s_l[k], 16)

                        def body(i):
                            for k in range(SLOTS):
                                load(i, k)
                                if has(i, k, 1):
                                    store_sums(i * SLOTS + k - 1, 0, 1 - k)
                                if has(i, k, lag + 1):
                                    store_rows(i * SLOTS + k - lag - 1, (k - lag - 1) % 2)
                        body(0)
                        body(1)
                        with sp.Fori(2, STEPS) as i:
                            body(i)
                        store_sums(NG - 1, 0, 1)
                        for g in range(NG - lag - 1, NG):
                            store_rows(g, g % 2)
                        sp.wait_ge(s_so[0], STEPS * 16)
                        sp.wait_ge(s_so[1], STEPS * 16)
                        sp.sem_inc(s_bs, 1)
                        sp.wait_ge(s_res, NG + 1)
                        for (d, w), r in zip(outs, res):
                            base = NP if d is T3r else BOUND0
                            sp.dma_start(d[base:base + P, :], r[:, 0, 0, :]).then_inc(s_ro[0], 16)
                        sp.wait_ge(s_ro[0], (STEPS + 1) * 16 * len(outs))
                        sp.wait_ge(s_ro[1], STEPS * 16 * len(outs))

                    @block.gpsimd
                    def _(pool):
                        def body(i):
                            for k in range(SLOTS):
                                g = i * SLOTS + k
                                pool.wait_ge(s_used, g + 1)
                                pool.sem_inc(s_turn, 1)
                                for q, (d, _) in enumerate(gathered):
                                    for t in range(G):
                                        pool.indirect_dma_start(out=gx[:, k, q, t, :], out_offset=None, in_=d, in_offset=bass.IndirectOffsetOnAxis(ap=idx[:, k, q, t:t + 1], axis=0)).then_inc(s_g[k], 16)
                        if gathered:
                            peeled(pool, STEPS, body)
                        pool.wait_ge(s_bs, 1)
                        pool.indirect_dma_start(out=sB[:, 0, :], out_offset=None, in_=S_d, in_offset=bass.IndirectOffsetOnAxis(ap=bidx[:, 0:1], axis=0)).then_inc(s_g[0], 16)
                        if kind == "att":
                            pool.indirect_dma_start(out=XB[:, 0, :], out_offset=None, in_=xd_lin, in_offset=bass.IndirectOffsetOnAxis(ap=bidx[:, 0:1], axis=0)).then_inc(s_g[0], 16)

                    @block.scalar
                    def _(act):
                        def work(g, n):
                            if kind == "gcn1":
                                mlp_act(act, M, n, S, g + 1)
                            if kind == "pna":
                                act.wait_ge(S["var"], g + 1)
                                nc.scalar.activation(hb[:, 0:n, :], hb[:, 0:n, :], ACT.Sqrt, bias=epst[:, 0:1], scale=1.0).then_inc(S["sd"], 1)
                            if kind in ("att", "gcn2"):
                                norm_act(act, B, n, S, g + 1)
                            if kind == "gcn2":
                                proj_act(act, J, n, S, g + 1)

                        def gat_u(g, k):
                            act.wait_ge(S["z"], g + 1)
                            nc.scalar.activation(uu[:, k, :, :], uu[:, k, :, :], ACT.Exp).then_inc(S["u"], 1)

                        def gat_f(g):
                            act.wait_ge(S["dm"], g + 1)
                            nc.scalar.activation(ff[:, :, :, :], dm[:, :, :, :], ACT.Exp).then_inc(S["f"], 1)

                        def body(i):
                            for k in range(SLOTS):
                                g = i * SLOTS + k
                                if kind == "gat":
                                    gat_u(g, k)
                                    if has(i, k, 1):
                                        gat_f(g - 1)
                                        norm_act(act, B, G, S, g)
                                elif has(i, k, 1):
                                    work(g - 1, G)
                        peeled(act, STEPS, body)
                        if kind == "gat":
                            gat_f(NG - 1)
                            norm_act(act, B, G, S, NG)
                            act.wait_ge(S["dm"], NG + 1)
                            nc.scalar.activation(fB[0:68, :, :], fB[0:68, :, :], ACT.Exp).then_inc(S["f"], 1)
                            act.wait_ge(S["dm"], NG + 2)
                            nc.scalar.activation(m68[:, 2:4, :], m68[:, 2:4, :], ACT.Exp).then_inc(S["f"], 1)
                            norm_act(act, B, 1, S, NG + 1)
                        else:
                            work(NG - 1, G)
                            work(NG, 1)

                    @block.tensor
                    def _(pe):
                        def work(g, n):
                            if kind == "gcn1":
                                mlp_pe(pe, M, n, S, g + 1)
                            if kind == "gcn2":
                                proj_pe(pe, J, xr, n, S, g + 1)
                            if kind == "pna":
                                pe.wait_ge(S["hq"], g + 1)
                                for t in range(n):
                                    last = nc.tensor.matmul(bnp[0:1, 0:2 * D], hb[:, t, 0:1], hq[:, t, :], start=False, stop=False)
                                last.then_inc(S["bn"], 1)

                        if kind == "pna":
                            pe.wait_ge(s_bp, 1)
                            nc.tensor.matmul(bnp[0:1, 0:2 * D], zc[:, :], ident[:, :], start=True, stop=False)
                        if kind in ("gcn1", "gcn2", "pna"):
                            def body(i):
                                for k in range(SLOTS):
                                    work(i * SLOTS + k, G)
                            peeled(pe, STEPS, body)
                        nq = 2 if kind in ("pna", "gat") else 1
                        w = {"pna": 2 * D, "gat": 68}.get(kind, D)
                        pe.wait_ge(s_bc, 1)
                        for q in range(nq):
                            srcv = m68[:, q, :] if kind == "gat" else acc[:, 2 * G - 1, q * w:(q + 1) * w]
                            last = nc.tensor.transpose(cps[0:w, q, 0:P], srcv, ident[:, :])
                        last.then_inc(s_bt, 1)
                        pe.wait_ge(s_bc, 2)
                        for q in range(nq):
                            last = nc.tensor.transpose(cps[:, q, 0:w], ct[0:w, q, :], ident[0:w, 0:w])
                        last.then_inc(s_bt, 1)
                        if kind in ("gcn1", "gcn2", "pna"):
                            work(NG, 1)
                        if kind == "pna":
                            nc.tensor.matmul(bnp[0:1, 0:2 * D], zc[:, :], ident[:, :], start=False, stop=True).then_inc(S["bn"], 1)

                    @block.vector
                    def _(dve):
                        V = nc.vector

                        def scans(k, v, lo, hi, is_max):
                            for t in range(G):
                                r = k * G + t
                                p = (r - 1) % (SLOTS * G)
                                last = V.scalar_tensor_tensor(acc[:, r, lo:hi], acc[:, p, lo:hi], md[:, k, t, NBIG:NBIG + 1] if is_max else md[:, k, t, CONT:CONT + 1],
                                                              v[:, t, lo:hi], ALU.add if is_max else ALU.mult, ALU.max if is_max else ALU.add)
                                if t < G - 1:
                                    dve.drain()
                            return last

                        def stage(g, k):
                            for q, (_, f) in enumerate(gathered):
                                V.tensor_copy(idx[:, k, q, :], meta_all[:, bass.ds(g * G, G), f])

                        def begin(i, k):
                            g = i * SLOTS + k
                            V.tensor_copy(md[:, k, :, :], meta[:, bass.ds(g * G, G), :])
                            dve.drain()
                            if gathered:
                                dve.wait_ge(s_g[k], i * per_gather + per_gather)
                                V.tensor_scalar(idx[:, k, 0, :], meta_all[:, bass.ds((g + SLOTS) * G, G), SROW], 1.0, None, ALU.mult)
                            if kind == "att":
                                dve.wait_ge(s_l[k], i * 16 + 16)
                                V.tensor_tensor(msg[:, :, :], lx[:, k, :, :], md[:, k, :, ALPHA:ALPHA + 1].broadcast_to([P, G, D]), ALU.mult).then_inc(s_used, 1)
                                dve.drain()
                            if kind == "pna":
                                dve.wait_ge(s_l[k], i * 48 + 48)
                                V.tensor_tensor(msg[:, :, 0:D], gx[:, k, 0, :, :], lx[:, k, :, :], ALU.add)
                                dve.drain()
                                dve.sem_inc(s_used, 1)
                                V.tensor_tensor(msg[:, :, D:2 * D], msg[:, :, 0:D], msg[:, :, 0:D], ALU.mult)
                                V.tensor_copy(msg[:, :, 2 * D:3 * D], msg[:, :, 0:D])
                                V.tensor_scalar(msg[:, :, 3 * D:4 * D], msg[:, :, 0:D], -1.0, None, ALU.mult)
                                dve.drain()
                            if has(i, k, 2):
                                dve.wait_ge(s_so[k], i * 16)
                            if kind == "att":
                                scans(k, msg, 0, D, False).then_inc(s_acc, 1)
                            if kind == "gcn1":
                                scans(k, gx[:, k, 0, :, :], 0, D, False).then_inc(s_acc, 1)
                                dve.drain()
                                dve.sem_inc(s_used, 1)
                            if kind == "gcn2":
                                scans(k, gx[:, k, 0, :, :], 0, D, False).then_inc(s_acc, 1)
                            if kind == "pna":
                                scans(k, msg, 0, 2 * D, False)
                                scans(k, msg, 2 * D, 4 * D, True).then_inc(s_acc, 1)
                            dve.drain()

                        def post(a, xv, m, lv, n, g):
                            if kind == "att":
                                V.scalar_tensor_tensor(B["y"][:, 0:n, :], a, 0.0, xv, ALU.max, ALU.add)
                                dve.drain()
                                norm_a(dve, B, n, S)
                            if kind == "gcn1":
                                dv = m[:, :, DINV:DINV + 1].broadcast_to([P, n, D])
                                V.tensor_tensor(msg[:, 0:n, :], xv, dv, ALU.mult)
                                dve.drain()
                                V.tensor_tensor(msg[:, 0:n, :], msg[:, 0:n, :], a, ALU.add)
                                dve.drain()
                                V.tensor_tensor(M["a"][:, 0:n, :], msg[:, 0:n, :], dv, ALU.mult).then_inc(S["ain"], 1)
                            if kind == "gcn2":
                                dv = m[:, :, DINV:DINV + 1].broadcast_to([P, n, D])
                                V.tensor_tensor(msg[:, 0:n, :], lv, a, ALU.add)
                                dve.drain()
                                if n == G:
                                    dve.sem_inc(s_used, 1)
                                V.tensor_tensor(msg[:, 0:n, :], msg[:, 0:n, :], dv, ALU.mult)
                                dve.drain()
                                V.tensor_tensor(msg[:, 0:n, :], msg[:, 0:n, :], xv, ALU.add)
                                dve.drain()
                                V.tensor_tensor(B["y"][:, 0:n, :], msg[:, 0:n, :], b2b[:, :].unsqueeze(1).broadcast_to([P, n, D]), ALU.add)
                                dve.drain()
                                norm_a(dve, B, n, S)
                            if kind == "gat":
                                av = a[:, :, 0:68].rearrange("p n (h e) -> p n h e", e=17)
                                V.reciprocal(lg[:, 0:n, :], av[:, :, :, 16])
                                dve.drain()
                                for t in range(n):
                                    V.tensor_tensor(t1[:, t, :].rearrange("p (h e) -> p h e", h=H), av[:, t, :, 0:16], lg[:, t, :].unsqueeze(2).broadcast_to([P, H, HD]), ALU.mult)
                                dve.drain()
                                V.tensor_tensor(B["y"][:, 0:n, :], t1[:, 0:n, :], xv, ALU.add)
                                dve.drain()
                                norm_a(dve, B, n, S)
                            if kind == "pna":
                                rc = m[:, :, RCNT:RCNT + 1].broadcast_to([P, n, D])
                                V.tensor_tensor(mm[:, 0:n, :], a[:, :, 0:D], rc, ALU.mult)
                                V.tensor_tensor(hb[:, 0:n, :], a[:, :, D:2 * D], rc, ALU.mult)
                                dve.drain()
                                V.tensor_tensor(msg[:, 0:n, 0:D], mm[:, 0:n, :], mm[:, 0:n, :], ALU.mult)
                                dve.drain()
                                V.tensor_tensor(hb[:, 0:n, :], hb[:, 0:n, :], msg[:, 0:n, 0:D], ALU.subtract)
                                V.tensor_tensor(mm[:, 0:n, :], mm[:, 0:n, :], a[:, :, 2 * D:3 * D], ALU.add)
                                dve.drain()
                                V.tensor_scalar(hb[:, 0:n, :], hb[:, 0:n, :], 0.0, None, ALU.max).then_inc(S["var"], 1)
                                V.tensor_tensor(mm[:, 0:n, :], mm[:, 0:n, :], a[:, :, 3 * D:4 * D], ALU.subtract)
                                dve.drain()
                                V.scalar_tensor_tensor(mm[:, 0:n, :], xv, 3.0, mm[:, 0:n, :], ALU.mult, ALU.add)

                        def finish(xv, m, k, n, g, last=False):
                            if kind == "att":
                                norm_b(dve, B, n, S, g + 1, xv)
                                dve.drain()
                                V.tensor_tensor(res[0][:, k, 0:n, :], xv, m[:, :, DINV:DINV + 1].broadcast_to([P, n, D]), ALU.mult).then_inc(s_res, 1)
                            if kind == "gcn1":
                                dve.wait_ge(S["o"], g + 1)
                                V.tensor_tensor(res[0][:, k, 0:n, :], M["op"][:, 0:n * D].rearrange("p (t d) -> p t d", d=D), m[:, :, DINV:DINV + 1].broadcast_to([P, n, D]), ALU.mult).then_inc(s_res, 1)
                            if kind == "gcn2":
                                norm_b(dve, B, n, S, g + 1, xr[:, 0:n, :])
                                dve.drain()
                                V.tensor_scalar(xv, xr[:, 0:n, :], 1.0, None, ALU.mult).then_inc(S["pin"], 1)
                            if kind == "gat":
                                norm_b(dve, B, n, S, g + 1, xv)
                                dve.drain()
                                V.tensor_scalar(res[0][:, k, 0:n, :], xv, 1.0, None, ALU.mult).then_inc(s_res, 1)
                            if kind == "pna":
                                r = res[0][:, k, 0:n, :]
                                V.tensor_scalar(r[:, :, 0:D], xv, 1.0, None, ALU.mult)
                                dve.drain()
                                dve.wait_ge(S["sd"], g + 1)
                                V.tensor_tensor(mm[:, 0:n, :], mm[:, 0:n, :], hb[:, 0:n, :], ALU.add)
                                dve.drain()
                                V.tensor_tensor(mm[:, 0:n, :], mm[:, 0:n, :], m[:, :, AMP:AMP + 1].broadcast_to([P, n, D]), ALU.mult)
                                V.tensor_copy(hb[:, 0:n, 0:1], m[:, :, MEND:MEND + 1])
                                dve.drain()
                                V.tensor_tensor(mm[:, 0:n, :], mm[:, 0:n, :], r[:, :, 0:D], ALU.add)
                                dve.drain()
                                V.tensor_scalar(r[:, :, D:2 * D], mm[:, 0:n, :], 1.0 / 13, None, ALU.mult).then_inc(s_res, 1)
                                dve.drain()
                                V.tensor_copy(hq[:, 0:n, 0:D], r[:, :, D:2 * D])
                                V.tensor_tensor(hq[:, 0:n, D:2 * D], r[:, :, D:2 * D], r[:, :, D:2 * D], ALU.mult).then_inc(S["hq"], 1)
                                dve.drain()
                                dve.wait_ge(S["bn"], g + 1)
                            if kind != "pna":
                                dve.drain()

                        def project(k, n, g):
                            dve.wait_ge(S["pj"], g + 1)
                            v = J["pj"][:, 0:n * 2 * D].rearrange("p (t d) -> p t d", d=2 * D)
                            V.tensor_copy(res[0][:, k, 0:n, :], v[:, :, 0:D])
                            V.tensor_copy(res[1][:, k, 0:n, :], v[:, :, D:2 * D]).then_inc(s_res, 1)
                            dve.drain()

                        def gat_front(i, k):
                            g = i * SLOTS + k
                            V.tensor_copy(md[:, k, :, :], meta[:, bass.ds(g * G, G), :])
                            dve.wait_ge(s_g[k], i * per_gather + per_gather)
                            V.tensor_tensor(zz[:, k, :, :], gx[:, k, 0, :, :], gx[:, k, 1, :, :], ALU.add)
                            stage(g + SLOTS, k)
                            dve.drain()
                            V.tensor_scalar(uu[:, k, :, :], zz[:, k, :, :], 20.0, None, ALU.min).then_inc(S["z"], 1)

                        def gat_back(g, k):
                            u, z = uu[:, k, :, :], zz[:, k, :, :]
                            dve.drain()
                            dve.wait_ge(S["u"], g + 1)
                            V.scalar_tensor_tensor(t1[:, :, :], u, 2.0, u, ALU.add, ALU.mult)
                            dve.drain()
                            V.tensor_scalar(t2[:, :, :], t1[:, :, :], 2.0, None, ALU.add)
                            V.tensor_tensor(t1[:, :, :], t1[:, :, :], z, ALU.mult)
                            dve.drain()
                            V.reciprocal(t2[:, :, :], t2[:, :, :])
                            dve.drain()
                            V.tensor_tensor(t1[:, :, :], t1[:, :, :], t2[:, :, :], ALU.mult)
                            dve.drain()
                            V.tensor_tensor(t1[:, :, :], t1[:, :, :], awb[:, :].unsqueeze(1).broadcast_to([P, G, D]), ALU.mult)
                            dve.drain()
                            V.tensor_reduce(lg[:, :, :], t1[:, :, :].rearrange("p t (h e) -> p t h e", h=H), AX.X, ALU.add)
                            dve.drain()
                            V.tensor_scalar(lg[:, :, :], lg[:, :, :], abb[:, 0:1], None, ALU.add)
                            dve.drain()
                            for t in range(G):
                                r = k * G + t
                                p = (r - 1) % (SLOTS * G)
                                V.scalar_tensor_tensor(mx[:, r, :], mx[:, p, :], md[:, k, t, NBIG:NBIG + 1], lg[:, t, :], ALU.add, ALU.max)
                                dve.drain()
                            V.tensor_tensor(dm[:, 0, 1:G, :], mx[:, k * G:(k + 1) * G - 1, :], mx[:, k * G + 1:(k + 1) * G, :], ALU.subtract)
                            p = (k * G - 1) % (SLOTS * G)
                            V.tensor_tensor(dm[:, 0, 0, :], mx[:, p, :], mx[:, k * G, :], ALU.subtract)
                            V.tensor_tensor(dm[:, 1, :, :], lg[:, :, :], mx[:, k * G:(k + 1) * G, :], ALU.subtract)
                            dve.drain()
                            V.tensor_scalar(dm[:, :, :, :], dm[:, :, :, :], 0.0, None, ALU.min).then_inc(S["dm"], 1)

                        def gat_sum(g, i, k):
                            dve.drain()
                            if i is not None:
                                dve.wait_ge(s_so[k], i)
                            dve.wait_ge(S["f"], g + 1)
                            V.tensor_tensor(ff[:, 0, :, :], ff[:, 0, :, :], md[:, k, :, CONT:CONT + 1].broadcast_to([P, G, H]), ALU.mult)
                            mv = msg[:, :, 0:68].rearrange("p t (h e) -> p t h e", e=17)
                            for h in range(H):
                                V.tensor_tensor(mv[:, :, h, 0:16], gx[:, k, 0, :, h * HD:(h + 1) * HD], ff[:, 1, :, h:h + 1].broadcast_to([P, G, HD]), ALU.mult)
                            V.tensor_copy(mv[:, :, :, 16], ff[:, 1, :, :])
                            dve.drain()
                            dve.sem_inc(s_used, 1)
                            for t in range(G):
                                r = k * G + t
                                p = (r - 1) % (SLOTS * G)
                                V.tensor_tensor(acc[:, r, 0:68].rearrange("p (h e) -> p h e", e=17), acc[:, p, 0:68].rearrange("p (h e) -> p h e", e=17),
                                                ff[:, 0, t, :].unsqueeze(2).broadcast_to([P, H, 17]), ALU.mult)
                                dve.drain()
                                V.tensor_tensor(acc[:, r, 0:68], acc[:, r, 0:68], msg[:, t, 0:68], ALU.add)
                                dve.drain()
                            V.tensor_copy(acc[:, k * G:(k + 1) * G, 68:72], mx[:, k * G:(k + 1) * G, :]).then_inc(s_acc, 1)
                            dve.drain()

                        V.memset(acc[:, :, :], 0.0)
                        if kind == "gcn2":
                            V.memset(J["xT"][D:D + 1, :], 1.0)
                        if kind == "pna":
                            dve.drain()
                            V.memset(acc[:, :, 2 * D:4 * D], -BIG)
                            V.memset(zc[:, :], 0.0).then_inc(s_bp, 1)
                        if kind == "gat":
                            V.memset(mx[:, :, :], -BIG)
                            V.memset(m68[:, :, :], 0.0)
                        if gathered:
                            for k in range(SLOTS):
                                stage(k, k)
                            dve.drain()
                            dve.sem_inc(s_used, SLOTS)
                        if kind == "att":
                            dve.wait_ge(s_xl, 16)
                        dve.drain()

                        def stage_b(g, i, k, waits=True):
                            j = bass.ds(g * G, G)
                            xv = X[:, j, :]
                            if kind == "gcn2":
                                dve.wait_ge(s_l[k], i)
                            post(acc[:, k * G:(k + 1) * G, :], xv, md[:, k, :, :], lx[:, k, :, :] if lx else None, G, g)

                        def res_free(k, n):
                            if n is not None:
                                dve.wait_ge(s_ro[k], n)

                        def body(i):
                            for k in range(SLOTS):
                                g = i * SLOTS + k
                                o = 1 - k
                                no = 16 * len(outs)
                                if kind == "gat":
                                    gat_front(i, k)
                                    if has(i, k, 1):
                                        gat_back(g - 1, o)
                                    if has(i, k, 2):
                                        dve.drain()
                                        res_free(k, (i - 1) * no if has(i, k, 4) else None)
                                        finish(X[:, bass.ds((g - 2) * G, G), :], md[:, k, :, :], k, G, g - 2)
                                    if has(i, k, 1):
                                        w = i + k - 1
                                        gat_sum(g - 1, (w * 16 if has(i, k, 3) else None), o)
                                        stage_b(g - 1, None, o)
                                    continue
                                begin(i, k)
                                if lag == 2 and has(i, k, 2):
                                    res_free(k, (i - 1) * no if has(i, k, 4) else None)
                                    project(k, G, g - 2)
                                if has(i, k, 1):
                                    if lag == 1:
                                        w = i + k - 1
                                        res_free(o, w * no if has(i, k, 3) else None)
                                    finish(X[:, bass.ds((g - 1) * G, G), :], md[:, o, :, :], o, G, g - 1)
                                stage_b(g, i * 16 + 16, k)
                        body(0)
                        body(1)
                        with dve.Fori(2, STEPS) as i:
                            body(i)
                        no = 16 * len(outs)
                        if kind == "gat":
                            gat_back(NG - 1, 1)
                            dve.drain()
                            res_free(0, (STEPS - 1) * no)
                            finish(X[:, (NG - 2) * G:(NG - 1) * G, :], md[:, 0, :, :], 0, G, NG - 2)
                            gat_sum(NG - 1, (STEPS - 1) * 16, 1)
                            stage_b(NG - 1, None, 1)
                            dve.drain()
                            res_free(1, (STEPS - 1) * no)
                            finish(X[:, (NG - 1) * G:NG * G, :], md[:, 1, :, :], 1, G, NG - 1)
                        else:
                            if lag == 2:
                                res_free(0, (STEPS - 1) * no)
                                project(0, G, NG - 2)
                            if lag == 1:
                                res_free(1, (STEPS - 1) * no)
                            finish(X[:, (NG - 1) * G:NG * G, :], md[:, 1, :, :], 1, G, NG - 1)
                            if lag == 2:
                                res_free(1, (STEPS - 1) * no)
                                project(1, G, NG - 1)
                        dve.drain()

                        w = {"pna": 2 * D, "gat": 68}.get(kind, D)
                        final = 2 * G - 1
                        if kind == "gat":
                            V.tensor_copy(m68[:, 1, :], acc[:, final, 0:68])
                            V.tensor_copy(m68[:, 0, :].rearrange("p (h e) -> p h e", e=17), mx[:, final, :].unsqueeze(2).broadcast_to([P, H, 17]))
                            dve.drain()
                        dve.sem_inc(s_bc, 1)
                        dve.wait_ge(s_bt, 1)
                        if kind == "gat":
                            V.memset(cr[0:68, 0, :], -BIG)
                            V.memset(cr[0:68, 1, :], 0.0)
                            dve.drain()
                            V.tensor_tensor(cr[0:68, 0, 1:P], carryFx[0:68, 1, 1:P], cps[0:68, 0, 0:P - 1], ALU.add)
                            dve.drain()
                            V.tensor_tensor_scan(ct[0:68, 0, :], carryFx[0:68, 0, :], cr[0:68, 0, :], initial=-BIG, op0=ALU.add, op1=ALU.max)
                            V.memset(fB[0:68, :, :], 0.0)
                            dve.drain()
                            V.tensor_tensor(fB[0:68, 0, 1:P], ct[0:68, 0, 0:P - 1], ct[0:68, 0, 1:P], ALU.subtract)
                            V.tensor_tensor(fB[0:68, 1, 1:P], cps[0:68, 0, 0:P - 1], ct[0:68, 0, 1:P], ALU.subtract)
                            dve.drain()
                            V.tensor_scalar(fB[0:68, :, :], fB[0:68, :, :], 0.0, None, ALU.min).then_inc(S["dm"], 1)
                            dve.wait_ge(S["f"], NG + 1)
                            V.tensor_tensor(fB[0:68, 0, :], fB[0:68, 0, :], carryF[0:68, 0, :], ALU.mult)
                            V.tensor_tensor(fB[0:68, 1, :], fB[0:68, 1, :], carryF[0:68, 1, :], ALU.mult)
                            dve.drain()
                            V.tensor_tensor(cr[0:68, 1, 1:P], fB[0:68, 1, 1:P], cps[0:68, 1, 0:P - 1], ALU.mult)
                            dve.drain()
                            V.tensor_tensor_scan(ct[0:68, 1, :], fB[0:68, 0, :], cr[0:68, 1, :], initial=0.0, op0=ALU.mult, op1=ALU.add)
                        else:
                            for q in range(W // w):
                                mxq = q == 1
                                cf = carryFx if mxq else carryF
                                V.memset(cr[0:w, q, :], -BIG if mxq else 0.0)
                                dve.drain()
                                V.tensor_tensor(cr[0:w, q, 1:P], cf[0:w, 1, 1:P], cps[0:w, q, 0:P - 1], ALU.add if mxq else ALU.mult)
                                dve.drain()
                                V.tensor_tensor_scan(ct[0:w, q, :], cf[0:w, 0, :], cr[0:w, q, :], initial=-BIG if mxq else 0.0,
                                                     op0=ALU.add if mxq else ALU.mult, op1=ALU.max if mxq else ALU.add)
                        dve.drain()
                        dve.sem_inc(s_bc, 1)
                        dve.wait_ge(s_bt, 2)
                        dve.wait_ge(s_g[0], STEPS * per_gather + (32 if kind == "att" else 16))
                        if kind == "gat":
                            V.tensor_copy(m68[:, 0, :], cps[:, 0, 0:68])
                            V.tensor_copy(m68[:, 1, :].rearrange("p (h e) -> p h e", e=17), sB[:, 0, 68:72].unsqueeze(2).broadcast_to([P, H, 17]))
                            dve.drain()
                            V.tensor_tensor(msg[:, 0, 0:68], m68[:, 0, :], m68[:, 1, :], ALU.max)
                            dve.drain()
                            V.tensor_tensor(m68[:, 2, :], m68[:, 0, :], msg[:, 0, 0:68], ALU.subtract)
                            V.tensor_tensor(m68[:, 3, :], m68[:, 1, :], msg[:, 0, 0:68], ALU.subtract).then_inc(S["dm"], 1)
                            dve.wait_ge(S["f"], NG + 2)
                            V.tensor_tensor(m68[:, 2, :], m68[:, 2, :], cps[:, 1, 0:68], ALU.mult)
                            V.tensor_tensor(m68[:, 3, :], m68[:, 3, :], sB[:, 0, 0:68], ALU.mult)
                            dve.drain()
                            V.tensor_tensor(sB[:, 0, 0:68], m68[:, 2, :], m68[:, 3, :], ALU.add)
                        else:
                            V.tensor_tensor(sB[:, 0, 0:w], sB[:, 0, 0:w], cps[:, 0, 0:w], ALU.add)
                            if kind == "pna":
                                V.tensor_tensor(sB[:, 0, w:2 * w], sB[:, 0, w:2 * w], cps[:, 1, 0:w], ALU.max)
                        dve.drain()
                        if kind == "gcn2":
                            V.tensor_copy(lx[:, 0, 0, :], own2[:, 0, :])
                            dve.drain()
                        post(sB[:, :, :], XB[:, :, :], metaB[:, :, :], lx[:, 0, 0:1, :] if kind == "gcn2" else None, 1, NG)
                        dve.drain()
                        res_free(0, STEPS * no)
                        finish(XB[:, :, :], metaB[:, :, :], 0, 1, NG)
                        if lag == 2 and kind == "gcn2":
                            project(0, 1, NG)
                        if kind == "gcn1":
                            dve.drain()
                            V.tensor_copy(own2[:, 0, :], res[0][:, 0, 0, :])
                        if kind == "pna":
                            dve.wait_ge(S["bn"], NG + 2)
                            V.tensor_copy(bn[0:1, 1, :], bnp[0:1, 0:2 * D])

            with nc.Block() as block:
                @block.sync
                def _(sp):
                    for role in roles.values():
                        sp.sem_clear(role)

        for kind in ('att', 'gcn1', 'gcn2', 'gat', 'pna'):
            edge_phase(kind)
        with ExitStack() as c1:
            S = {k: sem(f"s_{k}_fin") for k in ("var", "sd")}
            s_used = sem("s_used_fin"); s_bst = sem("s_bst"); s_bpe = sem("s_bpe"); s_res = sem("s_res_fin")
            s_g = [sem(f"s_g{k}_fin") for k in range(SLOTS)]
            s_ro = [sem(f"s_ro{k}_fin") for k in range(SLOTS)]
            s_gb = sem("s_gb")
            B = buffers(c1)
            idx = sb("idx", [P, SLOTS, G], I32, c1)
            gx = sb("gx", [P, SLOTS, G, 2 * D], F32, c1)
            res = sb("res", [P, SLOTS, G, D], F32, c1)
            row = sb("row", [1, 4, D], F32, c1)
            gb = sb("gb", [1, 2 * D], F32, c1)
            st = sb("st", [1, 2 * D], F32, c1)
            bc = sb("bc", [P, 2 * D], F32, c1)
            bps = ps("bps", [P, 512], c1)
            with nc.Block() as block:
                @block.sync
                def _(sp):
                    sp.dma_start(gb[0:1, 0:D], gamma.rearrange("(o f) -> o f", o=1)).then_inc(s_gb, 16)
                    sp.dma_start(gb[0:1, D:2 * D], beta.rearrange("(o f) -> o f", o=1)).then_inc(s_gb, 16)

                    def store(g, k, tail):
                        sp.wait_ge(s_res, g + 1)
                        sp.sem_inc(s_spturn, 1)
                        for p0, n in PARTS[0:2]:
                            v = out[p0 * T:(p0 + n) * T, :].rearrange("(p t) d -> p t d", t=T)
                            sp.dma_start(v[:, bass.ds(g * G, G), :], res[p0:p0 + n, k, :, :]).then_inc(s_ro[k], 16)
                        if tail:
                            v = out[(P - 1) * T:N, :].rearrange("(o t) d -> o t d", o=1)
                            sp.dma_start(v[:, bass.ds(g * G, tail), :], res[P - 1:P, k, 0:tail, :]).then_inc(s_ro[k], 16)
                        else:
                            sp.sem_inc(s_ro[k], 16)
                    whole = TAIL // (G * SLOTS)
                    with sp.Fori(0, whole) as i:
                        for k in range(SLOTS):
                            store(i * SLOTS + k, k, G)
                    for k in range(SLOTS):
                        g = whole * SLOTS + k
                        store(g, k, max(0, min(G, TAIL - g * G)))
                    with sp.Fori(whole + 1, STEPS) as i:
                        for k in range(SLOTS):
                            store(i * SLOTS + k, k, 0)
                    for k in range(SLOTS):
                        sp.wait_ge(s_ro[k], STEPS * 48)

                @block.gpsimd
                def _(pool):
                    def body(i):
                        for k in range(SLOTS):
                            g = i * SLOTS + k
                            pool.wait_ge(s_used, g + 1)
                            pool.sem_inc(s_turn, 1)
                            for t in range(G):
                                pool.indirect_dma_start(out=gx[:, k, t, :], out_offset=None, in_=T5, in_offset=bass.IndirectOffsetOnAxis(ap=idx[:, k, t:t + 1], axis=0)).then_inc(s_g[k], 16)
                    peeled(pool, STEPS, body)

                @block.scalar
                def _(act):
                    def body(i):
                        for k in range(SLOTS):
                            g = i * SLOTS + k
                            if isinstance(i, int) and k == 1:
                                act.wait_ge(s_bst, 1)
                                nc.scalar.activation(row[0:1, 1, :], row[0:1, 1, :], ACT.Sqrt, bias=epst[0:1, 0:1], scale=1.0).then_inc(s_bst, 1)
                            if k or not isinstance(i, int):
                                norm_act(act, B, G, S, g)
                    peeled(act, STEPS, body)
                    norm_act(act, B, G, S, NG)

                @block.tensor
                def _(pe):
                    pe.wait_ge(s_bst, 3)
                    nc.tensor.matmul(bps[:, 0:2 * D], ones[0:1, :], st[0:1, :], start=True, stop=True).then_inc(s_bpe, 1)

                @block.vector
                def _(dve):
                    V = nc.vector
                    for k in range(SLOTS):
                        V.tensor_copy(idx[:, k, :], rowtab[:, k * G:(k + 1) * G])
                    dve.drain()
                    dve.sem_inc(s_used, SLOTS)
                    V.tensor_tensor(bn[0:1, 2, :], bn[0:1, 0, :], bn[0:1, 1, :], ALU.add)
                    dve.drain()
                    V.tensor_scalar(bn[0:1, 2, :], bn[0:1, 2, :], 1.0 / N, None, ALU.mult)
                    dve.drain()
                    V.tensor_tensor(row[0:1, 0, :], bn[0:1, 2, 0:D], bn[0:1, 2, 0:D], ALU.mult)
                    dve.drain()
                    V.tensor_tensor(row[0:1, 1, :], bn[0:1, 2, D:2 * D], row[0:1, 0, :], ALU.subtract)
                    dve.drain()
                    V.tensor_scalar(row[0:1, 1, :], row[0:1, 1, :], 0.0, None, ALU.max).then_inc(s_bst, 1)
                    dve.wait_ge(s_bst, 2)
                    V.reciprocal(row[0:1, 2, :], row[0:1, 1, :])
                    dve.drain()
                    dve.wait_ge(s_gb, 32)
                    V.tensor_tensor(st[0:1, 0:D], row[0:1, 2, :], gb[0:1, 0:D], ALU.mult)
                    dve.drain()
                    V.tensor_tensor(row[0:1, 3, :], bn[0:1, 2, 0:D], st[0:1, 0:D], ALU.mult)
                    dve.drain()
                    V.tensor_tensor(st[0:1, D:2 * D], gb[0:1, D:2 * D], row[0:1, 3, :], ALU.subtract).then_inc(s_bst, 1)
                    dve.wait_ge(s_bpe, 1)
                    V.tensor_copy(bc[:, :], bps[:, 0:2 * D])
                    dve.drain()

                    def finish(g, k, n):
                        if n is not None:
                            dve.wait_ge(s_ro[k], n)
                        norm_b(dve, B, G, S, g + 1, res[:, k, :, :])
                        dve.drain()
                        dve.sem_inc(s_res, 1)

                    def body(i):
                        for k in range(SLOTS):
                            g = i * SLOTS + k
                            if not isinstance(i, int) or i * SLOTS + k >= 1:
                                finish(g - 1, 1 - k, (i + k - 1) * 48 if not isinstance(i, int) or i * SLOTS + k >= 3 else None)
                            dve.wait_ge(s_g[k], i * G * 16 + G * 16)
                            V.tensor_tensor(B["y"][:, :, :], gx[:, k, :, D:2 * D], bc[:, 0:D].unsqueeze(1).broadcast_to([P, G, D]), ALU.mult)
                            dve.drain()
                            V.tensor_tensor(B["y"][:, :, :], B["y"][:, :, :], bc[:, D:2 * D].unsqueeze(1).broadcast_to([P, G, D]), ALU.add)
                            dve.drain()
                            V.tensor_tensor(B["y"][:, :, :], B["y"][:, :, :], gx[:, k, :, 0:D], ALU.add)
                            V.tensor_copy(idx[:, k, :], rowtab_all[:, bass.ds((g + SLOTS) * G, G)])
                            dve.drain()
                            dve.sem_inc(s_used, 1)
                            norm_a(dve, B, G, S)
                    body(0)
                    body(1)
                    with dve.Fori(2, STEPS) as i:
                        body(i)
                    finish(NG - 1, 1, (STEPS - 1) * 48)


_INS = ["x", "src", "dst", "edge_attr_64", "edge_weight", "L1_gnn_W1", "L1_gnn_b1", "L1_gnn_W2", "L1_gnn_b2",
        "L2_gnn_Ws", "L2_gnn_bs", "L2_gnn_Wr", "L2_gnn_br", "L2_gnn_aw", "L2_gnn_ab", "L3_gnn_gamma", "L3_gnn_beta"]


def kernel(**inputs):
    import numpy as _np
    import concourse.bacc as _bacc
    from concourse import mybir as _mybir
    from concourse.bass_utils import run_bass_kernel_spmd as _run

    nc = _bacc.Bacc("TRN2", target_bir_lowering=False, num_devices=1)
    arrays, args = {}, []
    for name in _INS:
        a = _np.ascontiguousarray(inputs[name])
        arrays[f"in_{name}_dram"] = a
        args.append(nc.dram_tensor(f"in_{name}_dram", a.shape, _mybir.dt.from_np(a.dtype), kind="ExternalInput").ap())
    out = nc.dram_tensor("out_0_dram", (N, D), _mybir.dt.float32, kind="ExternalOutput").ap()
    build(nc, *args, out)
    r = _run(nc, [arrays], core_ids=[0])
    return r.results[0]["out_0_dram"]
```

```python
import concourse.bass as bass
from concourse import mybir
from contextlib import ExitStack

ALU = mybir.AluOpType
ACT = mybir.ActivationFunctionType
AX = mybir.AxisListType
F32 = mybir.dt.float32
I32 = mybir.dt.int32

P = 128
N = 50000
E = 50000
D = 64
H = 4
HD = D // H
F1 = 128
G = 7
T = 392
NG = T // G
SLOTS = 2
STEPS = NG // SLOTS
NP = P * T
EDGE0 = NP
BOUND0 = 2 * NP
NR = 2 * NP + P
TAIL = E - (P - 1) * T
PADKEY = NP - 1
BIG = 1e30
EPS = 1e-5
LO, HI, SHIFT = 2.0 ** -40, 2.0 ** 40, 2.0 ** 42

CONT, NBIG, MEND, DINV, ALPHA, CNT, SROW, DROW, SIDX, DIDX, RCNT, AMP = range(12)
NM = 12
AVG_D = 2.833213344056216


def edges_of(a):
    return a.rearrange("(p t) w -> p t w", p=P)


def peeled(eng, n, body):
    body(0)
    with eng.Fori(1, n) as i:
        body(i)


def build(nc, x, src, dst, ef, ew, W1, b1, W2, b2, Ws, bs, Wr, br, aw, ab, gamma, beta, out):
    ctx = ExitStack()
    with ctx:
        taken = {}

        def fresh(name):
            taken[name] = taken.get(name, 0) + 1
            return name if taken[name] == 1 else f"{name}_{taken[name]}"

        def sb(name, shape, dt=F32, c=ctx):
            return c.enter_context(nc.sbuf_tensor(fresh(name), shape, dt))

        def ps(name, shape, c):
            return c.enter_context(nc.psum_tensor(fresh(name), shape, F32))

        def sem(name):
            return ctx.enter_context(nc.semaphore(name))

        def dram(name, shape):
            return nc.dram_tensor(name, shape, F32, kind="Internal").ap()

        srcT_d, encT_d = dram("srcT_d", (T, P)), dram("encT_d", (T, P))
        xs_lin, xd_lin = dram("xs_lin", (NP, D)), dram("xd_lin", (NP, D))
        tab_m, tab_s, tab_sr = dram("tab_m", (NP, 1)), dram("tab_s", (NP, 1)), dram("tab_sr", (NP, 2))

        meta_all = sb("meta", [P, T + SLOTS * G, NM])
        meta = meta_all[:, 0:T, :]
        ident = sb("ident", [P, P])
        ones = sb("ones", [P, P])
        iota_p = sb("iota_p", [P, P])
        iota_j = sb("iota_j", [P, T])
        nidx = sb("nidx", [P, T])
        rowtab_all = sb("rowtab", [P, T + SLOTS * G])
        rowtab = rowtab_all[:, 0:T]
        iso = sb("iso", [P, T])
        carryF = sb("carryF", [P, 2, P])
        carryB = sb("carryB", [P, 2, P])
        carryFx = sb("carryFx", [P, 2, P])
        bidx = sb("bidx", [P, 1], I32)
        metaB = sb("metaB", [P, 1, NM])
        epst = sb("epst", [P, 1])
        w1s = sb("w1s", [D, F1]); w2s = sb("w2s", [F1, D]); wsr = sb("wsr", [D + 1, 2 * D])
        b1c = sb("b1c", [F1, 1]); b2b = sb("b2b", [P, D]); awb = sb("awb", [P, D]); abb = sb("abb", [P, 1])
        own2 = sb("own2", [P, 1, D])
        bn = sb("bn", [1, 4, 2 * D])
        s_load = sem("s_load")
        s_const = sem("s_const")
        s_pad = sem("s_pad")
        s_masks = sem("s_masks")
        s_ends = sem("s_ends"); s_rows = sem("s_rows"); s_scanned = sem("s_scanned"); s_cols = sem("s_cols")
        s_act = sem("s_act"); s_dve = sem("s_dve"); s_tr = sem("s_tr"); s_trc = sem("s_trc"); s_st = sem("s_st")
        ctxS = ExitStack()
        skey = sb("skey", [P, T, 4], F32, ctxS)
        dkey = sb("dkey", [P, T, 3], F32, ctxS)
        wt = sb("wt", [P, T], F32, ctxS)
        vi = sb("vi", [P, T], F32, ctxS)
        lower = sb("lower", [P, P], F32, ctxS)
        with ExitStack() as c1:
            a_ps = ps("a_ps", [P, 4, P], c1)
            r_ps = ps("r_ps", [1, 4, P], c1)
            c_ps = ps("c_ps", [P, 512], c1)
            t_ps = ps("t_ps", [P, 4, 512], c1)
            srcI = sb("srcI", [P, T], I32, c1)
            dstI = sb("dstI", [P, T], I32, c1)
            dstF = sb("dstF", [P, T], F32, c1)
            nbr = sb("nbr", [P, 2], I32, c1)
            nbrF = sb("nbrF", [P, 2], F32, c1)
            qI = sb("qI", [P, T], I32, c1)
            qF = sb("qF", [P, T], F32, c1)
            rF = sb("rF", [P, T], F32, c1)
            fx = sb("fx", [P, T], F32, c1)
            eidx = nidx
            pidx = sb("pidx", [P, 1], F32, c1)
            contb = sb("contb", [P, T], F32, c1)
            nbigb = sb("nbigb", [P, T], F32, c1)
            first = sb("first", [P, T], F32, c1)
            last = sb("last", [P, T], F32, c1)
            bend = sb("bend", [P, T], F32, c1)
            isend = sb("isend", [P, T], F32, c1)
            cc = sb("cc", [P, 4], F32, c1)
            dg = sb("dg", [P, 3, P], F32, c1)
            rowA = sb("rowA", [P, 3, P], F32, c1)
            carryBx = sb("carryBx", [P, 2, P], F32, c1)
            Fs = sb("Fs", [P, T], F32, c1)
            Bs = sb("Bs", [P, T], F32, c1)
            ur = sb("ur", [1, 2, P], F32, c1)
            ct = sb("ct", [1, 2, P], F32, c1)
            cb = sb("cb", [P, 2], F32, c1)
            wm = sb("wm", [P, T], F32, c1)
            ex = sb("ex", [P, T], F32, c1)
            on = sb("on", [P, T], F32, c1)
            tmp = sb("tmp", [P, T], F32, c1)
            tmp2 = sb("tmp2", [P, T], F32, c1)
            tout = sb("tout", [P, 8, P], F32, c1)

            with nc.Block() as block:
                @block.sync
                def _(sp):
                    sp.wait_ge(s_pad, 1)
                    for t, a in ((srcI, src), (dstI, dst)):
                        v = a.rearrange("(n w) -> n w", w=1)
                        sp.dma_start(t[0:P - 1, :], a[0:(P - 1) * T].rearrange("(p t) -> p t", t=T)).then_inc(s_load, 16)
                        sp.dma_start(t[P - 1:P, 0:TAIL], a[(P - 1) * T:E].rearrange("(p t) -> p t", p=1)).then_inc(s_load, 16)
                    sp.dma_start(wt[0:P - 1, :], ew[0:(P - 1) * T].rearrange("(p t) -> p t", t=T)).then_inc(s_load, 16)
                    sp.dma_start(wt[P - 1:P, 0:TAIL], ew[(P - 1) * T:E].rearrange("(p t) -> p t", p=1)).then_inc(s_load, 16)
                    per = dst[0:(P - 1) * T].rearrange("(p t) -> p t", t=T)
                    nxt = dst[0:(P - 1) * T].rearrange("(p t) -> p t", t=T)
                    sp.dma_start(nbr[1:P, 0:1], per[:, T - 1:T], allow_slow_non_contiguous=True).then_inc(s_load, 16)
                    sp.dma_start(nbr[0:P - 2, 1:2], nxt[1:P - 1, 0:1], allow_slow_non_contiguous=True).then_inc(s_load, 16)
                    sp.dma_start(nbr[P - 2:P - 1, 1:2], dst[(P - 1) * T:(P - 1) * T + 1].rearrange("(p t) -> p t", t=1), allow_slow_non_contiguous=True).then_inc(s_load, 16)
                    for k, d in enumerate((srcT_d, encT_d)):
                        for c in range(4):
                            rows = min(P, T - c * P)
                            sp.wait_ge(s_trc, k * 4 + c + 1)
                            sp.dma_start(d[c * P:c * P + rows, :], tout[0:rows, k * 4 + c, :]).then_inc(s_st, 16)
                    sp.wait_ge(s_st, 8 * 16)

                @block.gpsimd
                def _(pool):
                    pool.iota(iota_p[:, :], [[1, P]], base=0, channel_multiplier=0, allow_small_or_imprecise_dtypes=True)
                    pool.iota(iota_j[:, :], [[1, T]], base=0, channel_multiplier=0, allow_small_or_imprecise_dtypes=True)
                    pool.iota(eidx[:, :], [[1, T]], base=0, channel_multiplier=T, allow_small_or_imprecise_dtypes=True)
                    pool.iota(pidx[:, :], [[1, 1]], base=0, channel_multiplier=1, allow_small_or_imprecise_dtypes=True).then_inc(s_const, 1)

                @block.tensor
                def _(pe):
                    pe.wait_ge(s_masks, 1)
                    for k in range(3):
                        nc.tensor.matmul(a_ps[:, k, :], ones[:, :], dg[:, k, :], start=True, stop=True).then_inc(s_rows, 1)
                    for k in range(4):
                        pe.wait_ge(s_ends, k + 1)
                        nc.tensor.transpose(r_ps[0:1, 0, :], Fs[:, T - 1:T], ident[:, :])
                        nc.tensor.transpose(r_ps[0:1, 1, :], Bs[:, 0:1], ident[:, :]).then_inc(s_rows, 1)
                        pe.wait_ge(s_scanned, k + 1)
                        nc.tensor.transpose(c_ps[:, 0:1], ct[0:1, 0, :], ident[0:1, 0:1])
                        nc.tensor.transpose(c_ps[:, 1:2], ct[0:1, 1, :], ident[0:1, 0:1]).then_inc(s_cols, 1)
                    pe.wait_ge(s_tr, 1)
                    for k, f in enumerate((0, 3)):
                        for c in range(4):
                            rows = min(P, T - c * P)
                            n = k * 4 + c
                            if n >= 4:
                                pe.wait_ge(s_trc, n - 3)
                            nc.tensor.transpose(t_ps[0:rows, n % 4, 0:P], skey[:, c * P:c * P + rows, f], ident[:, :]).then_inc(s_dve, 1)

                @block.scalar
                def _(act):
                    act.wait_ge(s_act, 1)
                    nc.scalar.activation(ex[:, :], tmp[:, :], ACT.Exp).then_inc(s_act, 1)
                    act.wait_ge(s_act, 3)
                    nc.scalar.activation(tmp2[:, :], meta[:, :, CNT], ACT.Sqrt, bias=ones[:, 0:1], scale=1.0).then_inc(s_act, 1)
                    act.wait_ge(s_act, 5)
                    nc.scalar.activation(tmp2[:, :], tmp2[:, :], ACT.Ln).then_inc(s_act, 1)
                    for n in range(8):
                        rows = min(P, T - (n % 4) * P)
                        act.wait_ge(s_dve, n + 1)
                        nc.scalar.copy(tout[0:rows, n, :], t_ps[0:rows, n % 4, 0:P]).then_inc(s_trc, 1)

                @block.vector
                def _(dve):
                    V = nc.vector
                    V.memset(srcI[:, :], PADKEY)
                    V.memset(dstI[:, :], PADKEY)
                    V.memset(nbr[:, :], -1)
                    V.memset(ones[:, :], 1.0)
                    V.memset(on[:, :], 1.0)
                    V.memset(wt[:, :], 0.0)
                    V.memset(meta_all[:, :, :], 0.0)
                    V.memset(metaB[:, :, :], 0.0)
                    V.memset(epst[:, :], EPS)
                    V.memset(rowtab_all[:, :], 0.0)
                    dve.drain()
                    V.memset(cc[:, :], 0.0).then_inc(s_pad, 1)
                    dve.wait_ge(s_const, 1)
                    V.tensor_scalar(ident[:, :], iota_p[:, :], pidx[:, 0:1], None, ALU.is_equal)
                    V.tensor_scalar(lower[:, :], iota_p[:, :], pidx[:, 0:1], None, ALU.is_lt)
                    dve.wait_ge(s_load, 9 * 16)
                    V.tensor_copy(skey[:, :, 0], srcI[:, :])
                    V.tensor_copy(nbrF[:, :], nbr[:, :])
                    V.tensor_copy(dstF[:, :], dstI[:, :])
                    dve.drain()
                    for key, kp, kj in ((skey[:, :, 0], skey[:, :, 1], skey[:, :, 2]), (dstF[:, :], dkey[:, :, 0], dkey[:, :, 1])):
                        V.tensor_scalar(qI[:, :], key, 1.0 / T, None, ALU.mult)
                        dve.drain()
                        V.tensor_copy(qF[:, :], qI[:, :])
                        dve.drain()
                        V.scalar_tensor_tensor(rF[:, :], qF[:, :], -float(T), key, ALU.mult, ALU.add)
                        dve.drain()
                        V.tensor_scalar(fx[:, :], rF[:, :], 0.0, None, ALU.is_lt)
                        dve.drain()
                        V.tensor_tensor(qF[:, :], qF[:, :], fx[:, :], ALU.subtract)
                        V.scalar_tensor_tensor(rF[:, :], fx[:, :], float(T), rF[:, :], ALU.mult, ALU.add)
                        dve.drain()
                        V.tensor_scalar(fx[:, :], rF[:, :], float(T), None, ALU.is_ge)
                        dve.drain()
                        V.tensor_tensor(kp, qF[:, :], fx[:, :], ALU.add)
                        V.scalar_tensor_tensor(kj, fx[:, :], -float(T), rF[:, :], ALU.mult, ALU.add)
                        dve.drain()
                    V.tensor_scalar(meta[:, :, SIDX], skey[:, :, 0], float(N - 1), None, ALU.min)
                    V.tensor_scalar(meta[:, :, DIDX], dstF[:, :], float(N - 1), None, ALU.min)
                    V.tensor_tensor(meta[:, 1:T, CONT], dstF[:, 1:T], dstF[:, 0:T - 1], ALU.is_equal)
                    V.memset(contb[:, :], 0.0)
                    V.tensor_tensor(cc[:, 0:1], dstF[:, 0:1], nbrF[:, 0:1], ALU.is_equal)
                    V.tensor_tensor(cc[:, 1:2], dstF[:, T - 1:T], nbrF[:, 1:2], ALU.is_equal)
                    V.tensor_tensor(cc[:, 2:3], dstF[:, 0:1], dstF[:, T - 1:T], ALU.is_equal)
                    V.tensor_scalar(first[:, :], dstF[:, :], dstF[:, 0:1], None, ALU.is_equal)
                    V.tensor_scalar(last[:, :], dstF[:, :], dstF[:, T - 1:T], None, ALU.is_equal)
                    dve.drain()
                    V.tensor_copy(contb[:, 0:T - 1], meta[:, 1:T, CONT])
                    V.tensor_scalar(isend[:, 0:T - 1], meta[:, 1:T, CONT], -1.0, 1.0, ALU.mult, ALU.add)
                    V.tensor_scalar(isend[:, T - 1:T], cc[:, 1:2], -1.0, 1.0, ALU.mult, ALU.add)
                    V.tensor_scalar(meta[:, :, NBIG], meta[:, :, CONT], BIG, -BIG, ALU.mult, ALU.add)
                    for k in range(3):
                        V.tensor_scalar(dg[:, k, :], ident[:, :], cc[:, k:k + 1], None, ALU.mult)
                    dve.drain()
                    V.tensor_scalar(nbigb[:, :], contb[:, :], BIG, -BIG, ALU.mult, ALU.add).then_inc(s_masks, 1)
                    V.scalar_tensor_tensor(bend[:, :], isend[:, :], cc[:, 0:1], first[:, :], ALU.mult, ALU.mult)
                    dve.drain()
                    V.tensor_tensor(meta[:, :, MEND], isend[:, :], bend[:, :], ALU.subtract)
                    V.tensor_tensor(tmp[:, :], bend[:, :], eidx[:, :], ALU.mult)
                    dve.drain()
                    V.tensor_reduce(cb[:, 0:1], tmp[:, :], AX.X, ALU.add)
                    V.scalar_tensor_tensor(tmp2[:, :], eidx[:, :], float(EDGE0), meta[:, :, MEND], ALU.add, ALU.mult)
                    V.tensor_scalar(cc[:, 3:4], pidx[:, 0:1], float(BOUND0), None, ALU.add)
                    dve.drain()
                    V.tensor_copy(bidx[:, :], cb[:, 0:1])
                    V.scalar_tensor_tensor(dkey[:, :, 2], bend[:, :], cc[:, 3:4], tmp2[:, :], ALU.mult, ALU.add)
                    dve.wait_ge(s_rows, 3)
                    V.tensor_copy(rowA[:, :, :], a_ps[:, 0:3, :])
                    V.memset(carryF[:, :, :], 0.0)
                    V.memset(carryB[:, :, :], 0.0)
                    dve.drain()
                    V.tensor_copy(carryF[:, 1, 1:P], rowA[:, 0, 1:P])
                    V.tensor_tensor(carryF[:, 0, 1:P], rowA[:, 0, 1:P], rowA[:, 2, 0:P - 1], ALU.mult)
                    V.tensor_copy(carryB[:, 1, 0:P - 1], rowA[:, 1, 0:P - 1])
                    V.tensor_tensor(carryB[:, 0, 0:P - 1], rowA[:, 1, 0:P - 1], rowA[:, 2, 1:P], ALU.mult)
                    dve.drain()
                    V.tensor_scalar(carryFx[:, :, :], carryF[:, :, :], BIG, -BIG, ALU.mult, ALU.add)
                    V.tensor_scalar(carryBx[:, :, :], carryB[:, :, :], BIG, -BIG, ALU.mult, ALU.add)
                    dve.drain()

                    def total(k, val, res, is_max):
                        o0, o1 = (ALU.add, ALU.max) if is_max else (ALU.mult, ALU.add)
                        a = meta[:, :, NBIG] if is_max else meta[:, :, CONT]
                        b = nbigb if is_max else contb
                        cf, cbk = (carryFx, carryBx) if is_max else (carryF, carryB)
                        init = -BIG if is_max else 0.0
                        V.tensor_tensor_scan(Fs[:, :], a, val, initial=init, op0=o0, op1=o1)
                        V.tensor_tensor_scan(Bs[:, :][:, ::-1], b[:, :][:, ::-1], val[:, ::-1], initial=init, op0=o0, op1=o1).then_inc(s_ends, 1)
                        dve.wait_ge(s_ends, k + 1)
                        V.memset(ur[:, :, :], init)
                        dve.wait_ge(s_rows, 3 + k + 1)
                        dve.drain()
                        m = ALU.add if is_max else ALU.mult
                        V.tensor_tensor(ur[0:1, 0, 1:P], cf[0:1, 1, 1:P], r_ps[0:1, 0, 0:P - 1], m)
                        V.tensor_tensor(ur[0:1, 1, 0:P - 1], cbk[0:1, 1, 0:P - 1], r_ps[0:1, 1, 1:P], m)
                        dve.drain()
                        V.tensor_tensor_scan(ct[0:1, 0, :], cf[0:1, 0, :], ur[0:1, 0, :], initial=init, op0=o0, op1=o1)
                        V.tensor_tensor_scan(ct[0:1, 1, :][:, ::-1], cbk[0:1, 0, :][:, ::-1], ur[0:1, 1, :][:, ::-1], initial=init, op0=o0, op1=o1).then_inc(s_scanned, 1)
                        dve.wait_ge(s_cols, k + 1)
                        if is_max:
                            V.tensor_scalar(tmp[:, :], first[:, :], BIG, -BIG, ALU.mult, ALU.add)
                            V.tensor_scalar(tmp2[:, :], last[:, :], BIG, -BIG, ALU.mult, ALU.add)
                            V.tensor_tensor(res, Fs[:, :], Bs[:, :], ALU.max)
                            V.tensor_copy(cb[:, :], c_ps[:, 0:2])
                            dve.drain()
                            V.scalar_tensor_tensor(res, tmp[:, :], cb[:, 0:1], res, ALU.add, ALU.max)
                            dve.drain()
                            V.scalar_tensor_tensor(res, tmp2[:, :], cb[:, 1:2], res, ALU.add, ALU.max)
                        else:
                            V.tensor_tensor(res, Fs[:, :], Bs[:, :], ALU.add)
                            V.tensor_copy(cb[:, :], c_ps[:, 0:2])
                            dve.drain()
                            V.tensor_tensor(res, res, val, ALU.subtract)
                            dve.drain()
                            V.scalar_tensor_tensor(res, first[:, :], cb[:, 0:1], res, ALU.mult, ALU.add)
                            dve.drain()
                            V.scalar_tensor_tensor(res, last[:, :], cb[:, 1:2], res, ALU.mult, ALU.add)
                        dve.drain()

                    total(0, wt[:, :], wm[:, :], True)
                    V.tensor_tensor(tmp[:, :], wt[:, :], wm[:, :], ALU.subtract).then_inc(s_act, 1)
                    dve.drain()
                    V.tensor_scalar(wm[:, :], wt[:, :], -1.0, None, ALU.mult)
                    dve.drain()
                    V.tensor_tensor(wm[:, :], wm[:, :], wt[:, :], ALU.max)
                    V.tensor_scalar(fx[:, :], wt[:, :], 0.0, None, ALU.is_ge)
                    dve.drain()
                    V.tensor_scalar(wm[:, :], wm[:, :], LO, HI, ALU.max, ALU.min)
                    dve.drain()
                    V.tensor_scalar(qF[:, :], wm[:, :], SHIFT, None, ALU.mult)
                    V.tensor_scalar(tmp2[:, :].bitcast(I32), wm[:, :].bitcast(I32), 0x7FFFFFFF, None, ALU.bitwise_xor)
                    dve.drain()
                    V.tensor_scalar(rF[:, :], tmp2[:, :], 1.0 / SHIFT, None, ALU.mult)
                    dve.drain()
                    V.copy_predicated(rF[:, :], fx[:, :].bitcast(I32), qF[:, :])
                    dve.drain()
                    V.tensor_copy(skey[:, :, 3], rF[:, :]).then_inc(s_tr, 1)
                    dve.wait_ge(s_act, 2)
                    total(1, ex[:, :], wm[:, :], False)
                    V.tensor_scalar(wm[:, :], wm[:, :], 1e-16, None, ALU.add)
                    dve.drain()
                    V.reciprocal(wm[:, :], wm[:, :])
                    dve.drain()
                    V.tensor_tensor(vi[:, :], ex[:, :], wm[:, :], ALU.mult)
                    total(2, on[:, :], meta[:, :, CNT], False)
                    V.tensor_copy(cb[:, 0:1], cb[:, 1:2])
                    dve.drain()
                    V.memset(cc[:, 3:4], 0.0).then_inc(s_act, 1)
                    dve.wait_ge(s_act, 4)
                    V.reciprocal(meta[:, :, DINV], tmp2[:, :])
                    V.tensor_copy(tmp[:, :], dkey[:, :, 2])
                    dve.drain()
                    total(3, tmp[:, :], meta[:, :, DROW], False)
                    V.scalar_tensor_tensor(meta[:, :, MEND], dstF[:, :], float(N), meta[:, :, MEND], ALU.is_lt, ALU.mult)
                    V.tensor_scalar(meta[:, :, DROW], meta[:, :, DROW], -float(EDGE0), None, ALU.add)
                    V.reciprocal(meta[:, :, RCNT], meta[:, :, CNT])
                    V.tensor_scalar(tmp2[:, :], meta[:, :, CNT], 1.0, None, ALU.add).then_inc(s_act, 1)
                    dve.wait_ge(s_act, 6)
                    V.reciprocal(fx[:, :], tmp2[:, :])
                    V.tensor_scalar(tmp2[:, :], tmp2[:, :], 1.0 / AVG_D, 1.0, ALU.mult, ALU.add)
                    dve.drain()
                    V.scalar_tensor_tensor(meta[:, :, AMP], fx[:, :], AVG_D, tmp2[:, :], ALU.mult, ALU.add)
                    dve.drain()
                    for f in (DINV, RCNT, AMP):
                        V.tensor_tensor(tmp[:, :], meta[:, :, f], bend[:, :], ALU.mult)
                        dve.drain()
                        V.tensor_reduce(metaB[:, :, f], tmp[:, :].unsqueeze(1), AX.X, ALU.add)
                        dve.drain()
                    V.tensor_reduce(metaB[:, :, MEND], bend[:, :].unsqueeze(1), AX.X, ALU.add)
        tbl = sb("tbl", [P, T], F32, ctxS)
        sr = sb("sr", [P, T, 2], F32, ctxS)
        s_idx = sem("s_idx"); s_row = [sem(f"s_row{k}") for k in range(SLOTS)]
        s_gx = [sem(f"s_gx{k}") for k in range(SLOTS)]; s_sx = [sem(f"s_sx{k}") for k in range(SLOTS)]
        s_hot = sem("s_hot"); s_mm = sem("s_mm"); s_rmw = sem("s_rmw"); s_eq = sem("s_eq"); s_turn = sem("s_turn")
        s_tab = sem("s_tab")
        with ExitStack() as c1:
            pt = ps("pt", [P, G, 512], c1)
            srow = sb("srow", [P, SLOTS, G, P], F32, c1)
            erow = sb("erow", [P, SLOTS, G, P], F32, c1)
            xi = sb("xi", [P, SLOTS, 2, G], I32, c1)
            xg = sb("xg", [P, SLOTS, 2, G, D], F32, c1)
            ks = sb("ks", [P, SLOTS, G, 4], F32, c1)
            eq = sb("eq", [P, G, P], F32, c1)
            ev = sb("ev", [P, G, P], F32, c1)
            vt = sb("vt", [P, G], F32, c1)
            lt = sb("lt", [P, G], F32, c1)
            hp = sb("hp", [P, SLOTS, G, P], F32, c1)
            hj = sb("hj", [P, SLOTS, G, T], F32, c1)
            dec = sb("dec", [P, T], F32, c1)
            dec2 = sb("dec2", [P, T], F32, c1)
            with nc.Block() as block:
                @block.sync
                def _(sp):
                    def body(i):
                        for k in range(SLOTS):
                            g = i * SLOTS + k
                            if not isinstance(i, int):
                                sp.wait_ge(s_eq, (i - 1) * SLOTS + k + 1)
                            for d, t in ((srcT_d, srow), (encT_d, erow)):
                                sp.dma_start(t[:, k, :, :], d[bass.ds(g * G, G), :].rearrange("(o a) b -> o a b", o=1).broadcast_to([P, G, P])).then_inc(s_row[k], 16)
                    peeled(sp, STEPS, body)
                    sp.wait_ge(s_tab, 1)
                    sp.dma_start(tab_m.rearrange("(p t) w -> p (t w)", p=P), dec[:, :]).then_inc(s_st, 16)
                    sp.wait_ge(s_st, 9 * 16)

                @block.gpsimd
                def _(pool):
                    def body(i):
                        for k in range(SLOTS):
                            pool.wait_ge(s_idx, i * SLOTS + k + 1)
                            pool.sem_inc(s_turn, 1)
                            if not isinstance(i, int):
                                pool.wait_ge(s_sx[k], i * 32)
                                pool.sem_inc(s_turn, 1)
                            for q in range(2):
                                for t in range(G):
                                    pool.indirect_dma_start(out=xg[:, k, q, t, :], out_offset=None, in_=x, in_offset=bass.IndirectOffsetOnAxis(ap=xi[:, k, q, t:t + 1], axis=0)).then_inc(s_gx[k], 16)
                    peeled(pool, STEPS, body)

                @block.scalar
                def _(act):
                    def store(i, k):
                        for q, d in enumerate((xs_lin, xd_lin)):
                            act.dma_start(edges_of(d)[:, bass.ds((i * SLOTS + k) * G, G), :], xg[:, k, q, :, :]).then_inc(s_sx[k], 16)

                    def body(i):
                        for k in range(SLOTS):
                            j = (i * SLOTS + k) * G
                            if not isinstance(i, int):
                                act.wait_ge(s_gx[k], i * 2 * G * 16)
                                store(i - 1, k)
                            nc.scalar.copy(xi[:, k, 0, :], meta[:, bass.ds(j, G), SIDX])
                            nc.scalar.copy(xi[:, k, 1, :], meta[:, bass.ds(j, G), DIDX]).then_inc(s_idx, 1)
                    peeled(act, STEPS, body)
                    for k in range(SLOTS):
                        act.wait_ge(s_gx[k], STEPS * 2 * G * 16)
                        store(STEPS - 1, k)
                    for k in range(SLOTS):
                        act.wait_ge(s_sx[k], STEPS * 32)

                @block.tensor
                def _(pe):
                    def body(i):
                        for k in range(SLOTS):
                            pe.wait_ge(s_hot, i * SLOTS + k + 1)
                            if k or not isinstance(i, int):
                                pe.wait_ge(s_rmw, i * SLOTS + k)
                            for t in range(G):
                                last = nc.tensor.matmul(pt[:, t, 0:T], hp[:, k, t, :], hj[:, k, t, :], start=True, stop=True)
                            last.then_inc(s_mm, 1)
                    peeled(pe, STEPS, body)

                @block.vector
                def _(dve):
                    V = nc.vector

                    def take(g):
                        dve.wait_ge(s_mm, g + 1)
                        for t in range(G):
                            last = V.tensor_tensor(tbl[:, :], tbl[:, :], pt[:, t, 0:T], ALU.max)
                            if t < G - 1:
                                dve.drain()
                        last.then_inc(s_rmw, 1)

                    def body(i):
                        for k in range(SLOTS):
                            g = i * SLOTS + k
                            V.tensor_copy(ks[:, k, :, :], skey[:, bass.ds(g * G, G), :])
                            dve.drain()
                            dve.wait_ge(s_row[k], i * 32 + 32)
                            V.tensor_tensor(eq[:, :, :], srow[:, k, :, :], ks[:, k, :, 0:1].broadcast_to([P, G, P]), ALU.is_equal)
                            dve.drain()
                            V.tensor_tensor(ev[:, :, :], eq[:, :, :], erow[:, k, :, :], ALU.mult).then_inc(s_eq, 1)
                            dve.drain()
                            V.tensor_reduce(vt[:, :], ev[:, :, :], AX.X, ALU.max)
                            dve.drain()
                            V.tensor_tensor(ev[:, :, :], eq[:, :, :], lower[:, :].unsqueeze(1).broadcast_to([P, G, P]), ALU.mult)
                            dve.drain()
                            V.tensor_reduce(lt[:, :], ev[:, :, :], AX.X, ALU.add)
                            dve.drain()
                            V.scalar_tensor_tensor(vt[:, :], lt[:, :], 0.0, vt[:, :], ALU.is_equal, ALU.mult)
                            dve.drain()
                            if not isinstance(i, int):
                                dve.wait_ge(s_mm, g - 1)
                            for t in range(G):
                                V.tensor_scalar(hp[:, k, t, :], iota_p[:, :], ks[:, k, t, 1:2], vt[:, t:t + 1], ALU.is_equal, ALU.mult)
                                last = V.tensor_scalar(hj[:, k, t, :], iota_j[:, :], ks[:, k, t, 2:3], None, ALU.is_equal)
                            last.then_inc(s_hot, 1)
                            if k or not isinstance(i, int):
                                take(g - 1)
                    V.memset(tbl[:, :], LO / SHIFT / 2)
                    dve.drain()
                    peeled(dve, STEPS, body)
                    take(NG - 1)
                    dve.drain()
                    V.tensor_scalar(dec2[:, :], tbl[:, :], SHIFT, None, ALU.mult)
                    dve.drain()
                    V.tensor_scalar(dec2[:, :].bitcast(I32), dec2[:, :].bitcast(I32), 0x7FFFFFFF, None, ALU.bitwise_xor)
                    dve.drain()
                    V.tensor_scalar(dec[:, :], dec2[:, :], -1.0, None, ALU.mult)
                    dve.drain()
                    V.tensor_scalar(dec2[:, :], tbl[:, :], 1.0 / SHIFT, None, ALU.mult)
                    V.tensor_scalar(sr[:, :, 0], tbl[:, :], 1.0, None, ALU.is_ge)
                    dve.drain()
                    V.tensor_copy(iso[:, :], sr[:, :, 0])
                    dve.drain()
                    V.copy_predicated(dec[:, :], iso[:, :].bitcast(I32), dec2[:, :]).then_inc(s_tab, 1)

        exj = sb("exj", [P, T], F32, ctxS)
        s_gs = [[sem(f"s_gs{n}_{k}") for k in range(SLOTS)] for n in range(3)]
        s_si = [sem(f"s_si{n}") for n in range(3)]
        s_dif = [sem(f"s_dif{n}") for n in range(2)]; s_exp = [sem(f"s_exp{n}") for n in range(2)]
        s_fh = [sem(f"s_fh{n}") for n in range(2)]; s_fm = [sem(f"s_fm{n}") for n in range(2)]
        s_use = sem("s_use")
        for n in range(2):
            with ExitStack() as c1:
                table = (tab_m, tab_s)[n]
                pa = ps("pa", [P, 2, 512], c1)
                gi = sb("gi", [P, SLOTS, G], I32, c1)
                gv = sb("gv", [P, SLOTS, G, 1], F32, c1)
                dif = sb("dif", [P, SLOTS, G], F32, c1)
                zero = sb("zero", [P, P], F32, c1)
                hp = sb("hp", [P, SLOTS, 2, G, P], F32, c1)
                hj = sb("hj", [P, SLOTS, 2, G, T], F32, c1)
                ks = sb("ks", [P, SLOTS, G, 4], F32, c1)
                kd = sb("kd", [P, SLOTS, G, 3], F32, c1)
                nk = 2 if n == 0 else 1
                with nc.Block() as block:
                    @block.sync
                    def _(sp):
                        if n == 0:
                            sp.wait_ge(s_tab, 2)
                            sp.dma_start(tab_s.rearrange("(p t) w -> p (t w)", p=P), tbl[:, :]).then_inc(s_st, 16)
                            sp.wait_ge(s_st, 10 * 16)
                        if n == 1:
                            sp.wait_ge(s_tab, 3)
                            sp.dma_start(tab_sr.rearrange("(p t) w -> p (t w)", p=P), sr[:, :, :].rearrange("p t w -> p (t w)")).then_inc(s_st, 16)
                            sp.wait_ge(s_st, 11 * 16)

                    @block.gpsimd
                    def _(pool):
                        def body(i):
                            for k in range(SLOTS):
                                pool.wait_ge(s_si[n], i * SLOTS + k + 1)
                                pool.sem_inc(s_turn, 1)
                                for t in range(G):
                                    pool.indirect_dma_start(out=gv[:, k, t, :], out_offset=None, in_=table, in_offset=bass.IndirectOffsetOnAxis(ap=gi[:, k, t:t + 1], axis=0)).then_inc(s_gs[n][k], 16)
                        peeled(pool, STEPS, body)

                    @block.scalar
                    def _(act):
                        def exps(g, k):
                            act.wait_ge(s_dif[n], g + 1)
                            nc.scalar.activation(exj[:, bass.ds(g * G, G)], dif[:, k, :], ACT.Exp).then_inc(s_exp[n], 1)

                        def body(i):
                            for k in range(SLOTS):
                                g = i * SLOTS + k
                                if not isinstance(i, int):
                                    act.wait_ge(s_gs[n][k], i * G * 16)
                                    exps(g - SLOTS, k)
                                nc.scalar.copy(gi[:, k, :], skey[:, bass.ds(g * G, G), 0]).then_inc(s_si[n], 1)
                        peeled(act, STEPS, body)
                        for k in range(SLOTS):
                            g = NG - SLOTS + k
                            act.wait_ge(s_gs[n][k], STEPS * G * 16)
                            exps(g, k)

                    @block.tensor
                    def _(pe):
                        pe.wait_ge(s_fh[n], 1)
                        for q in range(nk):
                            nc.tensor.matmul(pa[:, q, 0:T], zero[:, :], iota_j[:, :], start=True, stop=False)

                        def body(i):
                            for k in range(SLOTS):
                                pe.wait_ge(s_fh[n], i * SLOTS + k + 2)
                                for q in range(nk):
                                    for t in range(G):
                                        last = nc.tensor.matmul(pa[:, q, 0:T], hp[:, k, q, t, :], hj[:, k, q, t, :], start=False, stop=False)
                                last.then_inc(s_fm[n], 1)
                        peeled(pe, STEPS, body)
                        for q in range(nk):
                            last = nc.tensor.matmul(pa[:, q, 0:T], zero[:, :], iota_j[:, :], start=False, stop=True)
                        last.then_inc(s_fm[n], 1)

                    @block.vector
                    def _(dve):
                        V = nc.vector
                        V.memset(zero[:, :], 0.0).then_inc(s_fh[n], 1)

                        def body(i):
                            for k in range(SLOTS):
                                g = i * SLOTS + k
                                j = bass.ds(g * G, G)
                                V.tensor_copy(ks[:, k, :, :], skey[:, j, :])
                                if n == 0:
                                    V.tensor_copy(kd[:, k, :, :], dkey[:, j, :])
                                dve.wait_ge(s_gs[n][k], i * G * 16 + G * 16)
                                if n == 0:
                                    V.tensor_tensor(dif[:, k, :], wt[:, j], gv[:, k, :, 0], ALU.subtract).then_inc(s_dif[n], 1)
                                else:
                                    V.tensor_scalar(dif[:, k, :], gv[:, k, :, 0], 1e-16, None, ALU.add)
                                    dve.drain()
                                    V.reciprocal(dif[:, k, :], dif[:, k, :])
                                    dve.drain()
                                    V.tensor_tensor(dif[:, k, :], dif[:, k, :], exj[:, j], ALU.mult)
                                    dve.drain()
                                    V.tensor_tensor(dif[:, k, :], dif[:, k, :], vi[:, j], ALU.add).then_inc(s_dif[n], 1)
                                dve.drain()
                                if not isinstance(i, int):
                                    dve.wait_ge(s_fm[n], g - 1)
                                for t in range(G):
                                    last = V.tensor_scalar(hj[:, k, 0, t, :], iota_j[:, :], ks[:, k, t, 2:3], None, ALU.is_equal)
                                    if n == 0:
                                        V.tensor_scalar(hp[:, k, 1, t, :], iota_p[:, :], kd[:, k, t, 0:1], kd[:, k, t, 2:3], ALU.is_equal, ALU.mult)
                                        V.tensor_scalar(hj[:, k, 1, t, :], iota_j[:, :], kd[:, k, t, 1:2], None, ALU.is_equal)
                                dve.wait_ge(s_exp[n], g + 1)
                                V.tensor_scalar(ks[:, k, :, 3], exj[:, j], 1.0, None, ALU.mult)
                                dve.drain()
                                for t in range(G):
                                    last = V.tensor_scalar(hp[:, k, 0, t, :], iota_p[:, :], ks[:, k, t, 1:2], ks[:, k, t, 3:4], ALU.is_equal, ALU.mult)
                                last.then_inc(s_fh[n], 1)
                        peeled(dve, STEPS, body)
                        dve.wait_ge(s_fm[n], NG + 1)
                        if n == 0:
                            V.tensor_copy(tbl[:, :], pa[:, 0, 0:T]).then_inc(s_tab, 1)
                            V.tensor_scalar(iso[:, :], pa[:, 1, 0:T], 0.0, None, ALU.is_equal)
                            dve.drain()
                            V.scalar_tensor_tensor(rowtab[:, :], nidx[:, :], 1.0, iso[:, :], ALU.mult, ALU.mult)
                            dve.drain()
                            V.tensor_tensor(rowtab[:, :], rowtab[:, :], pa[:, 1, 0:T], ALU.add)
                            V.scalar_tensor_tensor(iso[:, :], nidx[:, :], float(N), iso[:, :], ALU.is_lt, ALU.mult)
                        else:
                            V.tensor_copy(sr[:, :, 0], pa[:, 0, 0:T])
                            V.tensor_copy(sr[:, :, 1], rowtab[:, :])
                            dve.drain()
                            V.memset(zero[:, :], 0.0).then_inc(s_tab, 1)
        T1, T2, T3s, T4 = (dram(f"rows{k}", (NR, D)) for k in range(4))
        T3r = dram("rows_r", (NP + P, D))
        T5 = dram("rows5", (NR, 2 * D))
        S_lin = {w: dram(f"sums{w}", (NP, w)) for w in (D, 72, 4 * D)}
        ef_tail = dram("ef_tail", (T, D))
        PARTS = ((0, 112), (112, 15), (127, 1))

        s_w = sem("s_w")
        s_peturn = sem("s_peturn"); s_spturn = sem("s_spturn")

        def row_stage(tag):
            names = ("ain", "tp", "tc", "hp", "hc", "o", "pin", "ptp", "ptc", "pj", "var", "sd")
            return {k: sem(f"s_{k}_{tag}") for k in names}

        def buffers(c, n=G):
            return dict(
                y=sb("y", [P, n, D], F32, c), sq=sb("sq", [P, n, D], F32, c), mu=sb("mu", [P, n], F32, c),
                va=sb("va", [P, n], F32, c), sd=sb("sd", [P, n], F32, c), rs=sb("rs", [P, n], F32, c))

        def norm_a(dve, B, n, S):
            V = nc.vector
            y = B["y"][:, 0:n, :]
            V.tensor_reduce(B["mu"][:, 0:n], y, AX.X, ALU.add)
            dve.drain()
            V.scalar_tensor_tensor(y, B["mu"][:, 0:n].unsqueeze(2).broadcast_to([P, n, D]), -1.0 / D, y, ALU.mult, ALU.add).then_inc(S["cen"], 1)

        def norm_squares(act, B, n, S, count):
            act.wait_ge(S["cen"], count)
            nc.scalar.activation(B["sq"][:, 0:n, :], B["y"][:, 0:n, :], ACT.Square).then_inc(S["sq"], 1)

        def norm_sum(dve, B, n, S, count):
            dve.wait_ge(S["sq"], count)
            nc.vector.tensor_reduce(B["va"][:, 0:n], B["sq"][:, 0:n, :], AX.X, ALU.add).then_inc(S["var"], 1)

        def norm_act(act, B, n, S, count):
            act.wait_ge(S["var"], count)
            nc.scalar.activation(B["sd"][:, 0:n], B["va"][:, 0:n], ACT.Sqrt, bias=epst[:, 0:1], scale=1.0 / D).then_inc(S["sd"], 1)

        def norm_b(dve, B, n, S, count, res):
            V = nc.vector
            dve.wait_ge(S["sd"], count)
            V.reciprocal(B["rs"][:, 0:n], B["sd"][:, 0:n])
            dve.drain()
            return V.tensor_tensor(res, B["y"][:, 0:n, :], B["rs"][:, 0:n].unsqueeze(2).broadcast_to([P, n, D]), ALU.mult)

        def mlp_pe(pe, M, n, S, count, s_read):
            pe.wait_ge(S["ain"], count)
            pe.sem_inc(s_peturn, 1)
            for t in range(n):
                last = nc.tensor.transpose(M["aTp"][0:D, t * P:(t + 1) * P], M["a"][:, t, :], ident[:, :])
            last.then_inc(S["tp"], 1)
            pe.wait_ge(S["tc"], count)
            for c0 in range(0, n * P, 512):
                c1_ = min(n * P, c0 + 512)
                last = nc.tensor.matmul(M["hTp"][:, c0:c1_], w1s[:, :], M["aT"][0:D, c0:c1_], start=True, stop=True)
            last.then_inc(S["hp"], 1)
            pe.wait_ge(S["hc"], count)
            wait_used(pe, s_read, count - 1)
            for t in range(n):
                last = nc.tensor.matmul(M["op"][:, t * D:(t + 1) * D], M["hT"][:, t * P:(t + 1) * P], w2s[:, :], start=True, stop=True)
            last.then_inc(S["o"], 1)

        def mlp_act(act, M, n, S, count):
            act.wait_ge(S["tp"], count)
            nc.scalar.activation(M["aT"][0:D, 0:n * P], M["aTp"][0:D, 0:n * P], ACT.Copy).then_inc(S["tc"], 1)
            act.wait_ge(S["hp"], count)
            nc.scalar.activation(M["hT"][:, 0:n * P], M["hTp"][:, 0:n * P], ACT.Relu, bias=b1c[:, 0:1], scale=1.0).then_inc(S["hc"], 1)

        def proj_pe(pe, M, rows, n, S, count):
            pe.wait_ge(S["pin"], count)
            pe.sem_inc(s_peturn, 1)
            for t in range(n):
                last = nc.tensor.transpose(M["xTp"][0:D, t * P:(t + 1) * P], rows[:, t, :], ident[:, :])
            last.then_inc(S["ptp"], 1)
            pe.wait_ge(S["ptc"], count)
            for t in range(n):
                last = nc.tensor.matmul(M["pj"][:, t * 2 * D:(t + 1) * 2 * D], M["xT"][:, t * P:(t + 1) * P], wsr[:, :], start=True, stop=True)
            last.then_inc(S["pj"], 1)

        def proj_act(act, M, n, S, count):
            act.wait_ge(S["ptp"], count)
            nc.scalar.activation(M["xT"][0:D, 0:n * P], M["xTp"][0:D, 0:n * P], ACT.Copy).then_inc(S["ptc"], 1)

        def mlp_buffers(c, n=G):
            return dict(a=sb("a", [P, n, D], F32, c), aT=sb("aT", [D, n * P], F32, c), hT=sb("hT", [F1, n * P], F32, c),
                        aTp=ps("aTp", [P, 1024], c), hTp=ps("hTp", [P, 1024], c), op=ps("op", [P, 512], c))

        def proj_buffers(c, xTp=None, n=G):
            return dict(xT=sb("xT", [D + 1, n * P], F32, c), xTp=xTp or ps("xTp", [P, 1024], c), pj=ps("pj", [P, 1024], c))

        def wait_used(eng, s, count):
            if not isinstance(count, int) or count > 0:
                eng.wait_ge(s, count)

        def peeled2(eng, n, body):
            body(0)
            body(1)
            with eng.Fori(2, n) as i:
                body(i)

        with ExitStack() as c1:
            s_nst1 = [sem(f"s_nst1_{k}") for k in range(SLOTS)]
            s_nst2 = [sem(f"s_nst2_{k}") for k in range(SLOTS)]
            s_nconst = sem("s_nconst"); s_bnm = sem("s_bnm"); s_y2 = sem("s_y2_n"); s_bnp = sem("s_bnp"); s_xrest = sem("s_xrest"); s_o2 = sem("s_o2_n")
            s_cen, s_sq1, s_va1, s_sd1, s_sq2, s_va2, s_sd2 = (sem(f"s_{k}_n") for k in ("cen", "sq1", "va1", "sd1", "sq2", "va2", "sd2"))
            s_x1, s_x2, s_x3, s_tp1, s_tp2, s_tc1, s_tc2, s_hp, s_hc, s_op, s_pj, s_o3, s_hq = (sem(f"s_{k}_n") for k in ("x1", "x2", "x3", "tp1", "tp2", "tc1", "tc2", "hp", "hc", "op", "pj", "o3", "hq"))
            gi = sb("gi", [P, SLOTS, G], I32, c1)
            gv = sb("gv", [P, SLOTS, G, 2], F32, c1)
            Xn = sb("Xn", [P, T, D], F32, c1)
            y1 = sb("y1", [P, G, D], F32, c1)
            sq1 = sb("sq1", [P, G, D], F32, c1)
            sq2 = sb("sq2", [P, G, D], F32, c1)
            mu1 = sb("mu1", [P, G], F32, c1)
            va = sb("va", [P, 2, G], F32, c1)
            sd = sb("sd", [P, 3, G], F32, c1)
            rs = sb("rs", [P, 3, G], F32, c1)
            x1 = sb("x1", [P, SLOTS, G, D], F32, c1)
            x2 = sb("x2", [P, G, D], F32, c1)
            o2 = sb("o2", [P, SLOTS, G, D], F32, c1)
            o3 = sb("o3", [P, SLOTS, G, D], F32, c1)
            o5 = sb("o5", [P, SLOTS, G, 3 * D], F32, c1)
            aT = sb("aT", [D, G * P], F32, c1)
            xT = sb("xT", [D + 1, G * P], F32, c1)
            hT = sb("hT", [F1, G * P], F32, c1)
            mk = sb("mk", [P, G], F32, c1)
            w2c = sb("w2c", [F1, 2 * D], F32, c1)
            b2c = sb("b2c", [P, D], F32, c1)
            wm = sb("wm", [P, 2], F32, c1)
            x1b = sb("x1b", [P, SLOTS, G, D], F32, c1)
            y2 = sb("y2", [P, G, D], F32, c1)
            hm = sb("hm", [P, G, 2 * D], F32, c1)
            hs = sb("hs", [P, G, 2 * D], F32, c1)
            hr = sb("hr", [P, 2 * D], F32, c1)
            eps2 = sb("eps2", [P, 1], F32, c1)
            tps = ps("tps", [P, 1024], c1)
            hTp = ps("hTp", [P, 1024], c1)
            op = ps("op", [P, 1024], c1)
            pj = ps("pj", [P, 512], c1)
            bnp = ps("bnp", [1, 512], c1)
            opg = op[:, 0:G * 2 * D].rearrange("p (t d) -> p t d", d=2 * D)
            with nc.Block() as block:
                @block.sync
                def _(sp):
                    sp.wait_ge(s_nconst, 1)
                    def load_x(j0, j1, s_part):
                        for p0, k in PARTS:
                            w = TAIL if p0 == P - 1 else T
                            rows_in = x[p0 * T:p0 * T + (k - 1) * T + w, :].rearrange("(p t) d -> p t d", t=w)
                            sp.dma_start(Xn[p0:p0 + k, j0:min(j1, w), :], rows_in[:, j0:min(j1, w), :]).then_inc(s_part, 16)

                    load_x(0, 2 * SLOTS * G, s_w)
                    sp.dma_start(w1s[:, :], W1).then_inc(s_w, 16)
                    sp.dma_start(w2s[:, :], W2).then_inc(s_w, 16)
                    sp.dma_start(wsr[0:D, 0:D], Ws.rearrange("f h d -> f (h d)")).then_inc(s_w, 16)
                    sp.dma_start(wsr[0:D, D:2 * D], Wr.rearrange("f h d -> f (h d)")).then_inc(s_w, 16)
                    sp.dma_start(wsr[D:D + 1, 0:D], bs.rearrange("(o h) d -> o (h d)", o=1)).then_inc(s_w, 16)
                    sp.dma_start(wsr[D:D + 1, D:2 * D], br.rearrange("(o h) d -> o (h d)", o=1)).then_inc(s_w, 16)
                    sp.dma_start(b1c[:, :], b1.rearrange("(f o) -> f o", o=1)).then_inc(s_w, 16)
                    sp.dma_start(b2b[:, :], b2.rearrange("(o f) -> o f", o=1).broadcast_to([P, D])).then_inc(s_w, 16)
                    for h in range(H):
                        sp.dma_start(awb[:, h * HD:(h + 1) * HD], aw.rearrange("(o f) -> o f", o=1).broadcast_to([P, HD])).then_inc(s_w, 16)
                    sp.dma_start(abb[:, :], ab.rearrange("(o f) -> o f", o=1).broadcast_to([P, 1])).then_inc(s_w, 16)
                    sp.dma_start(ef_tail[0:TAIL, :], ef[(P - 1) * T:E, :]).then_inc(s_w, 16)
                    sp.dma_start(ef_tail[TAIL:T, :], ef[0:T - TAIL, :]).then_inc(s_w, 16)
                    load_x(2 * SLOTS * G, T, s_xrest)
                    sp.wait_ge(s_w, 18 * 16)
                    sp.sem_inc(s_w, 1)

                    def rows(t, g):
                        return edges_of(t[0:NP, :])[:, bass.ds(g * G, G), :]

                    def store_x3(g, k):
                        sp.wait_ge(s_hq, g + 1)
                        sp.sem_inc(s_spturn, 1)
                        sp.dma_start(rows(T4, g), o5[:, k, :, 0:D]).then_inc(s_nst2[k], 16)
                        sp.dma_start(rows(T5, g), o5[:, k, :, 0:2 * D]).then_inc(s_nst2[k], 16)

                    def store_projection(g, k):
                        sp.wait_ge(s_o3, g + 1)
                        sp.sem_inc(s_spturn, 1)
                        sp.dma_start(rows(T3s, g), o3[:, k, :, :]).then_inc(s_nst2[k], 16)

                    def body(i):
                        for k in range(SLOTS):
                            g = i * SLOTS + k
                            first = isinstance(i, int) and i + k == 0
                            sp.wait_ge(s_x1, g + 1)
                            sp.sem_inc(s_spturn, 1)
                            sp.dma_start(rows(T1, g), x1[:, k, :, :]).then_inc(s_nst1[k], 16)
                            if not first:
                                store_x3(g - 1, 1 - k)
                            sp.wait_ge(s_o2, g + 1)
                            sp.sem_inc(s_spturn, 1)
                            sp.dma_start(rows(T2, g), o2[:, k, :, :]).then_inc(s_nst1[k], 16)
                            if not first:
                                store_projection(g - 1, 1 - k)
                    peeled2(sp, STEPS, body)
                    store_x3(NG - 1, 1)
                    store_projection(NG - 1, 1)
                    for k in range(SLOTS):
                        sp.wait_ge(s_nst1[k], STEPS * 32)
                        sp.wait_ge(s_nst2[k], STEPS * 48)

                @block.gpsimd
                def _(pool):
                    def body(i):
                        for k in range(SLOTS):
                            pool.wait_ge(s_si[2], i * SLOTS + k + 1)
                            pool.sem_inc(s_turn, 1)
                            for t in range(G):
                                pool.indirect_dma_start(out=gv[:, k, t, :], out_offset=None, in_=tab_sr, in_offset=bass.IndirectOffsetOnAxis(ap=gi[:, k, t:t + 1], axis=0)).then_inc(s_gs[2][k], 16)
                    peeled(pool, STEPS, body)

                @block.tensor
                def _(pe):
                    pe.wait_ge(s_nconst, 2)
                    def front_hidden(g, k):
                        pe.wait_ge(s_x1, g + 1)
                        pe.sem_inc(s_peturn, 1)
                        for t in range(G):
                            last = nc.tensor.transpose(tps[0:D, t * P:(t + 1) * P], x1[:, k, t, :], ident[:, :])
                        last.then_inc(s_tp1, 1)
                        pe.wait_ge(s_tc1, g + 1)
                        for c0 in range(0, G * P, 512):
                            c1_ = min(G * P, c0 + 512)
                            last = nc.tensor.matmul(hTp[:, c0:c1_], w1s[:, :], aT[:, c0:c1_], start=True, stop=True)
                        last.then_inc(s_hp, 1)

                    def back_transposes(g):
                        pe.wait_ge(s_x2, g + 1)
                        pe.sem_inc(s_peturn, 1)
                        for t in range(G):
                            last = nc.tensor.transpose(tps[0:D, t * P:(t + 1) * P], x2[:, t, :], ident[:, :])
                        last.then_inc(s_tp2, 1)

                    def front_output(g):
                        pe.wait_ge(s_hc, g + 1)
                        wait_used(pe, s_y2, g)
                        for t in range(G):
                            last = nc.tensor.matmul(op[:, t * 2 * D:(t + 1) * 2 * D], hT[:, t * P:(t + 1) * P], w2c[:, :], start=True, stop=True)
                        last.then_inc(s_op, 1)

                    def back_projection(g):
                        pe.wait_ge(s_tc2, g + 1)
                        wait_used(pe, s_o3, g)
                        for t in range(G):
                            last = nc.tensor.matmul(pj[:, t * D:(t + 1) * D], xT[:, t * P:(t + 1) * P], wsr[:, 0:D], start=True, stop=True)
                        last.then_inc(s_pj, 1)

                    def body(i):
                        for k in range(SLOTS):
                            g = i * SLOTS + k
                            first = isinstance(i, int) and i + k == 0
                            front_hidden(g, k)
                            if not first:
                                back_transposes(g - 1)
                            front_output(g)
                            if not first:
                                back_projection(g - 1)
                    peeled2(pe, STEPS, body)
                    back_transposes(NG - 1)
                    back_projection(NG - 1)
                    pe.wait_ge(s_bnm, 1)
                    nc.tensor.matmul(bnp[0:1, 0:2 * D], ones[:, 0:1], hr[:, :], start=True, stop=True).then_inc(s_bnp, 1)

                @block.scalar
                def _(act):
                    A = nc.scalar

                    def taken_in(g, k):
                        A.copy(meta[:, bass.ds(g * G, G), ALPHA], gv[:, k, :, 0])
                        A.copy(meta[:, bass.ds(g * G, G), SROW], gv[:, k, :, 1]).then_inc(s_use, 1)

                    def gathers(g, k, i):
                        if not isinstance(i, int) or i:
                            act.wait_ge(s_gs[2][k], i * G * 16)
                            taken_in(g - SLOTS, k)
                            act.wait_ge(s_use, g - 1)
                        A.copy(gi[:, k, :], skey[:, bass.ds(g * G, G), 0]).then_inc(s_si[2], 1)

                    def front_squares(g):
                        act.wait_ge(s_cen, g + 1)
                        A.activation(sq1[:, :, :], y1[:, :, :], ACT.Square).then_inc(s_sq1, 1)

                    def front_deviation(g):
                        act.wait_ge(s_va1, g + 1)
                        A.activation(sd[:, 0, :], va[:, 0, :], ACT.Sqrt, bias=epst[:, 0:1], scale=1.0 / D).then_inc(s_sd1, 1)

                    def front_rows(g):
                        act.wait_ge(s_tp1, g + 1)
                        A.activation(aT[:, :], tps[0:D, 0:G * P], ACT.Copy).then_inc(s_tc1, 1)

                    def front_hidden(g):
                        act.wait_ge(s_hp, g + 1)
                        A.activation(hT[:, :], hTp[:, 0:G * P], ACT.Relu, bias=b1c[:, 0:1], scale=1.0).then_inc(s_hc, 1)

                    def front_results(g, k, used):
                        wait_used(act, s_nst1[k], used * 32)
                        act.wait_ge(s_op, g + 1)
                        A.activation(o2[:, k, :, :], opg[:, :, 0:D], ACT.Copy).then_inc(s_o2, 1)

                    def back_squares(g):
                        act.wait_ge(s_y2, g + 1)
                        A.activation(sq2[:, :, :], y2[:, :, :], ACT.Square).then_inc(s_sq2, 1)

                    def back_deviations(g):
                        act.wait_ge(s_va2, g + 1)
                        A.activation(sd[:, 1, :], va[:, 1, :], ACT.Sqrt, bias=epst[:, 0:1], scale=1.0 / D)
                        A.activation(sd[:, 2, :], va[:, 1, :], ACT.Sqrt, bias=eps2[:, 0:1], scale=(1.0 + EPS) / D).then_inc(s_sd2, 1)

                    def back_rows(g):
                        act.wait_ge(s_tp2, g + 1)
                        A.activation(xT[0:D, :], tps[0:D, 0:G * P], ACT.Copy).then_inc(s_tc2, 1)

                    def back_batch(g, k):
                        act.wait_ge(s_x3, g + 1)
                        A.activation(o5[:, k, :, 2 * D:3 * D], o5[:, k, :, 0:D], ACT.Square, scale=1.0 / 13).then_inc(s_hq, 1)

                    def back_results(g, k, used):
                        wait_used(act, s_nst2[k], used * 48)
                        act.wait_ge(s_pj, g + 1)
                        A.activation(o3[:, k, :, :], pj[:, 0:G * D].rearrange("p (t d) -> p t d", d=D), ACT.Copy).then_inc(s_o3, 1)

                    def body(i):
                        for k in range(SLOTS):
                            g = i * SLOTS + k
                            first = isinstance(i, int) and i + k == 0
                            if isinstance(i, int) and i + k == 0:
                                gathers(0, 0, 0)
                                gathers(1, 1, 0)
                            front_squares(g)
                            if not isinstance(i, int) or i > 0:
                                gathers(g, k, i)
                            front_deviation(g)
                            front_rows(g)
                            if not first:
                                back_squares(g - 1)
                                back_deviations(g - 1)
                            front_hidden(g)
                            if not first:
                                back_rows(g - 1)
                                back_batch(g - 1, 1 - k)
                            front_results(g, k, i)
                            if not first:
                                back_results(g - 1, 1 - k, i - 1 + k)
                    peeled2(act, STEPS, body)
                    back_squares(NG - 1)
                    back_deviations(NG - 1)
                    back_rows(NG - 1)
                    back_batch(NG - 1, 1)
                    back_results(NG - 1, 1, STEPS - 1)
                    for k in range(SLOTS):
                        act.wait_ge(s_gs[2][k], STEPS * G * 16)
                        taken_in(NG - SLOTS + k, k)

                @block.vector
                def _(dve):
                    V = nc.vector
                    V.memset(Xn[96:P, TAIL:T, :], 0.0)
                    V.memset(xT[D:D + 1, :], 1.0)
                    V.memset(bn[:, :, :], 0.0)
                    V.memset(eps2[:, :], EPS * EPS)
                    V.memset(hs[:, :, :], 0.0)
                    dve.drain()
                    V.memset(wm[:, :], 0.0).then_inc(s_nconst, 1)
                    dve.wait_ge(s_w, 18 * 16 + 1)
                    dve.drain()
                    V.tensor_reduce(wm[:, 0:1], w2s[:, :], AX.X, ALU.add)
                    V.tensor_reduce(wm[:, 1:2], b2b[:, :], AX.X, ALU.add)
                    V.tensor_copy(w2c[:, 0:D], w2s[:, :])
                    dve.drain()
                    V.tensor_scalar(wm[:, :], wm[:, :], 1.0 / D, None, ALU.mult)
                    dve.drain()
                    V.tensor_scalar(w2c[:, D:2 * D], w2s[:, :], wm[:, 0:1], None, ALU.subtract)
                    V.tensor_scalar(b2c[:, :], b2b[:, :], wm[:, 1:2], None, ALU.subtract)
                    dve.drain()
                    V.memset(wm[:, :], 0.0).then_inc(s_nconst, 1)

                    def wide(v):
                        return v.unsqueeze(2).broadcast_to([P, G, D])

                    def centre(g):
                        xv = Xn[:, bass.ds(g * G, G), :]
                        V.tensor_reduce(mu1[:, :], xv, AX.X, ALU.add)
                        dve.drain()
                        V.scalar_tensor_tensor(y1[:, :, :], wide(mu1[:, :]), -1.0 / D, xv, ALU.mult, ALU.add).then_inc(s_cen, 1)

                    def front_sums(g):
                        dve.wait_ge(s_sq1, g + 1)
                        V.tensor_reduce(va[:, 0, :], sq1[:, :, :], AX.X, ALU.add).then_inc(s_va1, 1)

                    def front_norm(g, k, used):
                        wait_used(dve, s_nst1[k], used * 32)
                        dve.wait_ge(s_sd1, g + 1)
                        V.reciprocal(rs[:, 0, :], sd[:, 0, :])
                        dve.drain()
                        V.tensor_tensor(x1[:, k, :, :], y1[:, :, :], wide(rs[:, 0, :]), ALU.mult).then_inc(s_x1, 1)
                        dve.drain()
                        V.tensor_tensor(x1b[:, k, :, :], x1[:, k, :, :], b2c[:, :].unsqueeze(1).broadcast_to([P, G, D]), ALU.add)
                        dve.drain()

                    def back_centre(g, k):
                        dve.wait_ge(s_o2, g + 1)
                        V.tensor_tensor(y2[:, :, :], opg[:, :, D:2 * D], x1b[:, k, :, :], ALU.add).then_inc(s_y2, 1)

                    def back_sums(g):
                        dve.wait_ge(s_sq2, g + 1)
                        V.tensor_reduce(va[:, 1, :], sq2[:, :, :], AX.X, ALU.add).then_inc(s_va2, 1)

                    def back_norm(g, k, used):
                        wait_used(dve, s_nst2[k], used * 48)
                        V.tensor_scalar(mk[:, :], iso[:, bass.ds(g * G, G)], 1.0, None, ALU.mult)
                        dve.wait_ge(s_sd2, g + 1)
                        V.reciprocal(rs[:, 1:3, :], sd[:, 1:3, :])
                        dve.drain()
                        V.tensor_tensor(x2[:, :, :], y2[:, :, :], wide(rs[:, 1, :]), ALU.mult).then_inc(s_x2, 1)
                        V.tensor_tensor(o5[:, k, :, 0:D], y2[:, :, :], wide(rs[:, 2, :]), ALU.mult)
                        dve.drain()
                        V.tensor_scalar(o5[:, k, :, D:2 * D], o5[:, k, :, 0:D], 1.0 / 13, None, ALU.mult).then_inc(s_x3, 1)

                    def back_batch(g, k):
                        dve.drain()
                        dve.wait_ge(s_hq, g + 1)
                        V.tensor_tensor(hm[:, :, :], o5[:, k, :, D:3 * D], mk[:, :].unsqueeze(2).broadcast_to([P, G, 2 * D]), ALU.mult)
                        dve.drain()
                        V.tensor_tensor(hs[:, :, :], hs[:, :, :], hm[:, :, :], ALU.add)

                    def body(i):
                        for k in range(SLOTS):
                            g = i * SLOTS + k
                            first = isinstance(i, int) and i + k == 0
                            centre(g)
                            front_sums(g)
                            front_norm(g, k, i)
                            if not first:
                                back_centre(g - 1, 1 - k)
                                back_sums(g - 1)
                                back_norm(g - 1, 1 - k, i - 1 + k)
                                back_batch(g - 1, 1 - k)
                    body(0)
                    body(1)
                    dve.wait_ge(s_xrest, 48)
                    with dve.Fori(2, STEPS) as i:
                        body(i)
                    back_centre(NG - 1, 1)
                    back_sums(NG - 1)
                    back_norm(NG - 1, 1, STEPS - 1)
                    back_batch(NG - 1, 1)
                    dve.drain()
                    V.tensor_reduce(hr[:, :], hs[:, :, :].rearrange("p t d -> p d t"), AX.X, ALU.add).then_inc(s_bnm, 1)
                    dve.wait_ge(s_bnp, 1)
                    V.tensor_copy(bn[0:1, 0, :], bnp[0:1, 0:2 * D])
                    dve.wait_ge(s_use, NG)
                    V.tensor_scalar(meta[:, :, ALPHA], meta[:, :, ALPHA], 1e-16, None, ALU.add)
                    dve.drain()
                    V.reciprocal(meta[:, :, ALPHA], meta[:, :, ALPHA])
                    dve.drain()
                    V.tensor_tensor(meta[:, :, ALPHA], meta[:, :, ALPHA], exj[:, :], ALU.mult)
        ctxS.close()
        X = sb("X", [P, T, D])
        XB = sb("XB", [P, 1, D])
        roles = {}

        def edge_phase(kind):
            W = {"gat": 72, "pna": 4 * D}.get(kind, D)
            S_d = S_lin[W]
            normed = kind in ("att", "gcn2", "gat")
            gathered = {"att": (), "gcn1": ((T1, SROW),), "gcn2": ((T2, SROW),), "gat": ((T3s, SROW), (T3r, DROW)),
                        "pna": ((T4, SROW),)}[kind]
            linear = {"att": 1, "gcn2": 1, "pna": 3}.get(kind, 0)
            outs = {"att": ((T1, D),), "gcn1": ((T2, D),), "gcn2": ((T3s, D), (T3r, D)), "gat": ((T4, D), (T5[:, 0:D], D)), "pna": ((T5[:, D:2 * D], D),)}[kind]
            lag = 1 if kind in ("att", "gcn1", "pna") else 2
            S = {}

            def psem(name):
                if name not in roles:
                    roles[name] = sem("edge_" + name[2:])
                return roles[name]

            for name in {"att": ("cen", "sq", "var", "sd"), "gcn1": ("ain", "tp", "tc", "hp", "hc", "o"), "gcn2": ("cen", "sq", "var", "sd", "pin", "ptp", "ptc", "pj"),
                         "gat": ("cen", "sq", "var", "sd", "z", "u", "se", "dm", "f", "sc"), "pna": ("var", "sd", "z", "m", "hq", "bn")}[kind]:
                S[name] = psem(f"s_{name}")
            s_acc = psem("s_acc"); s_res = psem("s_res"); s_used = psem("s_used")
            s_bc = psem("s_bc"); s_bp = psem("s_bp"); s_xl = psem("s_xl"); s_bs = psem("s_bs"); s_bt = psem("s_bt")
            s_g = [sem(f"s_g{k}_{kind}") for k in range(SLOTS)]
            s_l = [psem(f"s_l{k}") for k in range(SLOTS)]
            s_so = [psem(f"s_so{k}") for k in range(SLOTS)]
            s_ro = [psem(f"s_ro{k}") for k in range(SLOTS)]
            per_gather = G * 16 * len(gathered)
            with ExitStack() as c1:
                B = buffers(c1) if normed else None
                M = mlp_buffers(c1) if kind == "gcn1" else None
                J = proj_buffers(c1) if kind == "gcn2" else None
                xr = sb("xr", [P, G, D], F32, c1) if kind == "gcn2" else None
                cps = ps("cps", [P, 2, 512], c1)
                idx = sb("idx", [P, SLOTS, 2, G], I32, c1)
                gx = sb("gx", [P, SLOTS, max(1, len(gathered)), G, D], F32, c1)
                lx = sb("lx", [P, SLOTS, G, D], F32, c1) if linear else None
                acc = sb("acc", [P, SLOTS * G, W], F32, c1)
                md = sb("md", [P, SLOTS, G, NM], F32, c1)
                msg = sb("msg", [P, G, W], F32, c1)
                res = None if kind == "gat" else [sb("res", [P, SLOTS, G, w], F32, c1) for _, w in outs]
                sB = sb("sB", [P, 1, W], F32, c1)
                cr = sb("cr", [P, 2, P], F32, c1)
                ct = sb("ct", [P, 2, P], F32, c1)
                if kind == "pna":
                    hb = sb("hb", [P, G, D], F32, c1)
                    mm = sb("mm", [P, G, D], F32, c1)
                    hq = sb("hq", [P, G, 2 * D], F32, c1)
                    mk = sb("mk", [P, G], F32, c1)
                    zc = sb("zc", [P, 1], F32, c1)
                    bnp = ps("bnp", [1, 512], c1)
                if kind == "gat":
                    zz = sb("zz", [P, SLOTS, G, D], F32, c1)
                    uu = sb("uu", [P, SLOTS, G, D], F32, c1)
                    se = sb("se", [P, SLOTS, G, D], F32, c1)
                    t1 = sb("t1", [P, G, D], F32, c1)
                    t2 = sb("t2", [P, G, D], F32, c1)
                    lg = sb("lg", [P, G, H], F32, c1)
                    dm = sb("dm", [P, 2, G, H], F32, c1)
                    ff = sb("ff", [P, 2, G, H], F32, c1)
                    fs = sb("fs", [P, 68, G + 1], F32, c1)
                    ms = sb("ms", [P, 68, G + 1], F32, c1)
                    ac = sb("ac", [P, 68, G + 1], F32, c1)
                    mx = sb("mx", [P, SLOTS * G, H], F32, c1)
                    mB = sb("mB", [P, 2, H], F32, c1)
                    m68 = sb("m68", [P, 4, 68], F32, c1)
                    fB = sb("fB", [P, 2, P], F32, c1)

                def has(i, k, n):
                    return not isinstance(i, int) or i * SLOTS + k >= n

                with nc.Block() as block:
                    @block.sync
                    def _(sp):
                        if kind == "att":
                            sp.dma_start(X[:, :, :], edges_of(xd_lin)).then_inc(s_xl, 16)

                        def store_sums(g, k):
                            sp.wait_ge(s_acc, g + 1)
                            sp.sem_inc(s_spturn, 1)
                            sp.dma_start(edges_of(S_d)[:, bass.ds(g * G, G), :], acc[:, k * G:(k + 1) * G, :]).then_inc(s_so[k], 16)

                        def store_rows(g, k):
                            sp.wait_ge(s_res, g + 1)
                            sp.sem_inc(s_spturn, 1)
                            for q, (d, w) in enumerate(outs):
                                base = 0 if d is T3r else EDGE0
                                r = X[:, bass.ds(g * G, G), :] if kind == "gat" else res[q][:, k, :, :]
                                sp.dma_start(edges_of(d[base:base + NP, :])[:, bass.ds(g * G, G), :], r).then_inc(s_ro[k], 16)

                        def load(i, k):
                            g = i * SLOTS + k
                            j = bass.ds(g * G, G)
                            if has(i, k, 2) and linear:
                                sp.wait_ge(s_used, g - 1 + (SLOTS if gathered else 0))
                                sp.sem_inc(s_spturn, 1)
                            if kind == "att":
                                sp.dma_start(lx[:, k, :, :], edges_of(xs_lin)[:, j, :]).then_inc(s_l[k], 16)
                            if kind == "gcn2":
                                sp.dma_start(lx[:, k, :, :], edges_of(T2[EDGE0:EDGE0 + NP, :])[:, j, :]).then_inc(s_l[k], 16)
                            if kind == "pna":
                                for p0, n in PARTS[0:2]:
                                    v = ef[p0 * T:(p0 + n) * T, :].rearrange("(p t) d -> p t d", t=T)
                                    sp.dma_start(lx[p0:p0 + n, k, :, :], v[:, j, :]).then_inc(s_l[k], 16)
                                sp.dma_start(lx[P - 1:P, k, :, :], ef_tail[j, :].rearrange("(o t) d -> o t d", o=1)).then_inc(s_l[k], 16)

                        def body(i):
                            for k in range(SLOTS):
                                load(i, k)
                                if has(i, k, 1):
                                    store_sums(i * SLOTS + k - 1, 1 - k)
                                if has(i, k, lag + 1):
                                    store_rows(i * SLOTS + k - lag - 1, (k - lag - 1) % 2)
                        body(0)
                        body(1)
                        with sp.Fori(2, STEPS) as i:
                            body(i)
                        store_sums(NG - 1, 1)
                        for g in range(NG - lag - 1, NG):
                            store_rows(g, g % 2)
                        sp.wait_ge(s_so[0], STEPS * 16)
                        sp.wait_ge(s_so[1], STEPS * 16)
                        sp.sem_inc(s_bs, 1)
                        sp.wait_ge(s_res, NG + 1)
                        for q, (d, w) in enumerate(outs):
                            base = NP if d is T3r else BOUND0
                            sp.dma_start(d[base:base + P, :], XB[:, 0, :] if kind == "gat" else res[q][:, 0, 0, :]).then_inc(s_ro[0], 16)
                        sp.wait_ge(s_ro[0], (STEPS + 1) * 16 * len(outs))
                        sp.wait_ge(s_ro[1], STEPS * 16 * len(outs))

                    @block.gpsimd
                    def _(pool):
                        def body(i):
                            for k in range(SLOTS):
                                g = i * SLOTS + k
                                if kind == "gat" and has(i, k, 2):
                                    pool.wait_ge(S["se"], g - 1)
                                else:
                                    pool.wait_ge(s_used, g + 1)
                                pool.sem_inc(s_turn, 1)
                                for q, (d, _) in enumerate(gathered):
                                    for t in range(G):
                                        pool.indirect_dma_start(out=gx[:, k, q, t, :], out_offset=None, in_=d, in_offset=bass.IndirectOffsetOnAxis(ap=idx[:, k, q, t:t + 1], axis=0)).then_inc(s_g[k], 16)
                        if gathered:
                            peeled(pool, STEPS, body)
                        pool.wait_ge(s_bs, 1)
                        pool.indirect_dma_start(out=sB[:, 0, :], out_offset=None, in_=S_d, in_offset=bass.IndirectOffsetOnAxis(ap=bidx[:, 0:1], axis=0)).then_inc(s_g[0], 16)
                        if kind == "att":
                            pool.indirect_dma_start(out=XB[:, 0, :], out_offset=None, in_=xd_lin, in_offset=bass.IndirectOffsetOnAxis(ap=bidx[:, 0:1], axis=0)).then_inc(s_g[0], 16)

                    @block.scalar
                    def _(act):
                        def work(g, n):
                            if kind == "gcn1":
                                mlp_act(act, M, n, S, g + 1)
                            if kind in ("att", "gcn2"):
                                norm_squares(act, B, n, S, g + 1)
                                norm_act(act, B, n, S, g + 1)

                        def pna_deviation(g, n):
                            act.wait_ge(S["var"], g + 1)
                            nc.scalar.activation(hb[:, 0:n, :], hb[:, 0:n, :], ACT.Sqrt, bias=epst[:, 0:1], scale=1.0).then_inc(S["sd"], 1)

                        def pna_messages(g):
                            act.wait_ge(S["z"], g + 1)
                            nc.scalar.activation(msg[:, :, D:2 * D], msg[:, :, 0:D], ACT.Square)
                            nc.scalar.activation(msg[:, :, 2 * D:3 * D], msg[:, :, 0:D], ACT.Copy)
                            nc.scalar.activation(msg[:, :, 3 * D:4 * D], msg[:, :, 0:D], ACT.Copy, scale=-1.0).then_inc(S["m"], 1)

                        def pna_batch(g, k, n):
                            act.wait_ge(s_res, g + 1)
                            nc.scalar.activation(hq[:, 0:n, 0:D], res[0][:, k, 0:n, :], ACT.Copy)
                            nc.scalar.activation(hq[:, 0:n, D:2 * D], res[0][:, k, 0:n, :], ACT.Square).then_inc(S["hq"], 1)

                        def project(k, n, g, stored):
                            if stored is not None:
                                act.wait_ge(s_ro[k], stored)
                            act.wait_ge(S["pj"], g + 1)
                            v = J["pj"][:, 0:n * 2 * D].rearrange("p (t d) -> p t d", d=2 * D)
                            nc.scalar.activation(res[0][:, k, 0:n, :], v[:, :, 0:D], ACT.Copy)
                            nc.scalar.activation(res[1][:, k, 0:n, :], v[:, :, D:2 * D], ACT.Copy).then_inc(s_res, 1)

                        def gat_u(g, k):
                            act.wait_ge(S["z"], g + 1)
                            nc.scalar.activation(uu[:, k, :, :], uu[:, k, :, :], ACT.Exp).then_inc(S["u"], 1)
                            nc.scalar.activation(se[:, k, :, :], gx[:, k, 0, :, :], ACT.Copy).then_inc(S["se"], 1)

                        def gat_f(g):
                            act.wait_ge(S["dm"], g + 1)
                            nc.scalar.activation(ff[:, :, :, :], dm[:, :, :, :], ACT.Exp).then_inc(S["f"], 1)

                        def gat_rows(g, k, stored):
                            if stored is not None:
                                act.wait_ge(s_so[k], stored)
                            act.wait_ge(S["sc"], g + 1)
                            nc.scalar.activation(acc[:, k * G:(k + 1) * G, 0:68], ac[:, :, 1:G + 1].rearrange("p c t -> p t c"), ACT.Copy)
                            nc.scalar.activation(acc[:, k * G:(k + 1) * G, 68:72], mx[:, k * G:(k + 1) * G, :], ACT.Copy).then_inc(s_acc, 1)

                        def body(i):
                            for k in range(SLOTS):
                                g = i * SLOTS + k
                                if kind == "gat":
                                    gat_u(g, k)
                                    if has(i, k, 2):
                                        norm_act(act, B, G, S, g - 1)
                                    if has(i, k, 1):
                                        gat_f(g - 1)
                                        gat_rows(g - 1, 1 - k, (i + k - 1) * 16 if has(i, k, 3) else None)
                                        norm_squares(act, B, G, S, g)
                                elif kind == "pna":
                                    if has(i, k, 1):
                                        pna_deviation(g - 1, G)
                                    pna_messages(g)
                                    if has(i, k, 1):
                                        pna_batch(g - 1, 1 - k, G)
                                elif has(i, k, 1):
                                    if kind == "gcn2" and has(i, k, 2):
                                        proj_act(act, J, G, S, g - 1)
                                    work(g - 1, G)
                                    if kind == "gcn2" and has(i, k, 2):
                                        project(k, G, g - 2, (i - 1) * 32 if has(i, k, 4) else None)
                        peeled2(act, STEPS, body)
                        if kind == "gat":
                            norm_act(act, B, G, S, NG - 1)
                            gat_f(NG - 1)
                            gat_rows(NG - 1, 1, (STEPS - 1) * 16)
                            norm_squares(act, B, G, S, NG)
                            norm_act(act, B, G, S, NG)
                            act.wait_ge(S["dm"], NG + 1)
                            nc.scalar.activation(fB[0:68, :, :], fB[0:68, :, :], ACT.Exp).then_inc(S["f"], 1)
                            act.wait_ge(S["dm"], NG + 2)
                            nc.scalar.activation(m68[:, 2:4, :], m68[:, 2:4, :], ACT.Exp).then_inc(S["f"], 1)
                            norm_squares(act, B, 1, S, NG + 1)
                            norm_act(act, B, 1, S, NG + 1)
                        elif kind == "pna":
                            for g, k, n in ((NG - 1, 1, G), (NG, 0, 1)):
                                pna_deviation(g, n)
                                pna_batch(g, k, n)
                        elif kind == "gcn2":
                            proj_act(act, J, G, S, NG - 1)
                            work(NG - 1, G)
                            project(0, G, NG - 2, (STEPS - 1) * 32)
                            proj_act(act, J, G, S, NG)
                            project(1, G, NG - 1, (STEPS - 1) * 32)
                            work(NG, 1)
                            proj_act(act, J, 1, S, NG + 1)
                            project(0, 1, NG, STEPS * 32)
                        else:
                            work(NG - 1, G)
                            work(NG, 1)

                    @block.tensor
                    def _(pe):
                        def work(g, n):
                            if kind == "gcn1":
                                mlp_pe(pe, M, n, S, g + 1, s_res)
                            if kind == "gcn2":
                                proj_pe(pe, J, xr, n, S, g + 1)
                            if kind == "pna":
                                pe.wait_ge(S["hq"], g + 1)
                                for t in range(n):
                                    last = nc.tensor.matmul(bnp[0:1, 0:2 * D], mk[:, t:t + 1], hq[:, t, :], start=False, stop=False)
                                last.then_inc(S["bn"], 1)

                        if kind == "pna":
                            pe.wait_ge(s_bp, 1)
                            nc.tensor.matmul(bnp[0:1, 0:2 * D], zc[:, :], ident[:, :], start=True, stop=False)
                        if kind in ("gcn1", "gcn2", "pna"):
                            def body(i):
                                for k in range(SLOTS):
                                    work(i * SLOTS + k, G)
                            peeled(pe, STEPS, body)
                        nq = 2 if kind in ("pna", "gat") else 1
                        w = {"pna": 2 * D, "gat": 68}.get(kind, D)
                        pe.wait_ge(s_bc, 1)
                        for q in range(nq):
                            srcv = m68[:, q, :] if kind == "gat" else acc[:, 2 * G - 1, q * w:(q + 1) * w]
                            last = nc.tensor.transpose(cps[0:w, q, 0:P], srcv, ident[:, :])
                        last.then_inc(s_bt, 1)
                        pe.wait_ge(s_bc, 2)
                        for q in range(nq):
                            last = nc.tensor.transpose(cps[:, q, 0:w], ct[0:w, q, :], ident[0:w, 0:w])
                        last.then_inc(s_bt, 1)
                        if kind in ("gcn1", "gcn2", "pna"):
                            work(NG, 1)
                        if kind == "pna":
                            nc.tensor.matmul(bnp[0:1, 0:2 * D], zc[:, :], ident[:, :], start=False, stop=True).then_inc(S["bn"], 1)

                    @block.vector
                    def _(dve):
                        V = nc.vector

                        def scans(k, v, lo, hi, is_max):
                            for t in range(G):
                                r = k * G + t
                                p = (r - 1) % (SLOTS * G)
                                last = V.scalar_tensor_tensor(acc[:, r, lo:hi], acc[:, p, lo:hi], md[:, k, t, NBIG:NBIG + 1] if is_max else md[:, k, t, CONT:CONT + 1],
                                                              v[:, t, lo:hi], ALU.add if is_max else ALU.mult, ALU.max if is_max else ALU.add)
                                if t < G - 1:
                                    dve.drain()
                            return last

                        def stage(g, k):
                            for q, (_, f) in enumerate(gathered):
                                V.tensor_copy(idx[:, k, q, :], meta_all[:, bass.ds(g * G, G), f])

                        def begin(i, k):
                            g = i * SLOTS + k
                            V.tensor_copy(md[:, k, :, :], meta[:, bass.ds(g * G, G), :])
                            dve.drain()
                            if gathered:
                                dve.wait_ge(s_g[k], i * per_gather + per_gather)
                                V.tensor_scalar(idx[:, k, 0, :], meta_all[:, bass.ds((g + SLOTS) * G, G), SROW], 1.0, None, ALU.mult)
                            if kind == "att":
                                dve.wait_ge(s_l[k], i * 16 + 16)
                                V.tensor_tensor(msg[:, :, :], lx[:, k, :, :], md[:, k, :, ALPHA:ALPHA + 1].broadcast_to([P, G, D]), ALU.mult).then_inc(s_used, 1)
                                dve.drain()
                            if kind == "pna":
                                dve.wait_ge(s_l[k], i * 48 + 48)
                                V.tensor_tensor(msg[:, :, 0:D], gx[:, k, 0, :, :], lx[:, k, :, :], ALU.add).then_inc(S["z"], 1)
                                dve.drain()
                                dve.sem_inc(s_used, 1)

                        def sums(i, k):
                            g = i * SLOTS + k
                            if kind == "pna":
                                dve.wait_ge(S["m"], g + 1)
                            if has(i, k, 2):
                                dve.wait_ge(s_so[k], i * 16)
                            if kind == "att":
                                scans(k, msg, 0, D, False).then_inc(s_acc, 1)
                            if kind == "gcn1":
                                scans(k, gx[:, k, 0, :, :], 0, D, False).then_inc(s_acc, 1)
                                dve.drain()
                                dve.sem_inc(s_used, 1)
                            if kind == "gcn2":
                                scans(k, gx[:, k, 0, :, :], 0, D, False).then_inc(s_acc, 1)
                            if kind == "pna":
                                scans(k, msg, 0, 2 * D, False)
                                scans(k, msg, 2 * D, 4 * D, True).then_inc(s_acc, 1)
                            dve.drain()

                        def post(a, xv, m, lv, n, g):
                            if kind == "att":
                                V.scalar_tensor_tensor(B["y"][:, 0:n, :], a, 0.0, xv, ALU.max, ALU.add)
                                dve.drain()
                                norm_a(dve, B, n, S)
                            if kind == "gcn1":
                                wait_used(dve, S["tp"], g)
                                dv = m[:, :, DINV:DINV + 1].broadcast_to([P, n, D])
                                V.tensor_tensor(msg[:, 0:n, :], xv, dv, ALU.mult)
                                dve.drain()
                                V.tensor_tensor(msg[:, 0:n, :], msg[:, 0:n, :], a, ALU.add)
                                dve.drain()
                                V.tensor_tensor(M["a"][:, 0:n, :], msg[:, 0:n, :], dv, ALU.mult).then_inc(S["ain"], 1)
                            if kind == "gcn2":
                                dv = m[:, :, DINV:DINV + 1].broadcast_to([P, n, D])
                                V.tensor_tensor(msg[:, 0:n, :], lv, a, ALU.add)
                                dve.drain()
                                if n == G:
                                    dve.sem_inc(s_used, 1)
                                V.tensor_tensor(msg[:, 0:n, :], msg[:, 0:n, :], dv, ALU.mult)
                                dve.drain()
                                V.tensor_tensor(msg[:, 0:n, :], msg[:, 0:n, :], xv, ALU.add)
                                dve.drain()
                                V.tensor_tensor(B["y"][:, 0:n, :], msg[:, 0:n, :], b2b[:, :].unsqueeze(1).broadcast_to([P, n, D]), ALU.add)
                                dve.drain()
                                norm_a(dve, B, n, S)
                            if kind == "gat":
                                av = ac[:, :, 1:G + 1].rearrange("p (h e) t -> p t h e", e=17) if n == G else a[:, :, 0:68].rearrange("p n (h e) -> p n h e", e=17)
                                V.reciprocal(lg[:, 0:n, :], av[:, :, :, 16])
                                dve.drain()
                                V.tensor_tensor(t1[:, 0:n, :].rearrange("p n (h e) -> p n h e", h=H), av[:, :, :, 0:16], lg[:, 0:n, :].unsqueeze(3).broadcast_to([P, n, H, HD]), ALU.mult)
                                dve.drain()
                                V.tensor_tensor(B["y"][:, 0:n, :], t1[:, 0:n, :], xv, ALU.add)
                                dve.drain()
                                norm_a(dve, B, n, S)
                            if kind == "pna":
                                rc = m[:, :, RCNT:RCNT + 1].broadcast_to([P, n, D])
                                V.tensor_tensor(mm[:, 0:n, :], a[:, :, 0:D], rc, ALU.mult)
                                V.tensor_tensor(hb[:, 0:n, :], a[:, :, D:2 * D], rc, ALU.mult)
                                dve.drain()
                                V.tensor_tensor(msg[:, 0:n, 0:D], mm[:, 0:n, :], mm[:, 0:n, :], ALU.mult)
                                dve.drain()
                                V.tensor_tensor(hb[:, 0:n, :], hb[:, 0:n, :], msg[:, 0:n, 0:D], ALU.subtract)
                                V.tensor_tensor(mm[:, 0:n, :], mm[:, 0:n, :], a[:, :, 2 * D:3 * D], ALU.add)
                                dve.drain()
                                V.tensor_scalar(hb[:, 0:n, :], hb[:, 0:n, :], 0.0, None, ALU.max).then_inc(S["var"], 1)
                                V.tensor_tensor(mm[:, 0:n, :], mm[:, 0:n, :], a[:, :, 3 * D:4 * D], ALU.subtract)
                                dve.drain()
                                V.scalar_tensor_tensor(mm[:, 0:n, :], xv, 3.0, mm[:, 0:n, :], ALU.mult, ALU.add)

                        def finish(xv, m, k, n, g):
                            if kind == "att":
                                norm_b(dve, B, n, S, g + 1, xv)
                                dve.drain()
                                V.tensor_tensor(res[0][:, k, 0:n, :], xv, m[:, :, DINV:DINV + 1].broadcast_to([P, n, D]), ALU.mult).then_inc(s_res, 1)
                            if kind == "gcn1":
                                dve.wait_ge(S["o"], g + 1)
                                V.tensor_tensor(res[0][:, k, 0:n, :], M["op"][:, 0:n * D].rearrange("p (t d) -> p t d", d=D), m[:, :, DINV:DINV + 1].broadcast_to([P, n, D]), ALU.mult).then_inc(s_res, 1)
                            if kind == "gcn2":
                                wait_used(dve, S["ptp"], g)
                                norm_b(dve, B, n, S, g + 1, xr[:, 0:n, :])
                                dve.drain()
                                V.tensor_scalar(xv, xr[:, 0:n, :], 1.0, None, ALU.mult).then_inc(S["pin"], 1)
                            if kind == "gat":
                                norm_b(dve, B, n, S, g + 1, xv).then_inc(s_res, 1)
                            if kind == "pna":
                                r = res[0][:, k, 0:n, :]
                                wait_used(dve, S["bn"], g)
                                dve.wait_ge(S["sd"], g + 1)
                                V.tensor_tensor(mm[:, 0:n, :], mm[:, 0:n, :], hb[:, 0:n, :], ALU.add)
                                dve.drain()
                                V.tensor_tensor(mm[:, 0:n, :], mm[:, 0:n, :], m[:, :, AMP:AMP + 1].broadcast_to([P, n, D]), ALU.mult)
                                V.tensor_copy(mk[:, 0:n].unsqueeze(2), m[:, :, MEND:MEND + 1])
                                dve.drain()
                                V.tensor_tensor(mm[:, 0:n, :], mm[:, 0:n, :], xv, ALU.add)
                                dve.drain()
                                V.tensor_scalar(r, mm[:, 0:n, :], 1.0 / 13, None, ALU.mult).then_inc(s_res, 1)
                            dve.drain()

                        def gat_front(i, k):
                            g = i * SLOTS + k
                            V.tensor_copy(md[:, k, :, :], meta[:, bass.ds(g * G, G), :])
                            dve.wait_ge(s_g[k], i * per_gather + per_gather)
                            V.tensor_tensor(zz[:, k, :, :], gx[:, k, 0, :, :], gx[:, k, 1, :, :], ALU.add)
                            stage(g + SLOTS, k)
                            dve.drain()
                            V.tensor_scalar(uu[:, k, :, :], zz[:, k, :, :], 20.0, None, ALU.min).then_inc(S["z"], 1)

                        def gat_back(g, k):
                            u, z = uu[:, k, :, :], zz[:, k, :, :]
                            dve.drain()
                            dve.wait_ge(S["u"], g + 1)
                            V.scalar_tensor_tensor(t1[:, :, :], u, 2.0, u, ALU.add, ALU.mult)
                            dve.drain()
                            V.tensor_scalar(t2[:, :, :], t1[:, :, :], 2.0, None, ALU.add)
                            V.tensor_tensor(t1[:, :, :], t1[:, :, :], z, ALU.mult)
                            dve.drain()
                            V.reciprocal(t2[:, :, :], t2[:, :, :])
                            dve.drain()
                            V.tensor_tensor(t1[:, :, :], t1[:, :, :], t2[:, :, :], ALU.mult)
                            dve.drain()
                            V.tensor_tensor(t1[:, :, :], t1[:, :, :], awb[:, :].unsqueeze(1).broadcast_to([P, G, D]), ALU.mult)
                            dve.drain()
                            V.tensor_reduce(lg[:, :, :], t1[:, :, :].rearrange("p t (h e) -> p t h e", h=H), AX.X, ALU.add)
                            dve.drain()
                            V.tensor_scalar(lg[:, :, :], lg[:, :, :], abb[:, 0:1], None, ALU.add)
                            dve.drain()
                            for t in range(G):
                                r = k * G + t
                                p = (r - 1) % (SLOTS * G)
                                V.scalar_tensor_tensor(mx[:, r, :], mx[:, p, :], md[:, k, t, NBIG:NBIG + 1], lg[:, t, :], ALU.add, ALU.max)
                                dve.drain()
                            V.tensor_tensor(dm[:, 0, 1:G, :], mx[:, k * G:(k + 1) * G - 1, :], mx[:, k * G + 1:(k + 1) * G, :], ALU.subtract)
                            p = (k * G - 1) % (SLOTS * G)
                            V.tensor_tensor(dm[:, 0, 0, :], mx[:, p, :], mx[:, k * G, :], ALU.subtract)
                            V.tensor_tensor(dm[:, 1, :, :], lg[:, :, :], mx[:, k * G:(k + 1) * G, :], ALU.subtract)
                            dve.drain()
                            V.tensor_scalar(dm[:, :, :, :], dm[:, :, :, :], 0.0, None, ALU.min).then_inc(S["dm"], 1)

                        def gat_sum(g, k):
                            dve.drain()
                            wait_used(dve, s_acc, g)
                            dve.wait_ge(S["f"], g + 1)
                            V.tensor_tensor(fs[:, :, 1:G + 1].rearrange("p (h e) t -> p h e t", e=17), ff[:, 0, :, :].rearrange("p t h -> p h t").unsqueeze(2).broadcast_to([P, H, 17, G]),
                                            md[:, k, :, CONT].unsqueeze(1).unsqueeze(1).broadcast_to([P, H, 17, G]), ALU.mult)
                            mv = ms[:, :, 1:G + 1].rearrange("p (h e) t -> p t h e", e=17)
                            V.tensor_tensor(mv[:, :, :, 0:16], se[:, k, :, :].rearrange("p t (h e) -> p t h e", h=H), ff[:, 1, :, :].unsqueeze(3).broadcast_to([P, G, H, HD]), ALU.mult)
                            V.tensor_copy(mv[:, :, :, 16], ff[:, 1, :, :])
                            V.tensor_copy(ms[:, :, 0:1], ac[:, :, G:G + 1])
                            dve.drain()
                            V.tensor_tensor_scan(ac[:, :, :].rearrange("p c t -> p (c t)"), fs[:, :, :].rearrange("p c t -> p (c t)"),
                                                 ms[:, :, :].rearrange("p c t -> p (c t)"), initial=0.0, op0=ALU.mult, op1=ALU.add).then_inc(S["sc"], 1)
                            dve.drain()

                        V.memset(acc[:, :, :], 0.0)
                        if kind == "gcn2":
                            V.memset(J["xT"][D:D + 1, :], 1.0)
                        if kind == "pna":
                            dve.drain()
                            V.memset(acc[:, :, 2 * D:4 * D], -BIG)
                            V.memset(zc[:, :], 0.0).then_inc(s_bp, 1)
                        if kind == "gat":
                            V.memset(mx[:, :, :], -BIG)
                            V.memset(fs[:, :, :], 0.0)
                            V.memset(ms[:, :, :], 0.0)
                            V.memset(ac[:, :, :], 0.0)
                            V.memset(m68[:, :, :], 0.0)
                        if gathered:
                            for k in range(SLOTS):
                                stage(k, k)
                            dve.drain()
                            dve.sem_inc(s_used, SLOTS)
                        if kind == "att":
                            dve.wait_ge(s_xl, 16)
                        dve.drain()

                        def stage_b(g, i, k, waits=True):
                            j = bass.ds(g * G, G)
                            xv = X[:, j, :]
                            if kind == "gcn2":
                                dve.wait_ge(s_l[k], i)
                            post(acc[:, k * G:(k + 1) * G, :], xv, md[:, k, :, :], lx[:, k, :, :] if lx else None, G, g)

                        def res_free(k, n):
                            if kind == "pna":
                                dve.drain()
                            if n is not None:
                                dve.wait_ge(s_ro[k], n)

                        def body(i):
                            for k in range(SLOTS):
                                g = i * SLOTS + k
                                o = 1 - k
                                no = 16 * len(outs)
                                if kind == "gat":
                                    gat_front(i, k)
                                    if has(i, k, 2):
                                        norm_sum(dve, B, G, S, g - 1)
                                    if has(i, k, 1):
                                        gat_back(g - 1, o)
                                    if has(i, k, 2):
                                        dve.drain()
                                        finish(X[:, bass.ds((g - 2) * G, G), :], md[:, k, :, :], k, G, g - 2)
                                    if has(i, k, 1):
                                        gat_sum(g - 1, o)
                                        stage_b(g - 1, None, o)
                                    continue
                                begin(i, k)
                                if normed and has(i, k, 1):
                                    norm_sum(dve, B, G, S, g)

                                def last_group():
                                    if has(i, k, 1):
                                        if lag == 1:
                                            w = i + k - 1
                                            res_free(o, w * no if has(i, k, 3) else None)
                                        finish(X[:, bass.ds((g - 1) * G, G), :], md[:, o, :, :], o, G, g - 1)

                                if kind == "pna":
                                    last_group()
                                    sums(i, k)
                                    stage_b(g, i * 16 + 16, k)
                                elif kind == "gcn1":
                                    sums(i, k)
                                    stage_b(g, i * 16 + 16, k)
                                    last_group()
                                else:
                                    sums(i, k)
                                    last_group()
                                    stage_b(g, i * 16 + 16, k)
                        body(0)
                        body(1)
                        with dve.Fori(2, STEPS) as i:
                            body(i)
                        no = 16 * len(outs)
                        if kind == "gat":
                            norm_sum(dve, B, G, S, NG - 1)
                            gat_back(NG - 1, 1)
                            dve.drain()
                            finish(X[:, (NG - 2) * G:(NG - 1) * G, :], md[:, 0, :, :], 0, G, NG - 2)
                            gat_sum(NG - 1, 1)
                            stage_b(NG - 1, None, 1)
                            norm_sum(dve, B, G, S, NG)
                            dve.drain()
                            finish(X[:, (NG - 1) * G:NG * G, :], md[:, 1, :, :], 1, G, NG - 1)
                        else:
                            if normed:
                                norm_sum(dve, B, G, S, NG)
                            if lag == 1:
                                res_free(1, (STEPS - 1) * no)
                            finish(X[:, (NG - 1) * G:NG * G, :], md[:, 1, :, :], 1, G, NG - 1)
                        dve.drain()

                        w = {"pna": 2 * D, "gat": 68}.get(kind, D)
                        final = 2 * G - 1
                        if kind == "gat":
                            V.tensor_copy(m68[:, 1, :].unsqueeze(2), ac[:, :, G:G + 1])
                            V.tensor_copy(m68[:, 0, :].rearrange("p (h e) -> p h e", e=17), mx[:, final, :].unsqueeze(2).broadcast_to([P, H, 17]))
                            dve.drain()
                        dve.sem_inc(s_bc, 1)
                        dve.wait_ge(s_bt, 1)
                        if kind == "gat":
                            V.memset(cr[0:68, 0, :], -BIG)
                            V.memset(cr[0:68, 1, :], 0.0)
                            dve.drain()
                            V.tensor_tensor(cr[0:68, 0, 1:P], carryFx[0:68, 1, 1:P], cps[0:68, 0, 0:P - 1], ALU.add)
                            dve.drain()
                            V.tensor_tensor_scan(ct[0:68, 0, :], carryFx[0:68, 0, :], cr[0:68, 0, :], initial=-BIG, op0=ALU.add, op1=ALU.max)
                            V.memset(fB[0:68, :, :], 0.0)
                            dve.drain()
                            V.tensor_tensor(fB[0:68, 0, 1:P], ct[0:68, 0, 0:P - 1], ct[0:68, 0, 1:P], ALU.subtract)
                            V.tensor_tensor(fB[0:68, 1, 1:P], cps[0:68, 0, 0:P - 1], ct[0:68, 0, 1:P], ALU.subtract)
                            dve.drain()
                            V.tensor_scalar(fB[0:68, :, :], fB[0:68, :, :], 0.0, None, ALU.min).then_inc(S["dm"], 1)
                            dve.wait_ge(S["f"], NG + 1)
                            V.tensor_tensor(fB[0:68, 0, :], fB[0:68, 0, :], carryF[0:68, 0, :], ALU.mult)
                            V.tensor_tensor(fB[0:68, 1, :], fB[0:68, 1, :], carryF[0:68, 1, :], ALU.mult)
                            dve.drain()
                            V.tensor_tensor(cr[0:68, 1, 1:P], fB[0:68, 1, 1:P], cps[0:68, 1, 0:P - 1], ALU.mult)
                            dve.drain()
                            V.tensor_tensor_scan(ct[0:68, 1, :], fB[0:68, 0, :], cr[0:68, 1, :], initial=0.0, op0=ALU.mult, op1=ALU.add)
                        else:
                            for q in range(W // w):
                                mxq = q == 1
                                cf = carryFx if mxq else carryF
                                V.memset(cr[0:w, q, :], -BIG if mxq else 0.0)
                                dve.drain()
                                V.tensor_tensor(cr[0:w, q, 1:P], cf[0:w, 1, 1:P], cps[0:w, q, 0:P - 1], ALU.add if mxq else ALU.mult)
                                dve.drain()
                                V.tensor_tensor_scan(ct[0:w, q, :], cf[0:w, 0, :], cr[0:w, q, :], initial=-BIG if mxq else 0.0,
                                                     op0=ALU.add if mxq else ALU.mult, op1=ALU.max if mxq else ALU.add)
                        dve.drain()
                        dve.sem_inc(s_bc, 1)
                        dve.wait_ge(s_bt, 2)
                        dve.wait_ge(s_g[0], STEPS * per_gather + (32 if kind == "att" else 16))
                        if kind == "gat":
                            V.tensor_copy(m68[:, 0, :], cps[:, 0, 0:68])
                            V.tensor_copy(m68[:, 1, :].rearrange("p (h e) -> p h e", e=17), sB[:, 0, 68:72].unsqueeze(2).broadcast_to([P, H, 17]))
                            dve.drain()
                            V.tensor_tensor(msg[:, 0, 0:68], m68[:, 0, :], m68[:, 1, :], ALU.max)
                            dve.drain()
                            V.tensor_tensor(m68[:, 2, :], m68[:, 0, :], msg[:, 0, 0:68], ALU.subtract)
                            V.tensor_tensor(m68[:, 3, :], m68[:, 1, :], msg[:, 0, 0:68], ALU.subtract).then_inc(S["dm"], 1)
                            dve.wait_ge(S["f"], NG + 2)
                            V.tensor_tensor(m68[:, 2, :], m68[:, 2, :], cps[:, 1, 0:68], ALU.mult)
                            V.tensor_tensor(m68[:, 3, :], m68[:, 3, :], sB[:, 0, 0:68], ALU.mult)
                            dve.drain()
                            V.tensor_tensor(sB[:, 0, 0:68], m68[:, 2, :], m68[:, 3, :], ALU.add)
                        else:
                            V.tensor_tensor(sB[:, 0, 0:w], sB[:, 0, 0:w], cps[:, 0, 0:w], ALU.add)
                            if kind == "pna":
                                V.tensor_tensor(sB[:, 0, w:2 * w], sB[:, 0, w:2 * w], cps[:, 1, 0:w], ALU.max)
                        dve.drain()
                        if kind == "gcn2":
                            V.tensor_copy(lx[:, 0, 0, :], own2[:, 0, :])
                            dve.drain()
                        post(sB[:, :, :], XB[:, :, :], metaB[:, :, :], lx[:, 0, 0:1, :] if kind == "gcn2" else None, 1, NG)
                        if normed:
                            norm_sum(dve, B, 1, S, NG + 1)
                        dve.drain()
                        if kind not in ("gcn2", "gat"):
                            res_free(0, STEPS * no)
                        finish(XB[:, :, :], metaB[:, :, :], 0, 1, NG)
                        if kind == "gcn1":
                            dve.drain()
                            V.tensor_copy(own2[:, 0, :], res[0][:, 0, 0, :])
                        if kind == "pna":
                            dve.wait_ge(S["bn"], NG + 2)
                            V.tensor_copy(bn[0:1, 1, :], bnp[0:1, 0:2 * D])

            with nc.Block() as block:
                @block.sync
                def _(sp):
                    for role in roles.values():
                        sp.sem_clear(role)

        for kind in ('att', 'gcn1', 'gcn2', 'gat', 'pna'):
            edge_phase(kind)
        with ExitStack() as c1:
            S = {k: sem(f"s_{k}_fin") for k in ("cen", "sq", "var", "sd")}
            s_used = sem("s_used_fin"); s_bst = sem("s_bst"); s_bpe = sem("s_bpe"); s_res = sem("s_res_fin")
            s_g = [sem(f"s_g{k}_fin") for k in range(SLOTS)]
            s_ro = [sem(f"s_ro{k}_fin") for k in range(SLOTS)]
            s_gb = sem("s_gb")
            B = buffers(c1)
            idx = sb("idx", [P, SLOTS, G], I32, c1)
            gx = sb("gx", [P, SLOTS, G, 2 * D], F32, c1)
            res = sb("res", [P, SLOTS, G, D], F32, c1)
            row = sb("row", [1, 4, D], F32, c1)
            gb = sb("gb", [1, 2 * D], F32, c1)
            st = sb("st", [1, 2 * D], F32, c1)
            bc = sb("bc", [P, 2 * D], F32, c1)
            bps = ps("bps", [P, 512], c1)
            with nc.Block() as block:
                @block.sync
                def _(sp):
                    sp.dma_start(gb[0:1, 0:D], gamma.rearrange("(o f) -> o f", o=1)).then_inc(s_gb, 16)
                    sp.dma_start(gb[0:1, D:2 * D], beta.rearrange("(o f) -> o f", o=1)).then_inc(s_gb, 16)

                    def store(g, k, tail):
                        sp.wait_ge(s_res, g + 1)
                        sp.sem_inc(s_spturn, 1)
                        for p0, n in PARTS[0:2]:
                            v = out[p0 * T:(p0 + n) * T, :].rearrange("(p t) d -> p t d", t=T)
                            sp.dma_start(v[:, bass.ds(g * G, G), :], res[p0:p0 + n, k, :, :]).then_inc(s_ro[k], 16)
                        if tail:
                            v = out[(P - 1) * T:N, :].rearrange("(o t) d -> o t d", o=1)
                            sp.dma_start(v[:, bass.ds(g * G, tail), :], res[P - 1:P, k, 0:tail, :]).then_inc(s_ro[k], 16)
                        else:
                            sp.sem_inc(s_ro[k], 16)
                    whole = TAIL // (G * SLOTS)
                    with sp.Fori(0, whole) as i:
                        for k in range(SLOTS):
                            store(i * SLOTS + k, k, G)
                    for k in range(SLOTS):
                        g = whole * SLOTS + k
                        store(g, k, max(0, min(G, TAIL - g * G)))
                    with sp.Fori(whole + 1, STEPS) as i:
                        for k in range(SLOTS):
                            store(i * SLOTS + k, k, 0)
                    for k in range(SLOTS):
                        sp.wait_ge(s_ro[k], STEPS * 48)

                @block.gpsimd
                def _(pool):
                    def body(i):
                        for k in range(SLOTS):
                            g = i * SLOTS + k
                            pool.wait_ge(s_used, g + 1)
                            pool.sem_inc(s_turn, 1)
                            for t in range(G):
                                pool.indirect_dma_start(out=gx[:, k, t, :], out_offset=None, in_=T5, in_offset=bass.IndirectOffsetOnAxis(ap=idx[:, k, t:t + 1], axis=0)).then_inc(s_g[k], 16)
                    peeled(pool, STEPS, body)

                @block.scalar
                def _(act):
                    def body(i):
                        for k in range(SLOTS):
                            g = i * SLOTS + k
                            if isinstance(i, int) and k == 1:
                                act.wait_ge(s_bst, 1)
                                nc.scalar.activation(row[0:1, 1, :], row[0:1, 1, :], ACT.Sqrt, bias=epst[0:1, 0:1], scale=1.0).then_inc(s_bst, 1)
                            if k or not isinstance(i, int):
                                norm_squares(act, B, G, S, g)
                                norm_act(act, B, G, S, g)
                    peeled(act, STEPS, body)
                    norm_squares(act, B, G, S, NG)
                    norm_act(act, B, G, S, NG)

                @block.tensor
                def _(pe):
                    pe.wait_ge(s_bst, 3)
                    nc.tensor.matmul(bps[:, 0:2 * D], ones[0:1, :], st[0:1, :], start=True, stop=True).then_inc(s_bpe, 1)

                @block.vector
                def _(dve):
                    V = nc.vector
                    for k in range(SLOTS):
                        V.tensor_copy(idx[:, k, :], rowtab[:, k * G:(k + 1) * G])
                    dve.drain()
                    dve.sem_inc(s_used, SLOTS)
                    V.tensor_tensor(bn[0:1, 2, :], bn[0:1, 0, :], bn[0:1, 1, :], ALU.add)
                    dve.drain()
                    V.tensor_scalar(bn[0:1, 2, :], bn[0:1, 2, :], 1.0 / N, None, ALU.mult)
                    dve.drain()
                    V.tensor_tensor(row[0:1, 0, :], bn[0:1, 2, 0:D], bn[0:1, 2, 0:D], ALU.mult)
                    dve.drain()
                    V.tensor_tensor(row[0:1, 1, :], bn[0:1, 2, D:2 * D], row[0:1, 0, :], ALU.subtract)
                    dve.drain()
                    V.tensor_scalar(row[0:1, 1, :], row[0:1, 1, :], 0.0, None, ALU.max).then_inc(s_bst, 1)
                    dve.wait_ge(s_bst, 2)
                    V.reciprocal(row[0:1, 2, :], row[0:1, 1, :])
                    dve.drain()
                    dve.wait_ge(s_gb, 32)
                    V.tensor_tensor(st[0:1, 0:D], row[0:1, 2, :], gb[0:1, 0:D], ALU.mult)
                    dve.drain()
                    V.tensor_tensor(row[0:1, 3, :], bn[0:1, 2, 0:D], st[0:1, 0:D], ALU.mult)
                    dve.drain()
                    V.tensor_tensor(st[0:1, D:2 * D], gb[0:1, D:2 * D], row[0:1, 3, :], ALU.subtract).then_inc(s_bst, 1)
                    dve.wait_ge(s_bpe, 1)
                    V.tensor_copy(bc[:, :], bps[:, 0:2 * D])
                    dve.drain()

                    def finish(g, k, n):
                        norm_sum(dve, B, G, S, g + 1)
                        if n is not None:
                            dve.wait_ge(s_ro[k], n)
                        norm_b(dve, B, G, S, g + 1, res[:, k, :, :])
                        dve.drain()
                        dve.sem_inc(s_res, 1)

                    def body(i):
                        for k in range(SLOTS):
                            g = i * SLOTS + k
                            if not isinstance(i, int) or i * SLOTS + k >= 1:
                                finish(g - 1, 1 - k, (i + k - 1) * 48 if not isinstance(i, int) or i * SLOTS + k >= 3 else None)
                            dve.wait_ge(s_g[k], i * G * 16 + G * 16)
                            V.tensor_tensor(B["y"][:, :, :], gx[:, k, :, D:2 * D], bc[:, 0:D].unsqueeze(1).broadcast_to([P, G, D]), ALU.mult)
                            dve.drain()
                            V.tensor_tensor(B["y"][:, :, :], B["y"][:, :, :], bc[:, D:2 * D].unsqueeze(1).broadcast_to([P, G, D]), ALU.add)
                            dve.drain()
                            V.tensor_tensor(B["y"][:, :, :], B["y"][:, :, :], gx[:, k, :, 0:D], ALU.add)
                            V.tensor_copy(idx[:, k, :], rowtab_all[:, bass.ds((g + SLOTS) * G, G)])
                            dve.drain()
                            dve.sem_inc(s_used, 1)
                            norm_a(dve, B, G, S)
                    body(0)
                    body(1)
                    with dve.Fori(2, STEPS) as i:
                        body(i)
                    finish(NG - 1, 1, (STEPS - 1) * 48)


_INS = ["x", "src", "dst", "edge_attr_64", "edge_weight", "L1_gnn_W1", "L1_gnn_b1", "L1_gnn_W2", "L1_gnn_b2",
        "L2_gnn_Ws", "L2_gnn_bs", "L2_gnn_Wr", "L2_gnn_br", "L2_gnn_aw", "L2_gnn_ab", "L3_gnn_gamma", "L3_gnn_beta"]


def kernel(**inputs):
    import numpy as _np
    import concourse.bacc as _bacc
    from concourse import mybir as _mybir
    from concourse.bass_utils import run_bass_kernel_spmd as _run

    nc = _bacc.Bacc("TRN2", target_bir_lowering=False, num_devices=1)
    arrays, args = {}, []
    for name in _INS:
        a = _np.ascontiguousarray(inputs[name])
        arrays[f"in_{name}_dram"] = a
        args.append(nc.dram_tensor(f"in_{name}_dram", a.shape, _mybir.dt.from_np(a.dtype), kind="ExternalInput").ap())
    out = nc.dram_tensor("out_0_dram", (N, D), _mybir.dt.float32, kind="ExternalOutput").ap()
    build(nc, *args, out)
    r = _run(nc, [arrays], core_ids=[0])
    return r.results[0]["out_0_dram"]
```
